# Optimizing a Trainium2 kernel written in Bass

```python
import numpy as np
import jax
import jax.numpy as jnp

def _softmax(x, axis=-1):
    return jax.nn.softmax(x, axis=axis)

def _gelu(x):
    return jax.nn.gelu(x, approximate=True)

def _silu(x):
    return jax.nn.silu(x)

def _sigmoid(x):
    return jax.nn.sigmoid(x)

def _layernorm(x, axis=-1, eps=1e-05):
    m = jnp.mean(x, axis=axis, keepdims=True)
    v = jnp.var(x, axis=axis, keepdims=True)
    return (x - m) / jnp.sqrt(v + eps)

def _scatter_add(tgt, idx, src, axis=0):
    return tgt.at[idx].add(src)

def _segment_sum(src, seg, n):
    return jax.ops.segment_sum(src, seg, n)
kernel_name = 'mk_gnn_resnorm_d4_gnn_r8_5281bd'

def setup_inputs(seed: int=0):
    np.random.seed(seed)
    _w = jnp.asarray

    def _rec_inputs():
        import jax
        import jax.numpy as jnp
        _gk = jax.random.key(seed)
        x = -0.000202 + 1 * jax.random.normal(jax.random.fold_in(_gk, 1), (6250, 128), jnp.float32)
        _s = jax.random.randint(jax.random.fold_in(_gk, 2), (100000,), 0, 6250, jnp.int32)
        _d = jax.random.randint(jax.random.fold_in(_gk, 3), (100000,), 0, 6250, jnp.int32)
        _loop = jnp.arange(6250, dtype=jnp.int32)
        src = jnp.concatenate([_s, _d, _loop])
        dst = jnp.concatenate([_d, _s, _loop])
        _o = jnp.argsort(dst, stable=True)
        src = src[_o]
        dst = dst[_o]
        edge_weight = jax.random.uniform(jax.random.fold_in(_gk, 13), (206250,), jnp.float32, 0.0, 0.799017)
        return (x, src, dst, edge_weight)
    x, src, dst, edge_weight = _rec_inputs()

    def _L0_gnn_setup():
        import jax, jax.numpy as jnp
        import numpy as np
        N = 6250
        E = 100000
        H = 4
        NEG_SLOPE = 0.2
        EPS = 1e-16

        def gat_conv(x, W, a_src, a_dst, bias, src, dst):
            C = a_src.shape[1]
            h = (x @ W).reshape(N, H, C)
            alpha_s = jnp.einsum('nhc,hc->nh', h, a_src)
            alpha_d = jnp.einsum('nhc,hc->nh', h, a_dst)
            e = jax.nn.leaky_relu(alpha_s[src] + alpha_d[dst], NEG_SLOPE)
            e_max = jax.ops.segment_max(e, dst, num_segments=N)
            e_exp = jnp.exp(e - e_max[dst])
            denom = jax.ops.segment_sum(e_exp, dst, num_segments=N)
            alpha = e_exp / (denom[dst] + EPS)
            out = jax.ops.segment_sum(h[src] * alpha[:, :, None], dst, num_segments=N)
            return out.reshape(N, H * C) + bias
        key = jax.random.key(seed)
        ks = jax.random.split(key, 10)
        m, hidden, m_y = (128, 32, 32)
        x = jax.random.normal(ks[0], (N, m), jnp.float32)
        edge_index = jax.random.randint(ks[1], (2, E), 0, N, jnp.int32)
        s1 = 1.0 / np.sqrt(m)
        s2 = 1.0 / np.sqrt(H * hidden)
        W1 = jax.random.normal(ks[2], (m, H * hidden), jnp.float32) * s1
        a1_src = jax.random.normal(ks[3], (H, hidden), jnp.float32) * s1
        a1_dst = jax.random.normal(ks[4], (H, hidden), jnp.float32) * s1
        b1 = jnp.zeros((H * hidden,), jnp.float32)
        W2 = jax.random.normal(ks[5], (H * hidden, H * m_y), jnp.float32) * s2
        a2_src = jax.random.normal(ks[6], (H, m_y), jnp.float32) * s2
        a2_dst = jax.random.normal(ks[7], (H, m_y), jnp.float32) * s2
        b2 = jnp.zeros((H * m_y,), jnp.float32)
        return {'x': x, 'edge_index': edge_index, 'W1': W1, 'a1_src': a1_src, 'a1_dst': a1_dst, 'b1': b1, 'W2': W2, 'a2_src': a2_src, 'a2_dst': a2_dst, 'b2': b2}
    _L0_gnn_all = _L0_gnn_setup()
    _L0_gnn_in = {k: v for k, v in _L0_gnn_all.items() if k in ('W1', 'a1_src', 'a1_dst', 'b1', 'W2', 'a2_src', 'a2_dst', 'b2')}
    del _L0_gnn_all

    def _L1_gnn_setup():
        import jax, jax.numpy as jnp
        import numpy as np
        N_NODES = 6250
        N_EDGES = 100000
        DIM_IN = 128
        DIM_OUT = 128
        EPS = 1e-09

        def _branch(x, W, b, scale, offset, idx):
            h = jax.nn.relu(x @ W.T + b)
            mean = jnp.mean(h, axis=1, keepdims=True)
            var = jnp.var(h, axis=1, keepdims=True) + EPS
            d = h.shape[1]
            s = scale[idx * d:(idx + 1) * d]
            o = offset[idx * d:(idx + 1) * d]
            return (h - mean) * s * jax.lax.rsqrt(var) + o
        key = jax.random.key(seed)
        ks = jax.random.split(key, 8)
        feat_in = jax.random.normal(ks[0], (N_NODES, DIM_IN), dtype=jnp.float32)
        edge_row = jax.random.randint(ks[1], (N_EDGES,), 0, N_NODES, dtype=jnp.int32)
        edge_col = jax.random.randint(ks[2], (N_EDGES,), 0, N_NODES, dtype=jnp.int32)
        raw = jax.random.uniform(ks[3], (N_EDGES,), dtype=jnp.float32) + 0.1
        row_sum = jax.ops.segment_sum(raw, edge_row, num_segments=N_NODES)
        edge_val = raw / jnp.maximum(row_sum, EPS)[edge_row]
        W_self = jax.random.normal(ks[4], (DIM_OUT, DIM_IN), dtype=jnp.float32) * (1.0 / np.sqrt(DIM_IN))
        b_self = jax.random.normal(ks[5], (DIM_OUT,), dtype=jnp.float32) * 0.01
        W_neigh = jax.random.normal(ks[6], (DIM_OUT, DIM_IN), dtype=jnp.float32) * (1.0 / np.sqrt(DIM_IN))
        b_neigh = jax.random.normal(ks[7], (DIM_OUT,), dtype=jnp.float32) * 0.01
        scale = jnp.ones((2 * DIM_OUT,), dtype=jnp.float32)
        offset = jnp.zeros((2 * DIM_OUT,), dtype=jnp.float32)
        return {'feat_in': feat_in, 'edge_row': edge_row, 'edge_col': edge_col, 'edge_val': edge_val, 'W_self': W_self, 'b_self': b_self, 'W_neigh': W_neigh, 'b_neigh': b_neigh, 'scale': scale, 'offset': offset}
    _L1_gnn_all = _L1_gnn_setup()
    _L1_gnn_in = {k: v for k, v in _L1_gnn_all.items() if k in ('W_self', 'b_self', 'W_neigh', 'b_neigh', 'scale', 'offset')}
    del _L1_gnn_all

    def _L2_gnn_setup():
        import jax, jax.numpy as jnp
        import numpy as np
        N, D, H, F = (6250, 128, 8, 512)
        HD = D // H
        EPS_BN = 1e-05

        def _batchnorm(x, gamma, beta):
            m = x.mean(axis=0)
            v = x.var(axis=0)
            return (x - m) * jax.lax.rsqrt(v + EPS_BN) * gamma + beta
        key = jax.random.key(seed)
        ks = jax.random.split(key, 12)
        s = 0.05
        return {'src': jax.random.normal(ks[0], (N, D), jnp.float32), 'edge_index': jax.random.randint(ks[1], (2, 100000), 0, N, jnp.int64), 'q_w': jax.random.normal(ks[2], (D, D), jnp.float32) * s, 'q_b': jnp.zeros((D,), jnp.float32), 'k_w': jax.random.normal(ks[3], (D, D), jnp.float32) * s, 'v_w': jax.random.normal(ks[4], (D, D), jnp.float32) * s, 'out_w': jax.random.normal(ks[5], (D, D), jnp.float32) * s, 'out_b': jnp.zeros((D,), jnp.float32), 'g1': jnp.ones((D,), jnp.float32), 'b1': jnp.zeros((D,), jnp.float32), 'lin1_w': jax.random.normal(ks[6], (F, D), jnp.float32) * s, 'lin1_b': jnp.zeros((F,), jnp.float32), 'lin2_w': jax.random.normal(ks[7], (D, F), jnp.float32) * s, 'lin2_b': jnp.zeros((D,), jnp.float32), 'g2': jnp.ones((D,), jnp.float32), 'b2': jnp.zeros((D,), jnp.float32)}
    _L2_gnn_all = _L2_gnn_setup()
    _L2_gnn_in = {k: v for k, v in _L2_gnn_all.items() if k in ('q_w', 'q_b', 'k_w', 'v_w', 'out_w', 'out_b', 'g1', 'b1', 'lin1_w', 'lin1_b', 'lin2_w', 'lin2_b', 'g2', 'b2')}
    del _L2_gnn_all

    def _L3_gnn_setup():
        import jax, jax.numpy as jnp
        import numpy as np
        N, E, C = (12500, 200000, 128)
        EPS = 1e-05

        def _bn(x, g, b):
            mu = jnp.mean(x, axis=0)
            var = jnp.mean((x - mu) ** 2, axis=0)
            return g * (x - mu) * jax.lax.rsqrt(var + EPS) + b
        key = jax.random.key(seed)
        ks = jax.random.split(key, 8)
        s = 1.0 / np.sqrt(C)
        return {'h': jax.random.normal(ks[0], (N, C), jnp.float32), 'src': jax.random.randint(ks[1], (E,), 0, N, jnp.int32), 'dst': jax.random.randint(ks[2], (E,), 0, N, jnp.int32), 'theta_w': jax.random.normal(ks[3], (C, C), jnp.float32) * s, 'phi_w': jax.random.normal(ks[4], (C, C), jnp.float32) * s, 'fc1_w': jax.random.normal(ks[5], (C, C), jnp.float32) * s, 'bn0_g': jnp.ones((C,), jnp.float32), 'bn0_b': jnp.zeros((C,), jnp.float32), 'bn1_g': jnp.ones((C,), jnp.float32), 'bn1_b': jnp.zeros((C,), jnp.float32)}
    _L3_gnn_all = _L3_gnn_setup()
    _L3_gnn_in = {k: v for k, v in _L3_gnn_all.items() if k in ('theta_w', 'phi_w', 'fc1_w', 'bn0_g', 'bn0_b', 'bn1_g', 'bn1_b')}
    del _L3_gnn_all
    return {'x': x, 'src': src, 'dst': dst, 'edge_weight': edge_weight, 'L0_gnn_W1': _L0_gnn_in['W1'], 'L0_gnn_a1_src': _L0_gnn_in['a1_src'], 'L0_gnn_a1_dst': _L0_gnn_in['a1_dst'], 'L0_gnn_b1': _L0_gnn_in['b1'], 'L0_gnn_W2': _L0_gnn_in['W2'], 'L0_gnn_a2_src': _L0_gnn_in['a2_src'], 'L0_gnn_a2_dst': _L0_gnn_in['a2_dst'], 'L0_gnn_b2': _L0_gnn_in['b2'], 'L1_gnn_W_self': _L1_gnn_in['W_self'], 'L1_gnn_b_self': _L1_gnn_in['b_self'], 'L1_gnn_W_neigh': _L1_gnn_in['W_neigh'], 'L1_gnn_b_neigh': _L1_gnn_in['b_neigh'], 'L1_gnn_scale': _L1_gnn_in['scale'], 'L1_gnn_offset': _L1_gnn_in['offset'], 'L2_gnn_q_w': _L2_gnn_in['q_w'], 'L2_gnn_q_b': _L2_gnn_in['q_b'], 'L2_gnn_k_w': _L2_gnn_in['k_w'], 'L2_gnn_v_w': _L2_gnn_in['v_w'], 'L2_gnn_out_w': _L2_gnn_in['out_w'], 'L2_gnn_out_b': _L2_gnn_in['out_b'], 'L2_gnn_g1': _L2_gnn_in['g1'], 'L2_gnn_b1': _L2_gnn_in['b1'], 'L2_gnn_lin1_w': _L2_gnn_in['lin1_w'], 'L2_gnn_lin1_b': _L2_gnn_in['lin1_b'], 'L2_gnn_lin2_w': _L2_gnn_in['lin2_w'], 'L2_gnn_lin2_b': _L2_gnn_in['lin2_b'], 'L2_gnn_g2': _L2_gnn_in['g2'], 'L2_gnn_b2': _L2_gnn_in['b2'], 'L3_gnn_theta_w': _L3_gnn_in['theta_w'], 'L3_gnn_phi_w': _L3_gnn_in['phi_w'], 'L3_gnn_fc1_w': _L3_gnn_in['fc1_w'], 'L3_gnn_bn0_g': _L3_gnn_in['bn0_g'], 'L3_gnn_bn0_b': _L3_gnn_in['bn0_b'], 'L3_gnn_bn1_g': _L3_gnn_in['bn1_g'], 'L3_gnn_bn1_b': _L3_gnn_in['bn1_b']}

def reference(x, src, dst, edge_weight, L0_gnn_W1, L0_gnn_a1_src, L0_gnn_a1_dst, L0_gnn_b1, L0_gnn_W2, L0_gnn_a2_src, L0_gnn_a2_dst, L0_gnn_b2, L1_gnn_W_self, L1_gnn_b_self, L1_gnn_W_neigh, L1_gnn_b_neigh, L1_gnn_scale, L1_gnn_offset, L2_gnn_q_w, L2_gnn_q_b, L2_gnn_k_w, L2_gnn_v_w, L2_gnn_out_w, L2_gnn_out_b, L2_gnn_g1, L2_gnn_b1, L2_gnn_lin1_w, L2_gnn_lin1_b, L2_gnn_lin2_w, L2_gnn_lin2_b, L2_gnn_g2, L2_gnn_b2, L3_gnn_theta_w, L3_gnn_phi_w, L3_gnn_fc1_w, L3_gnn_bn0_g, L3_gnn_bn0_b, L3_gnn_bn1_g, L3_gnn_bn1_b):
    import jax
    import jax.numpy as jnp

    def _L0_gnn_ref(x, edge_index, W1, a1_src, a1_dst, b1, W2, a2_src, a2_dst, b2):
        import jax, jax.numpy as jnp
        import numpy as np
        N = 6250
        E = 100000
        H = 4
        NEG_SLOPE = 0.2
        EPS = 1e-16

        def gat_conv(x, W, a_src, a_dst, bias, src, dst):
            C = a_src.shape[1]
            h = (x @ W).reshape(N, H, C)
            alpha_s = jnp.einsum('nhc,hc->nh', h, a_src)
            alpha_d = jnp.einsum('nhc,hc->nh', h, a_dst)
            e = jax.nn.leaky_relu(alpha_s[src] + alpha_d[dst], NEG_SLOPE)
            e_max = jax.ops.segment_max(e, dst, num_segments=N)
            e_exp = jnp.exp(e - e_max[dst])
            denom = jax.ops.segment_sum(e_exp, dst, num_segments=N)
            alpha = e_exp / (denom[dst] + EPS)
            out = jax.ops.segment_sum(h[src] * alpha[:, :, None], dst, num_segments=N)
            return out.reshape(N, H * C) + bias
        loops = jnp.arange(N, dtype=edge_index.dtype)
        src = jnp.concatenate([edge_index[0], loops])
        dst = jnp.concatenate([edge_index[1], loops])
        out = gat_conv(x, W1, a1_src, a1_dst, b1, src, dst)
        out = jax.nn.elu(out)
        out = gat_conv(out, W2, a2_src, a2_dst, b2, src, dst)
        return out

    def _L1_gnn_ref(feat_in, edge_row, edge_col, edge_val, W_self, b_self, W_neigh, b_neigh, scale, offset):
        import jax, jax.numpy as jnp
        import numpy as np
        N_NODES = 6250
        N_EDGES = 100000
        DIM_IN = 128
        DIM_OUT = 128
        EPS = 1e-09

        def _branch(x, W, b, scale, offset, idx):
            h = jax.nn.relu(x @ W.T + b)
            mean = jnp.mean(h, axis=1, keepdims=True)
            var = jnp.var(h, axis=1, keepdims=True) + EPS
            d = h.shape[1]
            s = scale[idx * d:(idx + 1) * d]
            o = offset[idx * d:(idx + 1) * d]
            return (h - mean) * s * jax.lax.rsqrt(var) + o
        n = feat_in.shape[0]
        feat_neigh = jax.ops.segment_sum(edge_val[:, None] * feat_in[edge_col], edge_row, num_segments=n)
        feat_self_trans = _branch(feat_in, W_self, b_self, scale, offset, 0)
        feat_neigh_trans = _branch(feat_neigh, W_neigh, b_neigh, scale, offset, 1)
        return feat_self_trans + feat_neigh_trans

    def _L2_gnn_ref(src, edge_index, q_w, q_b, k_w, v_w, out_w, out_b, g1, b1, lin1_w, lin1_b, lin2_w, lin2_b, g2, b2):
        import jax, jax.numpy as jnp
        import numpy as np
        N, D, H, F = (6250, 128, 8, 512)
        HD = D // H
        EPS_BN = 1e-05

        def _batchnorm(x, gamma, beta):
            m = x.mean(axis=0)
            v = x.var(axis=0)
            return (x - m) * jax.lax.rsqrt(v + EPS_BN) * gamma + beta
        n = src.shape[0]
        loops = jnp.arange(n, dtype=edge_index.dtype)
        ei = jnp.concatenate([edge_index, jnp.stack([loops, loops])], axis=1)
        e_src, e_dst = (ei[0], ei[1])
        scaling = float(HD) ** (-0.5)
        q = ((src @ q_w.T + q_b) * scaling).reshape(n, H, HD)
        k = (src @ k_w.T).reshape(n, H, HD)
        v = (src @ v_w.T).reshape(n, H, HD)
        w = jnp.einsum('ehd,ehd->eh', q[e_dst], k[e_src])
        mx = jax.ops.segment_max(w, e_dst, num_segments=n)
        ex = jnp.exp(w - mx[e_dst])
        den = jax.ops.segment_sum(ex, e_dst, num_segments=n)
        attn_w = ex / (den[e_dst] + 1e-16)
        msgs = attn_w[:, :, None] * v[e_src]
        agg = jax.ops.segment_sum(msgs, e_dst, num_segments=n)
        attn_out = agg.reshape(n, D) @ out_w.T + out_b
        x = _batchnorm(src + attn_out, g1, b1)
        ff = jax.nn.leaky_relu(x @ lin1_w.T + lin1_b, negative_slope=0.01)
        ff = ff @ lin2_w.T + lin2_b
        x = _batchnorm(x + ff, g2, b2)
        return x

    def _L3_gnn_ref(h, src, dst, theta_w, phi_w, fc1_w, bn0_g, bn0_b, bn1_g, bn1_b):
        import jax, jax.numpy as jnp
        import numpy as np
        N, E, C = (12500, 200000, 128)
        EPS = 1e-05

        def _bn(x, g, b):
            mu = jnp.mean(x, axis=0)
            var = jnp.mean((x - mu) ** 2, axis=0)
            return g * (x - mu) * jax.lax.rsqrt(var + EPS) + b
        n = h.shape[0]
        x_src = h[src]
        x_dst = h[dst]
        e = (x_dst - x_src) @ theta_w.T + x_src @ phi_w.T
        e = jax.nn.relu(_bn(e, bn0_g, bn0_b))
        e = e @ fc1_w.T
        e = jax.nn.relu(_bn(e, bn1_g, bn1_b))
        agg = jax.ops.segment_sum(e, dst, num_segments=n)
        cnt = jax.ops.segment_sum(jnp.ones((e.shape[0],), e.dtype), dst, num_segments=n)
        x = agg / jnp.maximum(cnt, 1.0)[:, None]
        return jax.nn.relu(x + h)
    edge_index = jnp.stack([src, dst])
    x = _layernorm(x + _L0_gnn_ref(x, edge_index, L0_gnn_W1, L0_gnn_a1_src, L0_gnn_a1_dst, L0_gnn_b1, L0_gnn_W2, L0_gnn_a2_src, L0_gnn_a2_dst, L0_gnn_b2), axis=-1)
    x = _layernorm(x + _L1_gnn_ref(x, src, dst, edge_weight, L1_gnn_W_self, L1_gnn_b_self, L1_gnn_W_neigh, L1_gnn_b_neigh, L1_gnn_scale, L1_gnn_offset), axis=-1)
    x = _layernorm(x + _L2_gnn_ref(x, edge_index, L2_gnn_q_w, L2_gnn_q_b, L2_gnn_k_w, L2_gnn_v_w, L2_gnn_out_w, L2_gnn_out_b, L2_gnn_g1, L2_gnn_b1, L2_gnn_lin1_w, L2_gnn_lin1_b, L2_gnn_lin2_w, L2_gnn_lin2_b, L2_gnn_g2, L2_gnn_b2), axis=-1)
    x = _layernorm(x + _L3_gnn_ref(x, src, dst, L3_gnn_theta_w, L3_gnn_phi_w, L3_gnn_fc1_w, L3_gnn_bn0_g, L3_gnn_bn0_b, L3_gnn_bn1_g, L3_gnn_bn1_b), axis=-1)
    return x

_drawn_inputs = setup_inputs


def setup_inputs(seed=0):
    import zlib

    import numpy as np

    out = dict(_drawn_inputs(seed))
    spreads = {'L0_gnn_b1': (0.0, 0.1),
     'L0_gnn_b2': (0.0, 0.1),
     'L1_gnn_scale': (1.0, 0.2),
     'L1_gnn_offset': (0.0, 0.1),
     'L2_gnn_q_b': (0.0, 0.8),
     'L2_gnn_out_b': (0.0, 2.0),
     'L2_gnn_g1': (1.0, 0.2),
     'L2_gnn_b1': (0.0, 0.561),
     'L2_gnn_lin1_b': (0.0, 0.295),
     'L2_gnn_lin2_b': (0.0, 2.0),
     'L2_gnn_g2': (1.0, 0.2),
     'L2_gnn_b2': (0.0, 0.1),
     'L3_gnn_bn0_g': (1.0, 0.6),
     'L3_gnn_bn0_b': (0.0, 0.732),
     'L3_gnn_bn1_g': (1.0, 0.2),
     'L3_gnn_bn1_b': (0.0, 0.332)}
    factors = {'L0_gnn_a1_dst': 25.65,
     'L0_gnn_a2_src': 7.739,
     'L0_gnn_a2_dst': 29.52,
     'L1_gnn_b_self': 8.0,
     'L1_gnn_b_neigh': 26.175,
     'L2_gnn_q_w': 5.061,
     'L2_gnn_k_w': 5.006}
    for name, (base, spread) in spreads.items():
        noise = np.random.default_rng([zlib.crc32(name.encode()), seed]).standard_normal(out[name].shape)
        drawn = base * np.exp(spread * noise) if base else spread * noise
        out[name] = jnp.asarray(drawn.astype(out[name].dtype))
    for name, factor in factors.items():
        out[name] = (out[name] * factor).astype(out[name].dtype)
    return out
```

```python
from contextlib import ExitStack, contextmanager

import concourse.bass as bass
from concourse import mybir

F32 = mybir.dt.float32
BF16 = mybir.dt.bfloat16
I32 = mybir.dt.int32
ALU = mybir.AluOpType
ACT = mybir.ActivationFunctionType
AX = mybir.AxisListType
RMAX = bass.bass_isa.ReduceOp.max
ds = bass.ds

P = 128
N = 6250
E = 206250
T = -(-N // P)
NP = T * P
LAST = N - (T - 1) * P
DUMMY = NP
D = 128
B7 = 7
NB = T // B7
W7 = B7 * P
J = 4
R = 4
CH = 64
GC = CH // J
EROWS = -(-E // CH) + 3
HK = 16
HSTEPS = 2 * (-(-E // (P * HK * 2)))
ECOLS = HSTEPS * HK
GMAX = E // J + T + T * GC + 2 * GC
PITCH = 8192
FILL = NP + P
BIG = 1e30
BLK = 448
NBLK = NP // BLK


class Memory:

    def __init__(self, kit, stage):
        self.kit, self.stage = kit, stage

    def sb(self, s, shape, dt=F32):
        return self.stage.enter_context(self.kit.nc.sbuf_tensor(self.kit.name(s), shape, dt))

    def ps(self, s, shape, dt=F32):
        return self.stage.enter_context(self.kit.nc.psum_tensor(self.kit.name(s), shape, dt))


class Kit:

    def __init__(self, nc):
        self.nc, self.count, self.live = nc, 0, []

    def sub(self, stage):
        return Memory(self, stage)

    def name(self, s):
        self.count += 1
        return f"{s}_{self.count}"

    def sem(self, s):
        self.live.append(self.nc.alloc_semaphore(name=self.name(s)))
        return self.live[-1]

    @contextmanager
    def block(self):
        with self.nc.Block() as b:
            yield b
        self.nc.clear_and_free_semaphores(self.live)
        self.live.clear()
        self.nc.all_engine_barrier()


def take(eng, sem, n=1):
    eng.wait_ge(sem, n)
    eng.sem_clear(sem)


class Hold:

    def __init__(self, eng, turns):
        self.eng, self.turns = eng, turns

    def __call__(self, sem, count):
        self.eng.wait_ge(sem, count)
        self.eng.sem_inc(self.turns, 1)


class Chain:

    def __init__(self, eng, sem):
        self.eng, self.sem, self.n = eng, sem, 0

    def __call__(self, ins):
        self.n += 1
        ins.then_inc(self.sem, 1)
        self.eng.wait_ge(self.sem, self.n)

    def reset(self):
        if self.n:
            self.eng.sem_clear(self.sem)
        self.n = 0


def rows(ap1d, parts=P):
    return ap1d.partition_broadcast(parts)


def flat2(ap):
    return ap.rearrange("p t c -> p (t c)")


def split(total, step):
    return [(i, min(step, total - i)) for i in range(0, total, step)]


def make_constants(k, dense):
    nc = k.nc
    with ExitStack() as st:
        s = k.sub(st)
        zero = s.sb("zero", [P, FILL])
        zeroed, id0, ramps, cleared = (k.sem(x) for x in ("zeroed", "id0", "ramps", "cleared"))
        block = st.enter_context(k.block())

        @block.vector
        def _(dve):
            dve.memset(zero[:, :], 0.0).then_inc(zeroed, 1)
            dve.memset(k.ones[:, :], 1.0)

        @block.gpsimd
        def _(pool):
            pool.memset(k.ident[:, :], 0.0).then_inc(id0, 1)
            pool.memset(k.before[:, :], 0.0).then_inc(id0, 1)
            pool.wait_ge(id0, 2)
            pool.affine_select(out=k.ident[:, :], in_=k.ident[:, :], compare_op=ALU.not_equal, fill=1.0,
                               base=0, pattern=[[-1, P]], channel_multiplier=1)
            pool.affine_select(out=k.before[:, :], in_=k.before[:, :], compare_op=ALU.is_ge, fill=1.0,
                               base=0, pattern=[[-1, P]], channel_multiplier=1)
            pool.iota(k.ramp[:, :], [[1, P]], base=0, channel_multiplier=0,
                      allow_small_or_imprecise_dtypes=True)
            pool.iota(k.pos[:, :], [[P, T]], base=0, channel_multiplier=1)
            pool.iota(k.posf[:, :], [[P, T]], base=0, channel_multiplier=1,
                      allow_small_or_imprecise_dtypes=True)

        @block.sync
        def _(sp):
            sp.wait_ge(zeroed, 1)
            view = dense.rearrange("(t p c) o -> t p (c o)", p=P, c=PITCH)
            with sp.Fori(0, T) as t:
                sp.dma_start(view[ds(t, 1), :, 0:FILL].rearrange("t p c -> (t p) c"),
                             zero[:, :]).then_inc(cleared, 16)
            sp.wait_ge(cleared, 16 * T)


def order_nodes(k, dst_cols, keys_dram, info_dram):
    nc = k.nc
    with ExitStack() as st:
        s = k.sub(st)
        dst = s.sb("dst", [P, ECOLS], I32)
        low_i = s.sb("low_i", [P, ECOLS], I32)
        low, high = s.sb("low", [P, ECOLS], BF16), s.sb("high", [P, ECOLS], BF16)
        ramp = s.sb("rampb", [P, P], BF16)
        hot_low = s.sb("hot_low", [P, 2, HK, P], BF16)
        hot_high = s.sb("hot_high", [P, 2, HK, T], BF16)
        deg = s.sb("deg_n", [P, T])
        tot = s.sb("tot", [P, T])
        key, keyrow = s.sb("key", [P, T]), s.sb("keyrow", [P, NP])
        junk = s.sb("junk", [P, NP], BF16)
        rank, ranki = s.sb("rank", [P, T]), s.sb("ranki", [P, T], I32)
        tmp = s.sb("tmp", [P, T])
        info = s.sb("info", [P, T, 4], I32)
        infop = s.sb("infop", [P, T, 4], I32)
        md = s.sb("md", [P, T])
        ti = s.sb("ti", [P, T], I32)
        hist, pre, tots = s.ps("hist", [P, T]), s.ps("pre", [P, T]), s.ps("tots", [P, T])
        loaded, hot, free = k.sem("dst_loaded"), [k.sem("hot0"), k.sem("hot1")], [k.sem("hf0"), k.sem("hf1")]
        chain_s, key_out, key_in, key_ready = (k.sem(x) for x in ("ordchain", "key_out", "key_in", "key_ready"))
        deg_ready, pre_ready, info_ready, info_out, info_in = (k.sem(x) for x in (
            "deg_ready", "pre_ready", "info_ready", "info_out", "info_in"))
        infos_out, deg_pos, md_ready, z_ready, z_done = (k.sem(x) for x in (
            "infos_out", "deg_pos", "md_ready", "z_ready", "z_done"))
        block = st.enter_context(k.block())

        @block.sync
        def _(sp):
            sp.dma_start(dst[:, :], dst_cols).then_inc(loaded, 16)
            sp.wait_ge(key_ready, 1)
            sp.dma_start(keys_dram.rearrange("(p t) -> p t", p=P), key[:, :]).then_inc(key_out, 16)
            sp.wait_ge(key_out, 16)
            sp.dma_start(keyrow[:, :], rows(keys_dram)).then_inc(key_in, 16)
            sp.wait_ge(infos_out, 1)
            sp.dma_start(infop[:, :, :], info_dram.rearrange("(t p) k -> p t k", p=P)).then_inc(info_in, 16)

        @block.tensor
        def _(pe):
            pe.wait_ge(z_ready, 1)
            pe.matmul(hist[:, :], hot_low[:, 0, 0, :], hot_high[:, 0, 0, :], start=True, stop=False,
                      skip_group_check=True).then_inc(z_done, 1)
            with pe.Fori(0, HSTEPS // 2):
                for u in range(2):
                    take(pe, hot[u])
                    for c in range(HK):
                        mm = pe.matmul(hist[:, :], hot_low[:, u, c, :], hot_high[:, u, c, :], start=False,
                                       stop=False, skip_group_check=True)
                    mm.then_inc(free[u], 1)
            pe.wait_ge(deg_ready, 1)
            pe.matmul(pre[:, :], k.before[:, :], deg[:, :], start=True, stop=True)
            pe.matmul(tots[:, :], k.ones[:, :], deg[:, :], start=True, stop=True).then_inc(pre_ready, 1)

        @block.gpsimd
        def _(pool):
            pool.wait_ge(info_ready, 1)
            for t in range(T):
                pool.indirect_dma_start(info_dram, bass.IndirectOffsetOnAxis(ranki[:, t:t + 1], 0),
                                        info[:, t, :], None).then_inc(info_out, 16)
            pool.wait_ge(info_out, 16 * T)
            pool.sem_inc(infos_out, 1)
            pool.wait_ge(deg_pos, 1)
            pool.partition_all_reduce(md[:, :], k.deg[:, :], P, RMAX).then_inc(md_ready, 1)

        @block.vector
        def _(dve):
            c = Chain(dve, chain_s)
            c(dve.memset(hot_low[:, 0, 0, :], 0.0))
            c(dve.memset(hot_high[:, 0, 0, :], 0.0))
            dve.sem_inc(z_ready, 1)
            c(dve.tensor_copy(ramp[:, :], k.ramp[:, :]))
            dve.wait_ge(loaded, 16)
            c(dve.tensor_single_scalar(low_i[:, :], dst[:, :], P - 1, ALU.bitwise_and))
            c(dve.tensor_copy(low[:, :], low_i[:, :]))
            c(dve.tensor_single_scalar(low_i[:, :], dst[:, :], 7, ALU.arith_shift_right))
            c(dve.tensor_copy(high[:, :], low_i[:, :]))
            c.reset()
            dve.wait_ge(z_done, 1)
            for u in range(2):
                dve.sem_inc(free[u], 1)
            with dve.Fori(0, HSTEPS // 2) as i:
                for u in range(2):
                    take(dve, free[u])
                    lo = low[:, ds((2 * i + u) * HK, HK)].unsqueeze(2).broadcast_to([P, HK, P])
                    hi = high[:, ds((2 * i + u) * HK, HK)].unsqueeze(2).broadcast_to([P, HK, T])
                    c(dve.tensor_tensor(hot_low[:, u], lo, ramp[:, :].unsqueeze(1).broadcast_to([P, HK, P]),
                                        ALU.is_equal))
                    c(dve.tensor_tensor(hot_high[:, u], hi, ramp[:, 0:T].unsqueeze(1).broadcast_to([P, HK, T]),
                                        ALU.is_equal))
                    dve.sem_inc(hot[u], 1)
                c.reset()
            for u in range(2):
                dve.wait_ge(free[u], 1)
            c(dve.tensor_copy(deg[:, :], hist[:, :]))
            dve.sem_inc(deg_ready, 1)
            dve.wait_ge(pre_ready, 1)
            c(dve.tensor_copy(tot[:, :], tots[:, :]))
            c(dve.tensor_tensor_scan(tmp[:, :], k.ones[:, 0:T], tot[:, :], 0.0, ALU.mult, ALU.add))
            c(dve.tensor_tensor(tmp[:, :], tmp[:, :], tot[:, :], ALU.subtract))
            c(dve.tensor_tensor(tmp[:, :], tmp[:, :], pre[:, :], ALU.add))
            c(dve.memset(info[:, :, :], 0))
            c(dve.tensor_copy(info[:, :, 0], tmp[:, :]))
            c(dve.tensor_copy(info[:, :, 1], deg[:, :]))
            c(dve.tensor_copy(info[:, :, 2], k.pos[:, :]))
            c(dve.tensor_scalar(key[:, :], deg[:, :], 1023.0, 8192.0, ALU.min, ALU.mult))
            c(dve.tensor_tensor(key[:, :], key[:, :], k.posf[:, :], ALU.add))
            c(dve.tensor_scalar(tmp[:, :], k.posf[:, :], float(N), -16384.0, ALU.is_ge, ALU.mult))
            c(dve.tensor_tensor(key[:, :], key[:, :], tmp[:, :], ALU.add))
            dve.sem_inc(key_ready, 1)
            dve.wait_ge(key_in, 16)
            c.reset()
            with dve.Fori(0, T) as t:
                c(dve.tensor_scalar(junk[:, :], keyrow[:, :], key[:, ds(t, 1)], 0.0, ALU.is_gt, ALU.add,
                                    accum_out=rank[:, ds(t, 1)]))
                c.reset()
            c(dve.tensor_copy(ranki[:, :], rank[:, :]))
            dve.sem_inc(info_ready, 1)
            dve.wait_ge(info_in, 16)
            c(dve.tensor_copy(k.deg[:, :], infop[:, :, 1]))
            dve.sem_inc(deg_pos, 1)
            c(dve.tensor_copy(k.node[:, :], infop[:, :, 2]))
            c(dve.tensor_copy(tmp[:, :], infop[:, :, 2]))
            c(dve.tensor_scalar(k.nodec[:, :], tmp[:, :], float(N - 1), None, ALU.min))
            c(dve.tensor_single_scalar(k.row0[:, :], infop[:, :, 0], 6, ALU.arith_shift_right))
            c(dve.tensor_single_scalar(k.shift[:, :], infop[:, :, 0], CH - 1, ALU.bitwise_and))
            dve.wait_ge(md_ready, 1)
            for unit, count, first in ((J, k.groups, k.group0), (CH, k.chunks, k.chunk0)):
                c(dve.tensor_scalar(ti[:, :], md[:, :], float(unit - 1), None, ALU.add))
                c(dve.tensor_single_scalar(ti[:, :], ti[:, :], {J: 2, CH: 6}[unit], ALU.arith_shift_right))
                c(dve.tensor_scalar(tot[:, :], ti[:, :], 1.0, None, ALU.max))
                c(dve.tensor_copy(count[:, :], tot[:, :]))
                c(dve.tensor_tensor_scan(tmp[:, :], k.ones[:, 0:T], tot[:, :], 0.0, ALU.mult, ALU.add))
                if unit == J:
                    c(dve.tensor_copy(k.total[:, 0:1], tmp[:, T - 1:T]))
                    c(dve.tensor_scalar(ti[:, 0:1], tmp[:, T - 1:T], float(R - 1), None, ALU.add))
                    c(dve.tensor_single_scalar(k.total[:, 1:2], ti[:, 0:1], 2, ALU.arith_shift_right))
                    c(dve.tensor_scalar(k.empty[:, :], tot[:, :], float(J), None, ALU.mult))
                    c(dve.tensor_tensor(k.empty[:, :], k.empty[:, :], k.deg[:, :], ALU.subtract))
                    c(dve.tensor_reduce(rank[:, 0:NB],
                                        tot[:, :].rearrange("p (b u) -> p b u", u=B7), AX.X, ALU.max))
                    c(dve.tensor_copy(k.bgroups[:, :], rank[:, 0:NB]))
                    c(dve.tensor_tensor_scan(key[:, 0:NB], k.ones[:, 0:NB], rank[:, 0:NB], 0.0, ALU.mult, ALU.add))
                    c(dve.tensor_tensor(key[:, 0:NB], key[:, 0:NB], rank[:, 0:NB], ALU.subtract))
                    c(dve.tensor_copy(k.bgroup0[:, :], key[:, 0:NB]))
                c(dve.tensor_tensor(tmp[:, :], tmp[:, :], tot[:, :], ALU.subtract))
                c(dve.tensor_copy(first[:, :], tmp[:, :]))


def build_slots(k, src_rows, weight_rows, slot_src, slot_weight):
    nc = k.nc
    with ExitStack() as st:
        s = k.sub(st)
        rid = s.sb("rid", [P, 2], I32)
        ridf = s.sb("ridf", [P, 2])
        raw = s.sb("raw", [P, 2, 2 * CH], I32)
        tmp = s.sb("tmp", [P, 2, 2 * CH], I32)
        mask = s.sb("mask", [P, T, 6, 2], I32)
        bit = s.sb("bit", [P, T], I32)
        mrow = s.sb("mrow", [P, 6, 2], I32)
        left = s.sb("left", [P, 1])
        valid = s.sb("valid", [P, CH])
        outs = s.sb("outs", [P, CH], I32)
        outw = s.sb("outw", [P, CH], I32)
        blank = s.sb("blank", [P, CH], I32)
        chain_s, rid_ready, rows_in, out_ready, written, w_sem, turns, turns2, last = (k.sem(x) for x in (
            "slchain", "rid_ready", "rows_in", "out_ready", "written", "w_sem", "slt", "slt2", "last"))
        block = st.enter_context(k.block())

        def table(tab, g):
            return tab[ds(g, GC), :, :].rearrange("g p j -> p g j")

        def tile(x):
            return x[:, :].rearrange("p (g j) -> p g j", j=J)

        @block.gpsimd
        def _(pool):
            with pool.Fori(0, T) as t:
                n = pool.value_load(k.chunks[0:1, ds(t, 1)], min_val=1, max_val=EROWS)
                with pool.Fori(0, n):
                    take(pool, rid_ready)
                    for half in range(2):
                        at = bass.IndirectOffsetOnAxis(rid[:, half:half + 1], 0)
                        pool.indirect_dma_start(raw[:, 0, half * CH:(half + 1) * CH], None, src_rows,
                                                at).then_inc(rows_in, 16)
                        pool.indirect_dma_start(raw[:, 1, half * CH:(half + 1) * CH], None, weight_rows,
                                                at).then_inc(rows_in, 16)

        @block.vector
        def _(dve):
            c = Chain(dve, chain_s)
            hold = Hold(dve, turns)
            c(dve.memset(blank[:, :], DUMMY))
            for b in range(6):
                c(dve.tensor_single_scalar(bit[:, :], k.shift[:, :], 5 - b, ALU.arith_shift_right))
                c(dve.tensor_single_scalar(bit[:, :], bit[:, :], 1, ALU.bitwise_and))
                c(dve.tensor_scalar(mask[:, :, b, 0], bit[:, :], -1.0, None, ALU.mult))
                c(dve.tensor_scalar(mask[:, :, b, 1], bit[:, :], -1.0, None, ALU.add))
            c.reset()
            dve.sem_inc(written, 1)
            with dve.Fori(0, T) as t:
                n = dve.value_load(k.chunks[0:1, ds(t, 1)], min_val=1, max_val=EROWS)
                c0 = dve.value_load(k.chunk0[0:1, ds(t, 1)], min_val=0, max_val=EROWS)
                c(dve.tensor_copy(ridf[:, 0:1], k.row0[:, ds(t, 1)]))
                c(dve.tensor_scalar(ridf[:, 1:2], ridf[:, 0:1], 1.0, None, ALU.add))
                c(dve.tensor_copy(left[:, :], k.deg[:, ds(t, 1)]))
                c(dve.tensor_copy(mrow[:, :, :], mask[:, ds(t, 1)].rearrange("p t b m -> p (t b) m")))
                c.reset()
                with dve.Fori(c0, c0 + n) as g:
                    c(dve.tensor_scalar(rid[:, :], ridf[:, :], float(EROWS - 1), None, ALU.min))
                    c(dve.tensor_scalar(ridf[:, :], ridf[:, :], 1.0, None, ALU.add))
                    dve.sem_inc(rid_ready, 1)
                    hold(rows_in, 64 * (g + 1))
                    for b in range(6):
                        step = 32 >> b
                        wide = {32: 96, 16: 80, 8: 72, 4: 68, 2: 66, 1: 65}[step]
                        c(dve.tensor_single_scalar(tmp[:, :, 0:wide], raw[:, :, 0:wide], mrow[:, b, 1:2],
                                                   ALU.bitwise_and))
                        c(dve.scalar_tensor_tensor(raw[:, :, 0:wide], raw[:, :, step:step + wide],
                                                   mrow[:, b, 0:1], tmp[:, :, 0:wide],
                                                   ALU.bitwise_and, ALU.bitwise_or))
                    take(dve, written)
                    c(dve.tensor_scalar(valid[:, :], k.ramp[:, 0:CH], left[:, 0:1], None, ALU.is_lt))
                    c(dve.tensor_scalar(left[:, :], left[:, :], float(-CH), None, ALU.add))
                    c(dve.scalar_tensor_tensor(valid[:, :], raw[:, 0, 0:CH], float(-DUMMY), valid[:, :],
                                               ALU.add, ALU.mult))
                    c(dve.tensor_scalar(outs[:, :], valid[:, :], float(DUMMY), None, ALU.add))
                    c(dve.tensor_copy(outw[:, :], raw[:, 1, 0:CH]))
                    c.reset()
                    dve.sem_inc(out_ready, 1)

        @block.sync
        def _(sp):
            hold = Hold(sp, turns2)
            with sp.Fori(0, T) as t:
                n = sp.value_load(k.chunks[0:1, ds(t, 1)], min_val=1, max_val=EROWS)
                c0 = sp.value_load(k.chunk0[0:1, ds(t, 1)], min_val=0, max_val=EROWS)
                g0 = sp.value_load(k.group0[0:1, ds(t, 1)], min_val=0, max_val=GMAX - 2 * GC)
                with sp.Fori(c0, c0 + n) as g:
                    at = (g0 + (g - c0) * GC).with_bounds(min_val=0, max_val=GMAX - 2 * GC)
                    take(sp, out_ready)
                    sp.dma_start(table(slot_src, at), tile(outs)).then_inc(w_sem, 16)
                    sp.dma_start(table(slot_weight, at), tile(outw)).then_inc(w_sem, 16)
                    hold(w_sem, 32 * (g + 1))
                    sp.sem_inc(written, 1)
            g = sp.value_load(k.total[0:1, 0:1], min_val=0, max_val=GMAX - 2 * GC)
            sp.dma_start(table(slot_src, g), tile(blank)).then_inc(last, 16)
            sp.dma_start(table(slot_weight, g), tile(blank)).then_inc(last, 16)
            sp.wait_ge(last, 32)


def gather_rows(k, table, dst3, index):
    with ExitStack() as st:
        got = k.sem("got")
        block = st.enter_context(k.block())

        @block.gpsimd
        def _(pool):
            for t in range(T):
                pool.indirect_dma_start(dst3[:, t, :], None, table,
                                        bass.IndirectOffsetOnAxis(index[:, t:t + 1], 0)).then_inc(got, 16)
            pool.wait_ge(got, 16 * T)


def scatter_table(k, table, src3, width, dummy):
    with ExitStack() as st:
        s = k.sub(st)
        row = s.sb("dummy", [1, width])
        out, ready, dout, ch = k.sem("tab_out"), k.sem("dummy_ready"), k.sem("dummy_out"), k.sem("dch")
        block = st.enter_context(k.block())

        @block.vector
        def _(dve):
            c = Chain(dve, ch)
            c(dve.memset(row[:, :], 0.0))
            if dummy is not None:
                c(dve.memset(dummy(row), -BIG))
            dve.sem_inc(ready, 1)

        @block.sync
        def _(sp):
            sp.wait_ge(ready, 1)
            sp.dma_start(table[DUMMY:DUMMY + 1, :], row[:, :]).then_inc(dout, 16)
            sp.wait_ge(dout, 16)

        @block.gpsimd
        def _(pool):
            for t in range(T):
                pool.indirect_dma_start(table, bass.IndirectOffsetOnAxis(k.node[:, t:t + 1], 0),
                                        src3[:, t, 0:width], None).then_inc(out, 16)
            pool.wait_ge(out, 16 * T)


def dense_rows(k, src, products):
    nc = k.nc
    with ExitStack() as st:
        s = k.sub(st)
        stage, xt = s.sb("stage", [P, W7]), s.sb("xt", [P, W7])
        tp, acc = s.ps("tp", [P, 2, 512]), s.ps("acc", [P, 3, 512])
        staged, turned, xt_ready, mm_done, acc_free, ch = (k.sem(x) for x in (
            "staged", "turned", "xt_ready", "mm_done", "acc_free", "drchain"))
        block = st.enter_context(k.block())

        @block.vector
        def _(dve):
            c = Chain(dve, ch)
            with dve.Fori(0, NB) as b:
                c(dve.tensor_copy(stage[:, :].rearrange("p (u c) -> p u c", u=B7), src[:, ds(b * B7, B7), :]))
                dve.sem_inc(staged, 1)
                for w, width, store in products:
                    take(dve, mm_done)
                    for u, n in split(B7, 3):
                        store(dve, c, acc[:, u // 3, 0:n * width].rearrange("p (u c) -> p u c", u=n),
                              b * B7 + u, n)
                    dve.sem_inc(acc_free, 1)
                c.reset()

        @block.tensor
        def _(pe):
            with pe.Fori(0, NB):
                take(pe, staged)
                for u in range(B7):
                    mm = pe.transpose(tp[:, u // 4, (u % 4) * P:(u % 4 + 1) * P], stage[:, u * P:(u + 1) * P],
                                      k.ident[:, :])
                mm.then_inc(turned, 1)
                take(pe, xt_ready)
                for w, width, store in products:
                    for u in range(B7):
                        mm = pe.matmul(acc[:, u // 3, (u % 3) * width:(u % 3 + 1) * width],
                                       xt[:, u * P:(u + 1) * P], w, start=True, stop=True)
                    mm.then_inc(mm_done, 1)
                    take(pe, acc_free)

        @block.scalar
        def _(act):
            with act.Fori(0, NB):
                take(act, turned)
                act.activation(xt[:, 0:512], tp[:, 0, :], ACT.Copy)
                act.activation(xt[:, 512:W7], tp[:, 1, 0:W7 - 512], ACT.Copy).then_inc(xt_ready, 1)


def transpose_blocks(k, src, dst):
    nc = k.nc
    with ExitStack() as st:
        s = k.sub(st)
        stage = s.sb("stage", [P, W7])
        tp = s.ps("tp", [P, 2, 512])
        staged, turned, ch, ach = k.sem("tstaged"), k.sem("tturned"), k.sem("tchain"), k.sem("tachain")
        block = st.enter_context(k.block())

        @block.vector
        def _(dve):
            c = Chain(dve, ch)
            with dve.Fori(0, NB) as b:
                c(dve.tensor_copy(stage[:, :], src[:, ds(b * W7, W7)]))
                c.reset()
                dve.sem_inc(staged, 1)
                take(dve, turned)
                c(dve.tensor_copy(dst[:, ds(b * W7, 512)], tp[:, 0, :]))
                c(dve.tensor_copy(dst[:, ds(b * W7 + 512, W7 - 512)], tp[:, 1, 0:W7 - 512]))
                c.reset()

        @block.tensor
        def _(pe):
            with pe.Fori(0, NB):
                take(pe, staged)
                for u in range(B7):
                    mm = pe.transpose(tp[:, u // 4, (u % 4) * P:(u % 4 + 1) * P], stage[:, u * P:(u + 1) * P],
                                      k.ident[:, :])
                mm.then_inc(turned, 1)


def layernorm(k, src, dst, eps, scale=None, shift=None):
    nc = k.nc
    with ExitStack() as st:
        s = k.sub(st)
        stats = s.sb("stats", [P, T, 6])
        mean, var, tmp, epst = s.sb("mean", [P, T]), s.sb("var", [P, T]), s.sb("t", [P, T]), s.sb("eps", [P, 1])
        ch, var_ready, std_ready = k.sem("lnchain"), k.sem("var_ready"), k.sem("std_ready")
        block = st.enter_context(k.block())

        @block.vector
        def _(dve):
            c = Chain(dve, ch)
            with dve.Fori(0, T) as t:
                c(dve.bn_stats(flat2(stats[:, ds(t, 1), :]), flat2(src[:, ds(t, 1), :])))
                c.reset()
            c(dve.tensor_tensor(mean[:, :], stats[:, :, 1], stats[:, :, 4], ALU.add))
            c(dve.tensor_scalar(mean[:, :], mean[:, :], 0.5, None, ALU.mult))
            c(dve.tensor_tensor(var[:, :], stats[:, :, 2], stats[:, :, 5], ALU.add))
            c(dve.tensor_tensor(tmp[:, :], stats[:, :, 1], stats[:, :, 4], ALU.subtract))
            c(dve.scalar_tensor_tensor(tmp[:, :], tmp[:, :], 0.25, tmp[:, :], ALU.mult, ALU.mult))
            c(dve.scalar_tensor_tensor(var[:, :], var[:, :], 1.0 / D, tmp[:, :], ALU.mult, ALU.add))
            c(dve.memset(epst[:, :], eps))
            dve.sem_inc(var_ready, 1)
            c(dve.tensor_tensor(dst, src, mean[:, :].unsqueeze(2).broadcast_to([P, T, D]), ALU.subtract))
            dve.wait_ge(std_ready, 1)
            c(dve.reciprocal(tmp[:, :], var[:, :]))
            c(dve.tensor_tensor(dst, dst, tmp[:, :].unsqueeze(2).broadcast_to([P, T, D]), ALU.mult))
            if scale is not None:
                c(dve.tensor_tensor(dst, dst, scale.unsqueeze(1).broadcast_to([P, T, D]), ALU.mult))
                c(dve.tensor_tensor(dst, dst, shift.unsqueeze(1).broadcast_to([P, T, D]), ALU.add))

        @block.scalar
        def _(act):
            act.wait_ge(var_ready, 1)
            act.activation(var[:, :], var[:, :], ACT.Sqrt, bias=epst[:, 0:1]).then_inc(std_ready, 1)


def add_rows(k, dst, a, b):
    with ExitStack() as st:
        block = st.enter_context(k.block())

        @block.vector
        def _(dve):
            dve.tensor_tensor(dst, a, b, ALU.add)


def load(k, pairs):
    with ExitStack() as st:
        got = k.sem("loaded")
        block = st.enter_context(k.block())

        @block.sync
        def _(sp):
            for dst, src in pairs:
                sp.dma_start(dst, src).then_inc(got, 16)
            sp.wait_ge(got, 16 * len(pairs))


class Gather:

    def __init__(self, k, s, table, width, slot_src):
        self.k, self.table, self.width, self.slots = k, table, width, slot_src
        self.ring = s.sb("ring", [P, R * J, width])
        self.index = s.sb("index", [P, R * J], I32)
        self.landed, self.used = k.sem("landed"), k.sem("used")
        self.g_sem = [k.sem(f"group{r}_in") for r in range(R)]
        self.i_sem = [k.sem(f"index{h}_in") for h in range(2)]
        self.turns, self.sp_turns = k.sem("pool_turns"), k.sem("sp_turns")

    def pool(self, pool):
        hold = Hold(pool, self.turns)
        n = pool.value_load(self.k.total[0:1, 1:2], min_val=1, max_val=GMAX // R)
        with pool.Fori(0, n) as i:
            for r in range(R):
                if r % 2 == 0:
                    hold(self.i_sem[r // 2], 16 * (i + 1))
                hold(self.used, R * i + r + 1)
                for j in range(J):
                    at = r * J + j
                    pool.indirect_dma_start(self.ring[:, at, :], None, self.table,
                                            bass.IndirectOffsetOnAxis(self.index[:, at:at + 1], 0)
                                            ).then_inc(self.g_sem[r], 16)

    def load_index(self, sp, half, group):
        sp.dma_start(self.index[:, half * 2 * J:(half + 1) * 2 * J].rearrange("p (g j) -> p g j", j=J),
                     self.slots[ds(group, 2), :, :].rearrange("g p j -> p g j")).then_inc(self.i_sem[half], 16)

    def sync(self, sp):
        n = sp.value_load(self.k.total[0:1, 1:2], min_val=1, max_val=GMAX // R)
        for half in range(2):
            self.load_index(sp, half, 2 * half)
        with sp.Fori(0, n) as i:
            for r in range(R):
                sp.wait_ge(self.g_sem[r], 16 * J * (i + 1))
                sp.sem_inc(self.landed, 1)
                if r % 2 == 1:
                    self.load_index(sp, r // 2, (R * (i + 1) + r - 1).with_bounds(min_val=0, max_val=GMAX - 2))
        hold = Hold(sp, self.sp_turns)
        for half in range(2):
            hold(self.i_sem[half], 16 * (n + 1))

    def group(self, g):
        return self.ring[:, ds((g % R) * J, J), :]


def tiles_loop(k, eng):
    def bounds(t):
        n = eng.value_load(k.groups[0:1, ds(t, 1)], min_val=1, max_val=GMAX)
        g0 = eng.value_load(k.group0[0:1, ds(t, 1)], min_val=0, max_val=GMAX)
        return g0, n
    return bounds


def attention_pass(k, table, slot_src, width, heads, dim, own, scores, start, finish, extra):
    nc = k.nc
    VB = heads * (dim + 1)
    with ExitStack() as st:
        s = k.sub(st)
        ga = Gather(k, s, table, width, slot_src)
        e5, x5, p5 = (s.sb(x, [P, J + 1, heads]) for x in ("e5", "x5", "p5"))
        prod = s.sb("prod", [P, J + 1, VB])
        acc = s.sb("acc", [P, VB])
        rden = s.sb("rden", [P, heads])
        work = extra(s)
        ch, e_ready, p_ready, turns = (k.sem(x) for x in ("atchain", "e_ready", "p_ready", "dve_turns"))
        block = st.enter_context(k.block())
        block.gpsimd(ga.pool)
        block.sync(ga.sync)
        newmax = s.sb("newmax", [P, heads])

        @block.vector
        def _(dve):
            c = Chain(dve, ch)
            hold = Hold(dve, turns)
            dve.sem_inc(ga.used, R)
            bounds = tiles_loop(k, dve)
            with dve.Fori(0, T) as t:
                g0, n = bounds(t)
                start(dve, c, t, acc, e5[:, J, :], work)
                c.reset()
                with dve.Fori(g0, g0 + n) as g:
                    hold(ga.landed, g + 1)
                    rows_ = ga.group(g)
                    scores(dve, c, rows_, e5[:, 0:J, :], work)
                    c(dve.tensor_reduce(newmax[:, :], e5[:, :, :].rearrange("p s h -> p h s"), AX.X, ALU.max))
                    c(dve.tensor_tensor(x5[:, :, :], e5[:, :, :],
                                        newmax[:, :].unsqueeze(1).broadcast_to([P, J + 1, heads]), ALU.subtract))
                    dve.sem_inc(e_ready, 1)
                    c(dve.tensor_copy(e5[:, J, :], newmax[:, :]))
                    take(dve, p_ready)
                    c(dve.tensor_tensor(
                        prod[:, 0:J, :].rearrange("p s (h c) -> p s h c", h=heads),
                        rows_[:, :, 0:VB].rearrange("p s (h c) -> p s h c", h=heads),
                        p5[:, 0:J, :].unsqueeze(3).broadcast_to([P, J, heads, dim + 1]), ALU.mult))
                    dve.sem_inc(ga.used, 1)
                    c(dve.tensor_tensor(prod[:, J, :].rearrange("p (h c) -> p h c", h=heads),
                                        acc[:, :].rearrange("p (h c) -> p h c", h=heads),
                                        p5[:, J, :].unsqueeze(2).broadcast_to([P, heads, dim + 1]), ALU.mult))
                    c(dve.tensor_reduce(acc[:, :], prod[:, :, :].rearrange("p s c -> p c s"), AX.X, ALU.add))
                    c.reset()
                a3 = acc[:, :].rearrange("p (h c) -> p h c", h=heads)
                c(dve.tensor_scalar(rden[:, :], a3[:, :, dim], 1e-16, None, ALU.add))
                c(dve.reciprocal(rden[:, :], rden[:, :]))
                c(dve.tensor_tensor(k.out[:, ds(t, 1), :].rearrange("p t (h c) -> p (t h) c", h=heads),
                                    a3[:, :, 0:dim], rden[:, :].unsqueeze(2).broadcast_to([P, heads, dim]),
                                    ALU.mult))
                finish(dve, c, t)
                c.reset()

        @block.scalar
        def _(act):
            n = act.value_load(k.total[0:1, 0:1], min_val=1, max_val=GMAX)
            with act.Fori(0, n):
                take(act, e_ready)
                act.activation(p5[:, :, :], x5[:, :, :], ACT.Exp).then_inc(p_ready, 1)


def gat_conv(k, x, W, a_src, a_dst, bias, table, slot_src, elu):
    H, C = 4, 32
    VB = H * (C + 1)
    with ExitStack() as st:
        s = k.sub(st)
        wext = s.sb("wext", [P, D + 2 * H])
        arow, brow = s.sb("arow", [P, 2, D]), s.sb("brow", [P, D])
        tmp = s.sb("tmp", [P, D])
        own = s.sb("own", [P, T, VB + 2 * H])
        load(k, [(wext[:, 0:D], W), (arow[:, 0, :], rows(a_src.rearrange("h c -> (h c)"))),
                 (arow[:, 1, :], rows(a_dst.rearrange("h c -> (h c)"))), (brow[:, :], rows(bias))])
        with ExitStack() as st2:
            ch = k.sem("wchain")
            block = st2.enter_context(k.block())

            @block.vector
            def _(dve):
                c = Chain(dve, ch)
                for i in range(2):
                    c(dve.tensor_tensor(tmp[:, :], wext[:, 0:D], arow[:, i, :], ALU.mult))
                    c(dve.tensor_reduce(wext[:, D + i * H:D + (i + 1) * H],
                                        tmp[:, :].rearrange("p (h c) -> p h c", h=H), AX.X, ALU.add))
                c(dve.memset(own[:, :, :], 1.0))

        def store(dve, c, ps, t, n):
            c(dve.tensor_copy(own[:, ds(t, n), 0:VB].rearrange("p u (h c) -> p u h c", h=H)[:, :, :, 0:C],
                              ps[:, :, 0:D].rearrange("p u (h c) -> p u h c", h=H)))
            c(dve.tensor_copy(own[:, ds(t, n), VB:VB + 2 * H], ps[:, :, D:D + 2 * H]))

        dense_rows(k, x, [(wext[:, :], D + 2 * H, store)])
        scatter_table(k, table, own, VB + H, lambda row: row[:, VB:VB + H])

        def extra(s2):
            return s2.sb("ad", [P, H])

        def start(dve, c, t, acc, m, ad):
            o = own[:, ds(t, 1), :].rearrange("p t c -> p (t c)")
            c(dve.tensor_copy(acc[:, :], o[:, 0:VB]))
            c(dve.tensor_copy(ad[:, :], o[:, VB + H:VB + 2 * H]))
            c(dve.tensor_tensor(m, o[:, VB:VB + H], ad[:, :], ALU.add))
            c(dve.scalar_tensor_tensor(m, m, 0.2, m, ALU.mult, ALU.max))

        def scores(dve, c, g, e, ad):
            c(dve.tensor_tensor(e, g[:, :, VB:VB + H], ad[:, :].unsqueeze(1).broadcast_to([P, J, H]), ALU.add))
            c(dve.scalar_tensor_tensor(e, e, 0.2, e, ALU.mult, ALU.max))

        def finish(dve, c, t):
            o = k.out[:, ds(t, 1), :].rearrange("p t c -> p (t c)")
            c(dve.tensor_tensor(o, o, brow[:, :], ALU.add))

        attention_pass(k, table, slot_src, VB + H, H, C, own, scores, start, finish, extra)
    if elu:
        with ExitStack() as st:
            s = k.sub(st)
            neg = s.sb("neg", [P, NP])
            ch, n_ready, e_ready = k.sem("eluchain"), k.sem("neg_ready"), k.sem("exp_ready")
            block = st.enter_context(k.block())
            o = flat2(k.out[:, :, :])

            @block.vector
            def _(dve):
                c = Chain(dve, ch)
                c(dve.tensor_scalar(neg[:, :], o, 0.0, None, ALU.min))
                dve.sem_inc(n_ready, 1)
                dve.wait_ge(e_ready, 1)
                c(dve.tensor_scalar(neg[:, :], neg[:, :], -1.0, None, ALU.add))
                c(dve.scalar_tensor_tensor(o, o, 0.0, neg[:, :], ALU.max, ALU.add))

            @block.scalar
            def _(act):
                act.wait_ge(n_ready, 1)
                act.activation(neg[:, :], neg[:, :], ACT.Exp).then_inc(e_ready, 1)


def scatter_weights(k, dense, slot_src, slot_weight):
    nc = k.nc
    with ExitStack() as st:
        s = k.sub(st)
        sl, wl = s.sb("sl", [P, B7, J], I32), s.sb("wl", [P, B7, J])
        slot, valid = s.sb("slot", [P, B7, J]), s.sb("valid", [P, B7, J])
        nexti, nextw = s.sb("nexti", [P, B7, J], I32), s.sb("nextw", [P, B7, J])
        flat, wv = s.sb("flat", [P, B7, J], I32), s.sb("wv", [P, B7, J])
        posb, pos13 = s.sb("posb", [P, B7], I32), s.sb("pos13", [P, T], I32)
        degb = s.sb("degb", [P, B7])
        slots_in, slots_free, flat_ready, scattered, ch, dt, pt, st_ = (k.sem(x) for x in (
            "slots_in", "slots_free", "flat_ready", "scattered", "swchain", "sw_dt", "sw_pt", "sw_st"))
        done = [k.sem(f"added{u}") for u in range(B7)]
        block = st.enter_context(k.block())

        def bounds(eng, b):
            n = eng.value_load(k.bgroups[0:1, ds(b, 1)], min_val=1, max_val=GMAX)
            j0 = eng.value_load(k.bgroup0[0:1, ds(b, 1)], min_val=0, max_val=GMAX)
            return j0, n

        @block.sync
        def _(sp):
            with sp.Fori(0, NB) as b:
                j0, n = bounds(sp, b)
                g0 = [sp.value_load(k.group0[0:1, ds(b * B7 + u, 1)], min_val=0, max_val=GMAX)
                      for u in range(B7)]
                with sp.Fori(j0, j0 + n) as jj:
                    take(sp, slots_free)
                    for u in range(B7):
                        at = ds((g0[u] + (jj - j0)).with_bounds(min_val=0, max_val=GMAX - 1), 1)
                        sp.dma_start(sl[:, u, :], slot_src[at, :, :].rearrange("g p j -> (g p) j")
                                     ).then_inc(slots_in, 16)
                        sp.dma_start(wl[:, u, :], slot_weight[at, :, :].bitcast(F32).rearrange("g p j -> (g p) j")
                                     ).then_inc(slots_in, 16)

        @block.vector
        def _(dve):
            c = Chain(dve, ch)
            hold = Hold(dve, dt)
            c(dve.tensor_single_scalar(pos13[:, :], k.pos[:, :], 13, ALU.logical_shift_left))
            c.reset()
            dve.sem_inc(slots_free, 1)
            dve.sem_inc(scattered, 1)
            with dve.Fori(0, NB) as b:
                j0, n = bounds(dve, b)
                c(dve.tensor_copy(degb[:, :], k.deg[:, ds(b * B7, B7)]))
                c(dve.tensor_copy(posb[:, :], pos13[:, ds(b * B7, B7)]))
                c(dve.tensor_copy(slot[:, :, :], k.ramp[:, 0:J].unsqueeze(1).broadcast_to([P, B7, J])))
                c.reset()
                with dve.Fori(j0, j0 + n) as jj:
                    hold(slots_in, 16 * 2 * B7 * (jj + 1))
                    c(dve.tensor_tensor(valid[:, :, :], slot[:, :, :],
                                        degb[:, :].unsqueeze(2).broadcast_to([P, B7, J]), ALU.is_lt))
                    c(dve.tensor_scalar(slot[:, :, :], slot[:, :, :], float(J), None, ALU.add))
                    c(dve.scalar_tensor_tensor(valid[:, :, :], sl[:, :, :], float(-DUMMY), valid[:, :, :],
                                               ALU.add, ALU.mult))
                    c(dve.tensor_scalar(nexti[:, :, :], valid[:, :, :], float(DUMMY), None, ALU.add))
                    c(dve.tensor_tensor(nexti[:, :, :], nexti[:, :, :],
                                        posb[:, :].unsqueeze(2).broadcast_to([P, B7, J]), ALU.bitwise_or))
                    c(dve.tensor_copy(nextw[:, :, :], wl[:, :, :]))
                    dve.sem_inc(slots_free, 1)
                    take(dve, scattered)
                    c(dve.tensor_copy(flat[:, :, :], nexti[:, :, :]))
                    c(dve.tensor_copy(wv[:, :, :], nextw[:, :, :]))
                    dve.sem_inc(flat_ready, 1)
                    c.reset()

        @block.gpsimd
        def _(pool):
            hold = Hold(pool, pt)
            with pool.Fori(0, NB) as b:
                j0, n = bounds(pool, b)
                with pool.Fori(j0, j0 + n) as jj:
                    take(pool, flat_ready)
                    for j in range(J):
                        for u in range(B7):
                            if j:
                                hold(done[u], 16 * (J * jj + j))
                            pool.indirect_dma_start(
                                dense, bass.IndirectOffsetOnAxis(flat[:, u, j:j + 1], 0), wv[:, u, j:j + 1],
                                None, compute_op=ALU.add).then_inc(done[u], 16)
                    for u in range(B7):
                        hold(done[u], 16 * (J * jj + J))
                    pool.sem_inc(scattered, 1)


def sum_by_source(k, x, dense, fnt):
    nc = k.nc
    HALF, UN = NP // 2, 4
    MM = 448
    with ExitStack() as st:
        s = k.sub(st)
        mat = s.sb("mat", [P, UN, HALF])
        xs = s.sb("xs", [P, UN, D])
        acc = s.ps("fsum", [P, HALF // MM, 512])
        m_in = [k.sem(f"mat{u}_in") for u in range(UN)]
        m_free, x_ready = [k.sem(f"mfree{u}") for u in range(UN)], [k.sem(f"xs_ready{u}") for u in range(UN)]
        x_free = [k.sem(f"xs_free{u}") for u in range(UN)]
        ch, acc_done, acc_out, turns = (k.sem(x) for x in ("sschain", "acc_done", "acc_out", "ss_turns"))
        block = st.enter_context(k.block())
        view = dense.rearrange("(t p c) o -> t p (c o)", p=P, c=PITCH)
        IT = (T - 1) // UN

        @block.sync
        def _(sp):
            for h in range(2):
                def fetch(t, u):
                    take(sp, m_free[u])
                    sp.dma_start(mat[:, u, :], view[ds(t, 1), :, h * HALF:(h + 1) * HALF]
                                 .rearrange("t p c -> (t p) c")).then_inc(m_in[u], 16)
                fetch(0, 0)
                with sp.Fori(0, IT) as i:
                    for u in range(UN):
                        fetch(1 + UN * i + u, (u + 1) % UN)

        @block.vector
        def _(dve):
            c = Chain(dve, ch)
            for u in range(UN):
                dve.sem_inc(m_free[u], 1)
                dve.sem_inc(x_free[u], 1)
            for h in range(2):
                def stage(t, u):
                    take(dve, x_free[u])
                    c(dve.tensor_copy(xs[:, u, :], flat2(x[:, ds(t, 1), :])))
                    dve.sem_inc(x_ready[u], 1)
                stage(0, 0)
                c.reset()
                with dve.Fori(0, IT) as i:
                    for u in range(UN):
                        stage(1 + UN * i + u, (u + 1) % UN)
                    c.reset()
                dve.wait_ge(acc_done, h + 1)
                for m in range(HALF // MM):
                    c(dve.tensor_copy(fnt[:, h * HALF + m * MM:h * HALF + (m + 1) * MM], acc[:, m, 0:MM]))
                c.reset()
                dve.sem_inc(acc_out, 1)

        @block.tensor
        def _(pe):
            hold = Hold(pe, turns)
            for h in range(2):
                def product(u, count, start):
                    hold(m_in[u], count)
                    take(pe, x_ready[u])
                    for m in range(HALF // MM):
                        mm = pe.matmul(acc[:, m, 0:MM], xs[:, u, :], mat[:, u, m * MM:(m + 1) * MM],
                                       start=start, stop=start, skip_group_check=True)
                    mm.then_inc(m_free[u], 1)
                if h:
                    pe.wait_ge(acc_out, 1)
                each = [IT + (u == 0) for u in range(UN)]
                product_free(pe, product, 0, 16 * (h * each[0] + 1), True, x_free)
                with pe.Fori(0, IT) as i:
                    for u in range(UN):
                        v = (u + 1) % UN
                        product_free(pe, product, v, 16 * (h * each[v] + (v == 0) + 1) + 16 * i, False, x_free)
                pe.drain().then_inc(acc_done, 1)


def product_free(pe, product, u, count, start, x_free):
    product(u, count, start)
    pe.drain().then_inc(x_free[u], 1)


def residual_layer(k, x, w_self_t, b_self, w_neigh_t, b_neigh, scale, offset, dense, slot_src, slot_weight,
                   by_node):
    scatter_weights(k, dense, slot_src, slot_weight)
    with ExitStack() as st:
        s = k.sub(st)
        ws, wn = s.sb("ws", [P, D]), s.sb("wn", [P, D])
        br, sc, of = s.sb("br", [P, 2, D]), s.sb("sc", [P, 2 * D]), s.sb("of", [P, 2 * D])
        own = s.sb("selfrows", [P, T, D])
        load(k, [(ws[:, :], w_self_t), (wn[:, :], w_neigh_t), (br[:, 0, :], rows(b_self)),
                 (br[:, 1, :], rows(b_neigh)), (sc[:, :], rows(scale)), (of[:, :], rows(offset))])

        def store(dst, bias):
            def f(dve, c, ps, t, n):
                o = dst[:, ds(t, n), :]
                c(dve.tensor_tensor(o, ps, bias.unsqueeze(1).broadcast_to([P, n, D]), ALU.add))
                c(dve.tensor_scalar(o, o, 0.0, None, ALU.max))
            return f

        dense_rows(k, x, [(ws[:, :], D, store(own, br[:, 0, :]))])
        layernorm(k, own[:, :, :], own[:, :, :], 1e-9, sc[:, 0:D], of[:, 0:D])
        with ExitStack() as st2:
            s2 = k.sub(st2)
            fnt = s2.sb("fnt", [P, NP])
            sum_by_source(k, x, dense, fnt)
            transpose_blocks(k, fnt, flat2(k.out[:, :, :]))
        dense_rows(k, k.out[:, :, :], [(wn[:, :], D, store(k.out, br[:, 1, :]))])
        layernorm(k, k.out[:, :, :], k.out[:, :, :], 1e-9, sc[:, D:2 * D], of[:, D:2 * D])
        with ExitStack() as st3:
            done = k.sem("by_node_out")
            block = st3.enter_context(k.block())

            @block.sync
            def _(sp):
                sp.dma_start(by_node.rearrange("(t p) c -> p t c", p=P), k.out[:, :, :]).then_inc(done, 16)
                sp.wait_ge(done, 16)
        gather_rows(k, by_node, k.out[:, :, :], k.node)
        add_rows(k, k.out[:, :, :], k.out[:, :, :], own[:, :, :])
        add_rows(k, k.out[:, :, :], k.out[:, :, :], x)
    layernorm(k, k.out[:, :, :], x, 1e-5)


def dense_cols(k, src, weights, store, blocks=1):
    nc = k.nc
    with ExitStack() as st:
        s = k.sub(st)
        acc = s.ps("dcacc", [P, len(weights), 512])
        done, free, ch = k.sem("dc_done"), k.sem("dc_free"), k.sem("dcchain")
        block = st.enter_context(k.block())

        @block.tensor
        def _(pe):
            with pe.Fori(0, NBLK) as i:
                take(pe, free)
                for o, ws in enumerate(weights):
                    for b, w in enumerate(ws):
                        mm = pe.matmul(acc[:, o, 0:BLK], w, src[b][:, ds(i * BLK, BLK)], start=(b == 0),
                                       stop=(b == len(ws) - 1))
                mm.then_inc(done, 1)

        @block.vector
        def _(dve):
            c = Chain(dve, ch)
            dve.sem_inc(free, 1)
            with dve.Fori(0, NBLK) as i:
                take(dve, done)
                for o in range(len(weights)):
                    store(dve, c, acc[:, o, 0:BLK], i, o)
                c.reset()
                dve.sem_inc(free, 1)


def scale_shift(dve, c, act_std, mean, var, gamma, beta, scale, shift):
    act_std()
    c(dve.reciprocal(scale, var))
    c(dve.tensor_tensor(scale, scale, gamma, ALU.mult))
    c(dve.tensor_tensor(shift, mean, scale, ALU.mult))
    c(dve.tensor_tensor(shift, beta, shift, ALU.subtract))


def batchnorm_cols(k, a, gamma, beta):
    nc = k.nc
    with ExitStack() as st:
        s = k.sub(st)
        parts = split(N, 512)
        stats, mv, sc, sh, ep = (s.sb(x, sh_) for x, sh_ in (("stats", [P, len(parts), 6]), ("mv", [P, 2]),
                                                            ("sc", [P, 1]), ("sh", [P, 1]), ("ep", [P, 1])))
        ch, v_ready, s_ready = k.sem("bnchain"), k.sem("bn_var"), k.sem("bn_std")
        block = st.enter_context(k.block())

        @block.vector
        def _(dve):
            c = Chain(dve, ch)
            c(dve.memset(ep[:, :], 1e-5))
            for i, (at, n) in enumerate(parts):
                c(dve.bn_stats(stats[:, i, :], a[:, at:at + n]))
            c(dve.bn_aggr(mv[:, :], stats[:, :, :]))

            def std():
                dve.sem_inc(v_ready, 1)
                dve.wait_ge(s_ready, 1)
            scale_shift(dve, c, std, mv[:, 0:1], mv[:, 1:2], gamma, beta, sc[:, :], sh[:, :])
            c(dve.tensor_scalar(a[:, :], a[:, :], sc[:, 0:1], sh[:, 0:1], ALU.mult, ALU.add))

        @block.scalar
        def _(act):
            act.wait_ge(v_ready, 1)
            act.activation(mv[:, 1:2], mv[:, 1:2], ACT.Sqrt, bias=ep[:, 0:1]).then_inc(s_ready, 1)


def attention_layer(k, x, w, table, slot_src):
    H, C = 8, 16
    VB = H * (C + 1)
    F = 512
    with ExitStack() as st:
        s = k.sub(st)
        with ExitStack() as st1:
            s1 = k.sub(st1)
            wq, wk, wv = (s1.sb(n, [P, D]) for n in ("wq", "wk", "wv"))
            qb = s1.sb("qb", [P, D])
            kv = s1.sb("kv", [P, T, 2 * VB])
            q = s1.sb("q", [P, T, VB])
            load(k, [(wq[:, :], w["q_w"]), (wk[:, :], w["k_w"]), (wv[:, :], w["v_w"]), (qb[:, :], rows(w["q_b"]))])
            with ExitStack() as st2:
                block = st2.enter_context(k.block())

                @block.vector
                def _(dve):
                    dve.memset(kv[:, :, 0:VB], 1.0)
                    dve.memset(kv[:, :, VB:2 * VB], 0.0)
                    dve.memset(q[:, :, :], 1.0)

            def heads(ap):
                return ap.rearrange("p u (h c) -> p u h c", h=H)

            def store_v(dve, c, ps, t, n):
                c(dve.tensor_copy(heads(kv[:, ds(t, n), 0:VB])[:, :, :, 0:C], heads(ps)))

            def store_k(dve, c, ps, t, n):
                c(dve.tensor_copy(heads(kv[:, ds(t, n), VB:2 * VB])[:, :, :, 0:C], heads(ps)))

            def store_q(dve, c, ps, t, n):
                for u in range(n):
                    qq = q[:, ds(t + u, 1), :].rearrange("p u (h c) -> p (u h) c", h=H)[:, :, 0:C]
                    c(dve.tensor_tensor(qq, ps[:, u, :].rearrange("p (h c) -> p h c", h=H),
                                        qb[:, :].rearrange("p (h c) -> p h c", h=H), ALU.add))
                    c(dve.tensor_scalar(qq, qq, float(C) ** -0.5, None, ALU.mult))

            dense_rows(k, x, [(wv[:, :], D, store_v), (wk[:, :], D, store_k), (wq[:, :], D, store_q)])
            scatter_table(k, table, kv, 2 * VB,
                          lambda row: row[:, VB:2 * VB].rearrange("p (h c) -> p h c", h=H)[:, :, C:C + 1])

            def extra(s2):
                return s2.sb("qt", [P, VB]), s2.sb("qk", [P, J, VB])

            def start(dve, c, t, acc, m, work):
                qt, qk = work
                o = kv[:, ds(t, 1), :].rearrange("p t c -> p (t c)")
                c(dve.tensor_copy(acc[:, :], o[:, 0:VB]))
                c(dve.tensor_copy(qt[:, :], flat2(q[:, ds(t, 1), :])))
                c(dve.tensor_tensor(qk[:, 0, :], o[:, VB:2 * VB], qt[:, :], ALU.mult))
                c(dve.tensor_reduce(m, qk[:, 0, :].rearrange("p (h c) -> p h c", h=H), AX.X, ALU.add))

            def scores(dve, c, g, e, work):
                qt, qk = work
                c(dve.tensor_tensor(qk[:, :, :], g[:, :, VB:2 * VB],
                                    qt[:, :].unsqueeze(1).broadcast_to([P, J, VB]), ALU.mult))
                c(dve.tensor_reduce(e, qk[:, :, :].rearrange("p s (h c) -> p s h c", h=H), AX.X, ALU.add))

            attention_pass(k, table, slot_src, 2 * VB, H, C, kv, scores, start, lambda *a: None, extra)
        wo, l1, l2 = s.sb("wo", [P, D]), s.sb("l1", [P, F]), s.sb("l2", [P, F // P, D])
        vec = s.sb("vec", [P, 16])
        xt, st_ = s.sb("xt2", [P, NP]), s.sb("ot2", [P, NP])
        names = ("out_b", "g1", "b1", "lin2_b", "g2", "b2")
        load(k, [(wo[:, :], w["out_w"]), (l1[:, :], w["lin1_w"]),
                 (l2[:, :, :], w["lin2_w"].rearrange("(f p) d -> p f d", p=P)),
                 (vec[:, 8:12], w["lin1_b"])] +
             [(vec[:, i:i + 1], w[n]) for i, n in enumerate(names)])
        col = {n: vec[:, i:i + 1] for i, n in enumerate(names)}
        transpose_blocks(k, flat2(x), xt)
        transpose_blocks(k, flat2(k.out[:, :, :]), st_)

        def add_attn(dve, c, ps, i, o):
            a = xt[:, ds(i * BLK, BLK)]
            c(dve.scalar_tensor_tensor(a, ps, col["out_b"], a, ALU.add, ALU.add))

        dense_cols(k, [st_], [[wo[:, :]]], add_attn)
        batchnorm_cols(k, xt, col["g1"], col["b1"])
        with ExitStack() as st3:
            s3 = k.sub(st3)
            hid = [s3.sb(f"hid{f}", [P, NP]) for f in range(F // P - 2)] + [st_]
            hid.append(k.out[:, :, :].rearrange("p t c -> p (t c)"))

            def hidden(dve, c, ps, i, o):
                h = hid[o][:, ds(i * BLK, BLK)]
                c(dve.tensor_scalar(h, ps, vec[:, 8 + o:9 + o], None, ALU.add))
                c(dve.scalar_tensor_tensor(h, h, 0.01, h, ALU.mult, ALU.max))

            def add_ff(dve, c, ps, i, o):
                a = xt[:, ds(i * BLK, BLK)]
                c(dve.scalar_tensor_tensor(a, ps, col["lin2_b"], a, ALU.add, ALU.add))

            dense_cols(k, [xt], [[l1[:, f * P:(f + 1) * P]] for f in range(F // P)], hidden)
            dense_cols(k, hid, [[l2[:, f, :] for f in range(F // P)]], add_ff)
        batchnorm_cols(k, xt, col["g2"], col["b2"])
        transpose_blocks(k, xt, flat2(k.out[:, :, :]))
        add_rows(k, k.out[:, :, :], k.out[:, :, :], x)
    layernorm(k, k.out[:, :, :], x, 1e-5)


def edge_mlp_layer(k, x, w, table, slot_src, empty_dram, cnt_dram, out):
    nc = k.nc
    with ExitStack() as st:
        s = k.sub(st)
        th, ph, fc = s.sb("th", [P, D]), s.sb("ph", [P, D]), s.sb("fc", [P, D])
        vec = s.sb("vec3", [P, 4])
        at = s.sb("at", [P, NP])
        sums = s.sb("sums", [P, 8])
        coef = s.sb("coef", [P, 4])
        load(k, [(th[:, :], w["theta_w"]), (ph[:, :], w["phi_w"]), (fc[:, :], w["fc1_w"])] +
             [(vec[:, i:i + 1], w[n]) for i, n in enumerate(("bn0_g", "bn0_b", "bn1_g", "bn1_b"))])
        with ExitStack() as st1:
            block = st1.enter_context(k.block())
            ch1 = k.sem("l3c")

            @block.vector
            def _(dve):
                c = Chain(dve, ch1)
                c(dve.tensor_tensor(ph[:, :], ph[:, :], th[:, :], ALU.subtract))

        def store_b(dve, c, ps, t, n):
            c(dve.tensor_copy(k.out[:, ds(t, n), :], ps))

        dense_rows(k, x, [(ph[:, :], D, store_b)])
        scatter_table(k, table, k.out, D, None)
        degr, empr = s.sb("degr", [P, NP]), s.sb("empr", [P, NP])
        with ExitStack() as st1:
            s1 = k.sub(st1)
            tt = s1.sb("tt", [T, 2, P])
            pt = s1.ps("pt", [T, 2, P])
            a_, b_, c_ = k.sem("dr_t"), k.sem("dr_c"), k.sem("dr_o")
            d_ = k.sem("dr_i")
            block = st1.enter_context(k.block())

            @block.tensor
            def _(pe):
                pe.transpose(pt[:, 0, :], k.deg[:, :], k.ident[:, :])
                pe.transpose(pt[:, 1, :], k.empty[:, :], k.ident[:, :]).then_inc(a_, 1)

            @block.vector
            def _(dve):
                dve.wait_ge(a_, 1)
                dve.tensor_copy(tt[:, :, :], pt[:, :, :]).then_inc(b_, 1)

            @block.sync
            def _(sp):
                sp.wait_ge(b_, 1)
                sp.dma_start(cnt_dram.rearrange("(t p) -> t p", p=P), tt[:, 0, :]).then_inc(c_, 16)
                sp.dma_start(empty_dram.rearrange("(t p) -> t p", p=P), tt[:, 1, :]).then_inc(c_, 16)
                sp.wait_ge(c_, 32)
                sp.dma_start(degr[:, :], rows(cnt_dram)).then_inc(d_, 16)
                sp.dma_start(empr[:, :], rows(empty_dram)).then_inc(d_, 16)
                sp.wait_ge(d_, 32)

        hT = s.sb("hT", [P, NP])
        transpose_blocks(k, flat2(x), hT)

        def store_a(dve, c, ps, i, o):
            c(dve.tensor_copy(at[:, ds(i * BLK, BLK)], ps))

        dense_cols(k, [hT], [[th[:, :]]], store_a)

        sbt = hT

        edge_stats(k, table, slot_src, sbt, sums)
        edge_bn0(k, at, sbt, degr, sums, vec, coef)
        edge_main(k, table, slot_src, at, fc, coef, sums, None)
        edge_dummy(k, at, fc, coef, sums, empr, vec, hT, False)
        agg = k.out[:, :, :].rearrange("p t c -> p (t c)")
        edge_main(k, table, slot_src, at, fc, coef, sums, agg)
        edge_dummy(k, at, fc, coef, sums, empr, vec, hT, True)
        with ExitStack() as st1:
            ch = k.sem("l3e")
            block = st1.enter_context(k.block())

            @block.vector
            def _(dve):
                c = Chain(dve, ch)
                c(dve.tensor_tensor(agg, agg, hT[:, :], ALU.subtract))
                c(dve.tensor_scalar(degr[:, :], degr[:, :], 1.0, None, ALU.max))
                c(dve.reciprocal(degr[:, :], degr[:, :]))
                c(dve.tensor_tensor(hT[:, :], agg, degr[:, :], ALU.mult))
        transpose_blocks(k, hT, agg)
        with ExitStack() as st1:
            ch = k.sem("l3f")
            block = st1.enter_context(k.block())
            o, xx = k.out[:, :, :], x

            @block.vector
            def _(dve):
                c = Chain(dve, ch)
                c(dve.tensor_tensor(o, o, xx, ALU.add))
                c(dve.scalar_tensor_tensor(o, o, 0.0, xx, ALU.max, ALU.add))
    layernorm(k, k.out[:, :, :], k.out[:, :, :], 1e-5)
    with ExitStack() as st:
        done = k.sem("out_written")
        block = st.enter_context(k.block())

        @block.gpsimd
        def _(pool):
            for t in range(T):
                n = P if t < T - 1 else LAST
                pool.indirect_dma_start(out, bass.IndirectOffsetOnAxis(k.node[0:n, t:t + 1], 0),
                                        k.out[0:n, t, :], None).then_inc(done, 16)
            pool.wait_ge(done, 16 * T)


def edge_stats(k, table, slot_src, sbt, sums):
    nc = k.nc
    with ExitStack() as st:
        s = k.sub(st)
        ga = Gather(k, s, table, D, slot_src)
        stage, sq, zero = s.sb("estage", [P, J, D]), s.sb("sq", [P, J, D]), s.sb("zero", [P, D])
        bsum, sqsum = s.ps("bsum", [P, 512]), s.ps("sqsum", [P, 512])
        staged, staged2, turns, ch, zr, sq_ready, grp, tile_open, tile_done, all_done = (k.sem(n) for n in (
            "staged", "staged2", "turns", "ch", "zr", "sq_ready", "grp", "tile_open", "tile_done", "all_done"))
        block = st.enter_context(k.block())
        block.gpsimd(ga.pool)
        block.sync(ga.sync)

        @block.vector
        def _(dve):
            c = Chain(dve, ch)
            hold = Hold(dve, turns)
            dve.sem_inc(ga.used, R)
            c(dve.memset(zero[:, :], 0.0))
            c.reset()
            dve.sem_inc(zr, 1)
            dve.sem_inc(grp, 1)
            bounds = tiles_loop(k, dve)
            with dve.Fori(0, T) as t:
                g0, n = bounds(t)
                dve.sem_inc(tile_open, 1)
                with dve.Fori(g0, g0 + n) as g:
                    take(dve, grp)
                    hold(ga.landed, g + 1)
                    c(dve.tensor_copy(stage[:, :, :], ga.group(g)))
                    c.reset()
                    dve.sem_inc(ga.used, 1)
                    dve.sem_inc(staged, 1)
                    dve.sem_inc(staged2, 1)
                take(dve, tile_done)
                c(dve.tensor_copy(sbt[:, ds(t * P, P)], bsum[:, 0:D]))
                c.reset()
            c(dve.tensor_copy(sums[:, 0:1], sqsum[:, 0:1]))

        @block.tensor
        def _(pe):
            bounds = tiles_loop(k, pe)
            pe.wait_ge(zr, 1)
            pe.matmul(sqsum[:, 0:1], zero[:, :], zero[:, 0:1], start=True, stop=False, skip_group_check=True)
            with pe.Fori(0, T) as t:
                g0, n = bounds(t)
                take(pe, tile_open)
                pe.matmul(bsum[:, 0:D], zero[:, :], zero[:, :], start=True, stop=False, skip_group_check=True)
                with pe.Fori(g0, g0 + n):
                    take(pe, staged)
                    for j in range(J):
                        pe.matmul(bsum[:, 0:D], stage[:, j, :], k.ident[:, :], start=False, stop=False,
                                  skip_group_check=True)
                    take(pe, sq_ready)
                    for j in range(J):
                        mm = pe.matmul(sqsum[:, 0:1], sq[:, j, :], k.ones[:, 0:1], start=False, stop=False,
                                       skip_group_check=True)
                    mm.then_inc(grp, 1)
                pe.drain().then_inc(tile_done, 1)

        @block.scalar
        def _(act):
            n = act.value_load(k.total[0:1, 0:1], min_val=1, max_val=GMAX)
            with act.Fori(0, n):
                take(act, staged2)
                act.activation(sq[:, :, :], stage[:, :, :], ACT.Square).then_inc(sq_ready, 1)


def finish_bn(k, sums, mean_col, sq_col, gamma, beta, scale, shift):
    with ExitStack() as st:
        s = k.sub(st)
        m, v, t, ep = (s.sb(n, [P, 1]) for n in ("m", "v", "t", "ep"))
        ch, a_, b_ = k.sem("fbch"), k.sem("fba"), k.sem("fbb")
        block = st.enter_context(k.block())

        @block.vector
        def _(dve):
            c = Chain(dve, ch)
            c(dve.memset(ep[:, :], 1e-5))
            c(dve.tensor_scalar(m[:, :], sums[:, mean_col:mean_col + 1], 1.0 / E, None, ALU.mult))
            c(dve.tensor_scalar(v[:, :], sums[:, sq_col:sq_col + 1], 1.0 / E, None, ALU.mult))
            c(dve.tensor_tensor(t[:, :], m[:, :], m[:, :], ALU.mult))
            c(dve.tensor_tensor(v[:, :], v[:, :], t[:, :], ALU.subtract))
            c(dve.tensor_scalar(v[:, :], v[:, :], 0.0, None, ALU.max))

            def std():
                dve.sem_inc(a_, 1)
                dve.wait_ge(b_, 1)
            scale_shift(dve, c, std, m[:, :], v[:, :], gamma, beta, scale, shift)

        @block.scalar
        def _(act):
            act.wait_ge(a_, 1)
            act.activation(v[:, :], v[:, :], ACT.Sqrt, bias=ep[:, 0:1]).then_inc(b_, 1)


def edge_bn0(k, at, sbt, degr, sums, vec, coef):
    with ExitStack() as st:
        s = k.sub(st)
        da, junk = s.sb("da", [P, NP]), s.sb("junk3", [P, NP])
        ch = k.sem("bn0ch")
        with ExitStack() as st1:
            block = st1.enter_context(k.block())

            @block.vector
            def _(dve):
                c = Chain(dve, ch)
                c(dve.tensor_tensor(da[:, :], degr[:, :], at[:, :], ALU.mult))
                c(dve.tensor_reduce(sums[:, 1:2], da[:, :], AX.X, ALU.add))
                c(dve.tensor_reduce(sums[:, 2:3], sbt[:, :], AX.X, ALU.add))
                c(dve.tensor_tensor(sums[:, 4:5], sums[:, 1:2], sums[:, 2:3], ALU.add))
                c(dve.scalar_tensor_tensor(junk[:, :], sbt[:, :], 2.0, da[:, :], ALU.mult, ALU.add))
                c(dve.tensor_tensor(junk[:, :], junk[:, :], at[:, :], ALU.mult))
                c(dve.tensor_reduce(sums[:, 3:4], junk[:, :], AX.X, ALU.add))
                c(dve.tensor_tensor(sums[:, 5:6], sums[:, 0:1], sums[:, 3:4], ALU.add))
        finish_bn(k, sums, 4, 5, vec[:, 0:1], vec[:, 1:2], coef[:, 0:1], coef[:, 1:2])
        ch2 = k.sem("bn0ch2")
        with ExitStack() as st1:
            block = st1.enter_context(k.block())

            @block.vector
            def _(dve):
                c = Chain(dve, ch2)
                c(dve.tensor_scalar(at[:, :], at[:, :], coef[:, 0:1], coef[:, 1:2], ALU.mult, ALU.add))
                c(dve.memset(sums[:, :], 0.0))


def edge_main(k, table, slot_src, at, fc, coef, sums, agg):
    nc = k.nc
    with ExitStack() as st:
        s = k.sub(st)
        ga = Gather(k, s, table, D, slot_src)
        stage = s.sb("mstage", [P, J, D])
        att, pre, r, z = s.sb("att", [P, D]), s.sb("pre", [P, J, D]), s.sb("r", [P, J, D]), s.sb("z", [P, J, D])
        part, total = s.sb("part", [P, 2]), s.sb("tot2", [P, 2])
        zsum, zacc = s.sb("zsum", [P, D]), s.sb("zacc", [P, D])
        bt, e1 = s.ps("bt", [P, 512]), s.ps("e1", [P, 512])
        staged, turned, pre_ready, r_ready, e1_ready, z_ready, e1_free, turns, ch, ach = (
            k.sem(n) for n in ("staged", "turned", "pre_ready", "r_ready", "e1_ready", "z_ready", "e1_free",
                               "turns", "ch", "ach"))
        block = st.enter_context(k.block())
        block.gpsimd(ga.pool)
        block.sync(ga.sync)

        @block.vector
        def _(dve):
            c = Chain(dve, ch)
            hold = Hold(dve, turns)
            dve.sem_inc(ga.used, R)
            c(dve.memset(total[:, :], 0.0))
            c.reset()
            bounds = tiles_loop(k, dve)
            with dve.Fori(0, T) as t:
                g0, n = bounds(t)
                c(dve.tensor_copy(att[:, :], at[:, ds(t * P, P)]))
                if agg is not None:
                    c(dve.memset(zacc[:, :], 0.0))
                c.reset()
                with dve.Fori(g0, g0 + n) as g:
                    hold(ga.landed, g + 1)
                    c(dve.tensor_copy(stage[:, :, :], ga.group(g)))
                    dve.sem_inc(ga.used, 1)
                    dve.sem_inc(staged, 1)
                    take(dve, turned)
                    c(dve.scalar_tensor_tensor(pre[:, :, :], bt[:, :].rearrange("p (j c) -> p j c", j=J),
                                               coef[:, 0:1], att[:, :].unsqueeze(1).broadcast_to([P, J, D]),
                                               ALU.mult, ALU.add))
                    dve.sem_inc(pre_ready, 1)
                    take(dve, z_ready)
                    if agg is None:
                        c(dve.tensor_tensor(total[:, :], total[:, :], part[:, :], ALU.add))
                    else:
                        c(dve.tensor_reduce(zsum[:, :], z[:, :, :].rearrange("p j c -> p c j"), AX.X, ALU.add))
                        c(dve.tensor_tensor(zacc[:, :], zacc[:, :], zsum[:, :], ALU.add))
                    c.reset()
                if agg is not None:
                    c(dve.tensor_copy(agg[:, ds(t * P, P)], zacc[:, :]))
                    c.reset()
            if agg is None:
                c(dve.tensor_copy(sums[:, 0:2], total[:, :]))

        @block.tensor
        def _(pe):
            n = pe.value_load(k.total[0:1, 0:1], min_val=1, max_val=GMAX)
            with pe.Fori(0, n):
                take(pe, staged)
                for j in range(J):
                    mm = pe.transpose(bt[:, j * P:(j + 1) * P], stage[:, j, :], k.ident[:, :])
                mm.then_inc(turned, 1)
                take(pe, r_ready)
                pe.matmul(e1[:, :], fc[:, :], r[:, :, :].rearrange("p j c -> p (j c)"), start=True,
                          stop=True).then_inc(e1_ready, 1)

        @block.scalar
        def _(act):
            n = act.value_load(k.total[0:1, 0:1], min_val=1, max_val=GMAX)
            with act.Fori(0, n):
                take(act, pre_ready)
                rf, pf, zf = (a[:, :, :].rearrange("p j c -> p (j c)") for a in (r, pre, z))
                if agg is None:
                    act.activation(rf, pf, ACT.Relu, accum_out=part[:, 0:1]).then_inc(r_ready, 1)
                    take(act, e1_ready)
                    act.activation(zf, e1[:, :], ACT.Square, accum_out=part[:, 1:2]).then_inc(z_ready, 1)
                else:
                    act.activation(rf, pf, ACT.Relu).then_inc(r_ready, 1)
                    take(act, e1_ready)
                    act.activation(zf, e1[:, :], ACT.Relu, bias=coef[:, 3:4], scale=coef[:, 2:3]).then_inc(z_ready, 1)


def edge_dummy(k, at, fc, coef, sums, empr, vec, spare, final):
    nc = k.nc
    with ExitStack() as st:
        s = k.sub(st)
        e1 = s.sb("e1a", [P, NP])
        r = spare

        with ExitStack() as st1:
            ch = k.sem("edch")
            block = st1.enter_context(k.block())

            @block.vector
            def _(dve):
                c = Chain(dve, ch)
                c(dve.tensor_scalar(r[:, :], at[:, :], 0.0, None, ALU.max))

        def store(dve, c, ps, i, o):
            c(dve.tensor_copy(e1[:, ds(i * BLK, BLK)], ps))

        dense_cols(k, [r], [[fc[:, :]]], store)
        with ExitStack() as st1:
            ch = k.sem("edch2")
            mm_r, mm_d = k.sem("edr"), k.sem("edd")
            ps = k.sub(st1).ps("fcr", [P, 512])
            block = st1.enter_context(k.block())

            @block.vector
            def _(dve):
                c = Chain(dve, ch)
                if final:
                    c(dve.tensor_scalar(e1[:, :], e1[:, :], coef[:, 2:3], coef[:, 3:4], ALU.mult, ALU.add))
                    c(dve.scalar_tensor_tensor(spare[:, :], e1[:, :], 0.0, empr[:, :], ALU.max, ALU.mult))
                else:
                    c(dve.tensor_tensor(r[:, :], r[:, :], empr[:, :], ALU.mult))
                    c(dve.tensor_reduce(sums[:, 2:3], r[:, :], AX.X, ALU.add))
                    c(dve.tensor_tensor(sums[:, 0:1], sums[:, 0:1], sums[:, 2:3], ALU.subtract))
                    dve.sem_inc(mm_r, 1)
                    c(dve.tensor_tensor(r[:, :], e1[:, :], empr[:, :], ALU.mult))
                    c(dve.tensor_tensor(r[:, :], r[:, :], e1[:, :], ALU.mult))
                    c(dve.tensor_reduce(sums[:, 3:4], r[:, :], AX.X, ALU.add))
                    c(dve.tensor_tensor(sums[:, 5:6], sums[:, 1:2], sums[:, 3:4], ALU.subtract))
                    dve.wait_ge(mm_d, 1)
                    c(dve.tensor_copy(sums[:, 4:5], ps[:, 0:1]))

            @block.tensor
            def _(pe):
                if not final:
                    pe.wait_ge(mm_r, 1)
                    pe.matmul(ps[:, 0:1], fc[:, :], sums[:, 0:1], start=True, stop=True).then_inc(mm_d, 1)
        if not final:
            finish_bn(k, sums, 4, 5, vec[:, 2:3], vec[:, 3:4], coef[:, 2:3], coef[:, 3:4])


def build(nc, a, out):
    def dram(name, shape, dt=F32):
        return nc.dram_tensor(name, shape, dt, kind="Internal").ap()

    with ExitStack() as whole:
        k = Kit(nc)
        m = k.sub(whole)
        k.ident, k.ones, k.before = (m.sb(n, [P, P]) for n in ("ident", "ones", "before"))
        k.ramp = m.sb("ramp", [P, P])
        k.pos, k.posf = m.sb("pos", [P, T], I32), m.sb("posf", [P, T])
        k.deg, k.empty = m.sb("deg", [P, T]), m.sb("empty", [P, T])
        k.node, k.nodec, k.row0, k.shift = (m.sb(n, [P, T], I32) for n in ("node", "nodec", "row0", "shift"))
        k.groups, k.group0, k.chunks, k.chunk0 = (m.sb(n, [P, T], I32) for n in (
            "groups", "group0", "chunks", "chunk0"))
        k.bgroups, k.bgroup0 = m.sb("bgroups", [P, NB], I32), m.sb("bgroup0", [P, NB], I32)
        k.total = m.sb("total", [P, 2], I32)
        k.out = m.sb("layer_out", [P, T, D])
        xs = m.sb("x_state", [P, T, D])
        x = xs[:, :, :]

        dense = dram("dense_weights", (NP * PITCH, 1))
        slot_src, slot_weight = dram("slot_src", (GMAX, P, J), I32), dram("slot_weight", (GMAX, P, J), I32)
        keys, info = dram("keys", (NP,)), dram("info", (NP, 4), I32)
        gat_table = dram("gat_table", (NP + 1, 136))
        kv_table = dram("kv_table", (NP + 1, 272))
        b_table = dram("b_table", (NP + 1, D))
        by_node = dram("by_node", (NP, D))
        empty_row, cnt_row = dram("empty_row", (NP,)), dram("cnt_row", (NP,))

        make_constants(k, dense)
        order_nodes(k, a["dst"], keys, info)
        build_slots(k, a["src"], a["edge_weight"], slot_src, slot_weight)
        gather_rows(k, a["x"], x, k.nodec)
        gat_conv(k, x, a["L0_gnn_W1"], a["L0_gnn_a1_src"], a["L0_gnn_a1_dst"], a["L0_gnn_b1"], gat_table,
                 slot_src, True)
        gat_conv(k, k.out[:, :, :], a["L0_gnn_W2"], a["L0_gnn_a2_src"], a["L0_gnn_a2_dst"], a["L0_gnn_b2"],
                 gat_table, slot_src, False)
        add_rows(k, k.out[:, :, :], k.out[:, :, :], x)
        layernorm(k, k.out[:, :, :], x, 1e-5)
        residual_layer(k, x, a["L1_gnn_W_self"], a["L1_gnn_b_self"], a["L1_gnn_W_neigh"], a["L1_gnn_b_neigh"],
                       a["L1_gnn_scale"], a["L1_gnn_offset"], dense, slot_src, slot_weight, by_node)
        attention_layer(k, x, {n[7:]: v for n, v in a.items() if n.startswith("L2_gnn_")}, kv_table, slot_src)
        edge_mlp_layer(k, x, {n[7:]: v for n, v in a.items() if n.startswith("L3_gnn_")}, b_table, slot_src,
                       empty_row, cnt_row, out)


TRANSPOSED = ("L1_gnn_W_self", "L1_gnn_W_neigh", "L2_gnn_q_w", "L2_gnn_k_w", "L2_gnn_v_w", "L2_gnn_out_w",
              "L2_gnn_lin1_w", "L2_gnn_lin2_w", "L3_gnn_theta_w", "L3_gnn_phi_w", "L3_gnn_fc1_w")
COLUMNS = ("L2_gnn_out_b", "L2_gnn_g1", "L2_gnn_b1", "L2_gnn_lin2_b", "L2_gnn_g2", "L2_gnn_b2",
           "L3_gnn_bn0_g", "L3_gnn_bn0_b", "L3_gnn_bn1_g", "L3_gnn_bn1_b")


def kernel(**inputs):
    import numpy as _np
    import concourse.bacc as _bacc
    from concourse import mybir as _mybir
    from concourse.bass_utils import run_bass_kernel_spmd as _run

    nc = _bacc.Bacc("TRN2", target_bir_lowering=False, num_devices=1)
    arrays, args = {}, {}
    for name, value in inputs.items():
        v = _np.asarray(value)
        if name == "dst":
            v = _np.concatenate([v, _np.full(P * ECOLS - E, NP, v.dtype)]).reshape(P, ECOLS)
        elif name in ("src", "edge_weight"):
            v = _np.concatenate([v, _np.zeros(EROWS * CH - E, v.dtype)]).reshape(EROWS, CH)
            if name == "edge_weight":
                v = v.view(_np.int32)
        elif name in TRANSPOSED:
            v = v.T
        elif name in COLUMNS:
            v = v.reshape(-1, 1)
        elif name == "L2_gnn_lin1_b":
            v = v.reshape(-1, P).T
        v = _np.ascontiguousarray(v)
        arrays[f"in_{name}_dram"] = v
        args[name] = nc.dram_tensor(f"in_{name}_dram", v.shape, _mybir.dt.from_np(v.dtype),
                                    kind="ExternalInput").ap()
    out = nc.dram_tensor("out_0_dram", (N, D), _mybir.dt.float32, kind="ExternalOutput").ap()
    build(nc, args, out)
    r = _run(nc, [arrays], core_ids=[0])
    return r.results[0]["out_0_dram"]
```

```python
from contextlib import ExitStack, contextmanager

import concourse.bass as bass
from concourse import mybir

F32 = mybir.dt.float32
BF16 = mybir.dt.bfloat16
I32 = mybir.dt.int32
ALU = mybir.AluOpType
ACT = mybir.ActivationFunctionType
AX = mybir.AxisListType
RMAX = bass.bass_isa.ReduceOp.max
ds = bass.ds

P = 128
N = 6250
E = 206250
T = -(-N // P)
NP = T * P
LAST = N - (T - 1) * P
DUMMY = NP
D = 128
B7 = 7
NB = T // B7
W7 = B7 * P
J = 4
R = 4
CH = 64
GC = CH // J
EROWS = -(-E // CH) + 3
HK = 16
HSTEPS = 2 * (-(-E // (P * HK * 2)))
ECOLS = HSTEPS * HK
GMAX = E // J + 3 * T + T * GC + 2 * GC
CAP = 512
PITCH = 8192
FILL = NP + P
BIG = 1e30
BLK = 448
NBLK = NP // BLK


class Memory:

    def __init__(self, kit, stage):
        self.kit, self.stage = kit, stage

    def sb(self, s, shape, dt=F32):
        return self.stage.enter_context(self.kit.nc.sbuf_tensor(self.kit.name(s), shape, dt))

    def ps(self, s, shape, dt=F32):
        return self.stage.enter_context(self.kit.nc.psum_tensor(self.kit.name(s), shape, dt))


class Kit:

    def __init__(self, nc):
        self.nc, self.count, self.live = nc, 0, []

    def sub(self, stage):
        return Memory(self, stage)

    def name(self, s):
        self.count += 1
        return f"{s}_{self.count}"

    def sem(self, s):
        self.live.append(self.nc.alloc_semaphore(name=self.name(s)))
        return self.live[-1]

    @contextmanager
    def block(self):
        with self.nc.Block() as b:
            yield b
        self.nc.clear_and_free_semaphores(self.live)
        self.live.clear()
        self.nc.all_engine_barrier()


def take(eng, sem, n=1):
    eng.wait_ge(sem, n)
    eng.sem_clear(sem)


class Hold:

    def __init__(self, eng, turns):
        self.eng, self.turns = eng, turns

    def __call__(self, sem, count):
        self.eng.wait_ge(sem, count)
        self.eng.sem_inc(self.turns, 1)


class Chain:

    def __init__(self, eng, sem):
        self.eng, self.sem, self.n = eng, sem, 0

    def __call__(self, ins):
        self.n += 1
        ins.then_inc(self.sem, 1)
        self.eng.wait_ge(self.sem, self.n)

    def go(self, ins):
        self.n += 1
        ins.then_inc(self.sem, 1)
        return self.n

    def until(self, n):
        self.eng.wait_ge(self.sem, n)

    def reset(self):
        if self.n:
            self.eng.sem_clear(self.sem)
        self.n = 0


def rows(ap1d, parts=P):
    return ap1d.partition_broadcast(parts)


def flat2(ap):
    return ap.rearrange("p t c -> p (t c)")


def split(total, step):
    return [(i, min(step, total - i)) for i in range(0, total, step)]


def make_constants(k):
    with ExitStack() as st:
        id0 = k.sem("id0")
        block = st.enter_context(k.block())

        @block.vector
        def _(dve):
            dve.memset(k.ones[:, :], 1.0)

        @block.gpsimd
        def _(pool):
            pool.memset(k.ident[:, :], 0.0).then_inc(id0, 1)
            pool.memset(k.before[:, :], 0.0).then_inc(id0, 1)
            pool.wait_ge(id0, 2)
            pool.affine_select(out=k.ident[:, :], in_=k.ident[:, :], compare_op=ALU.not_equal, fill=1.0,
                               base=0, pattern=[[-1, P]], channel_multiplier=1)
            pool.affine_select(out=k.before[:, :], in_=k.before[:, :], compare_op=ALU.is_ge, fill=1.0,
                               base=0, pattern=[[-1, P]], channel_multiplier=1)
            pool.iota(k.ramp[:, :], [[1, P]], base=0, channel_multiplier=0,
                      allow_small_or_imprecise_dtypes=True)
            pool.iota(k.pos[:, :], [[P, T]], base=0, channel_multiplier=1)
            pool.iota(k.posf[:, :], [[P, T]], base=0, channel_multiplier=1,
                      allow_small_or_imprecise_dtypes=True)


def order_nodes(k, dst_cols, keys_dram, info_dram, dense):
    nc = k.nc
    with ExitStack() as st:
        s = k.sub(st)
        dst = s.sb("dst", [P, ECOLS], I32)
        zero = s.sb("zero", [P, FILL])
        zeroed, cleared = k.sem("zeroed"), k.sem("cleared")
        low_i = s.sb("low_i", [P, ECOLS], I32)
        low, high = s.sb("low", [P, ECOLS], BF16), s.sb("high", [P, ECOLS], BF16)
        ramp = s.sb("rampb", [P, P], BF16)
        hot_low = s.sb("hot_low", [P, 2, HK, P], BF16)
        hot_high = s.sb("hot_high", [P, 2, HK, T], BF16)
        deg = s.sb("deg_n", [P, T])
        tot = s.sb("tot", [P, T])
        key, keyrow = s.sb("key", [P, T]), s.sb("keyrow", [P, NP])
        junk = s.sb("junk", [P, NP], BF16)
        rank, ranki = s.sb("rank", [P, T]), s.sb("ranki", [P, T], I32)
        tmp = s.sb("tmp", [P, T])
        info = s.sb("info", [P, T, 4], I32)
        infop = s.sb("infop", [P, T, 4], I32)
        md = s.sb("md", [P, T])
        ti = s.sb("ti", [P, T], I32)
        hist, pre, tots = s.ps("hist", [P, T]), s.ps("pre", [P, T]), s.ps("tots", [P, T])
        loaded, hot, free = k.sem("dst_loaded"), [k.sem("hot0"), k.sem("hot1")], [k.sem("hf0"), k.sem("hf1")]
        chain_s, key_out, key_in, key_ready = (k.sem(x) for x in ("ordchain", "key_out", "key_in", "key_ready"))
        deg_ready, pre_ready, info_ready, info_out, info_in = (k.sem(x) for x in (
            "deg_ready", "pre_ready", "info_ready", "info_out", "info_in"))
        infos_out, deg_pos, md_ready, z_ready, z_done = (k.sem(x) for x in (
            "infos_out", "deg_pos", "md_ready", "z_ready", "z_done"))
        block = st.enter_context(k.block())

        @block.scalar
        def _(act):
            act.wait_ge(zeroed, 1)
            view = dense.rearrange("(t p c) o -> t p (c o)", p=P, c=PITCH)
            with act.Fori(0, T) as t:
                act.dma_start(view[ds(t, 1), :, 0:FILL].rearrange("t p c -> (t p) c"),
                              zero[:, :]).then_inc(cleared, 16)
            act.wait_ge(cleared, 16 * T)

        @block.sync
        def _(sp):
            sp.dma_start(dst[:, :], dst_cols).then_inc(loaded, 16)
            sp.wait_ge(key_ready, 1)
            sp.dma_start(keys_dram.rearrange("(p t) -> p t", p=P), key[:, :]).then_inc(key_out, 16)
            sp.wait_ge(key_out, 16)
            sp.dma_start(keyrow[:, :], rows(keys_dram)).then_inc(key_in, 16)
            sp.wait_ge(infos_out, 1)
            sp.dma_start(infop[:, :, :], info_dram.rearrange("(t p) k -> p t k", p=P)).then_inc(info_in, 16)

        @block.tensor
        def _(pe):
            pe.wait_ge(z_ready, 1)
            pe.matmul(hist[:, :], hot_low[:, 0, 0, :], hot_high[:, 0, 0, :], start=True, stop=False,
                      skip_group_check=True).then_inc(z_done, 1)
            with pe.Fori(0, HSTEPS // 2):
                for u in range(2):
                    take(pe, hot[u])
                    for c in range(HK):
                        mm = pe.matmul(hist[:, :], hot_low[:, u, c, :], hot_high[:, u, c, :], start=False,
                                       stop=False, skip_group_check=True)
                    mm.then_inc(free[u], 1)
            pe.wait_ge(deg_ready, 1)
            pe.matmul(pre[:, :], k.before[:, :], deg[:, :], start=True, stop=True)
            pe.matmul(tots[:, :], k.ones[:, :], deg[:, :], start=True, stop=True).then_inc(pre_ready, 1)

        @block.gpsimd
        def _(pool):
            pool.wait_ge(info_ready, 1)
            for t in range(T):
                pool.indirect_dma_start(info_dram, bass.IndirectOffsetOnAxis(ranki[:, t:t + 1], 0),
                                        info[:, t, :], None).then_inc(info_out, 16)
            pool.wait_ge(info_out, 16 * T)
            pool.sem_inc(infos_out, 1)
            pool.wait_ge(deg_pos, 1)
            pool.partition_all_reduce(md[:, :], k.deg[:, :], P, RMAX).then_inc(md_ready, 1)

        @block.vector
        def _(dve):
            c = Chain(dve, chain_s)
            dve.memset(zero[:, :], 0.0).then_inc(zeroed, 1)
            c(dve.memset(hot_low[:, 0, 0, :], 0.0))
            c(dve.memset(hot_high[:, 0, 0, :], 0.0))
            dve.sem_inc(z_ready, 1)
            c(dve.tensor_copy(ramp[:, :], k.ramp[:, :]))
            dve.wait_ge(loaded, 16)
            c(dve.tensor_single_scalar(low_i[:, :], dst[:, :], P - 1, ALU.bitwise_and))
            c(dve.tensor_copy(low[:, :], low_i[:, :]))
            c(dve.tensor_single_scalar(low_i[:, :], dst[:, :], 7, ALU.arith_shift_right))
            c(dve.tensor_copy(high[:, :], low_i[:, :]))
            c.reset()
            dve.wait_ge(z_done, 1)
            for u in range(2):
                dve.sem_inc(free[u], 1)
            with dve.Fori(0, HSTEPS // 2) as i:
                for u in range(2):
                    take(dve, free[u])
                    lo = low[:, ds((2 * i + u) * HK, HK)].unsqueeze(2).broadcast_to([P, HK, P])
                    hi = high[:, ds((2 * i + u) * HK, HK)].unsqueeze(2).broadcast_to([P, HK, T])
                    c(dve.tensor_tensor(hot_low[:, u], lo, ramp[:, :].unsqueeze(1).broadcast_to([P, HK, P]),
                                        ALU.is_equal))
                    c(dve.tensor_tensor(hot_high[:, u], hi, ramp[:, 0:T].unsqueeze(1).broadcast_to([P, HK, T]),
                                        ALU.is_equal))
                    dve.sem_inc(hot[u], 1)
                c.reset()
            for u in range(2):
                dve.wait_ge(free[u], 1)
            c(dve.tensor_copy(deg[:, :], hist[:, :]))
            dve.sem_inc(deg_ready, 1)
            dve.wait_ge(pre_ready, 1)
            c(dve.tensor_copy(tot[:, :], tots[:, :]))
            c(dve.tensor_tensor_scan(tmp[:, :], k.ones[:, 0:T], tot[:, :], 0.0, ALU.mult, ALU.add))
            c(dve.tensor_tensor(tmp[:, :], tmp[:, :], tot[:, :], ALU.subtract))
            c(dve.tensor_tensor(tmp[:, :], tmp[:, :], pre[:, :], ALU.add))
            c(dve.memset(info[:, :, :], 0))
            c(dve.tensor_copy(info[:, :, 0], tmp[:, :]))
            c(dve.tensor_copy(info[:, :, 1], deg[:, :]))
            c(dve.tensor_copy(info[:, :, 2], k.pos[:, :]))
            c(dve.tensor_scalar(key[:, :], deg[:, :], 1023.0, 8192.0, ALU.min, ALU.mult))
            c(dve.tensor_tensor(key[:, :], key[:, :], k.posf[:, :], ALU.add))
            c(dve.tensor_scalar(tmp[:, :], k.posf[:, :], float(N), -16384.0, ALU.is_ge, ALU.mult))
            c(dve.tensor_tensor(key[:, :], key[:, :], tmp[:, :], ALU.add))
            dve.sem_inc(key_ready, 1)
            dve.wait_ge(key_in, 16)
            c.reset()
            with dve.Fori(0, T) as t:
                c(dve.tensor_scalar(junk[:, :], keyrow[:, :], key[:, ds(t, 1)], 0.0, ALU.is_gt, ALU.add,
                                    accum_out=rank[:, ds(t, 1)]))
                c.reset()
            c(dve.tensor_copy(ranki[:, :], rank[:, :]))
            dve.sem_inc(info_ready, 1)
            dve.wait_ge(info_in, 16)
            c(dve.tensor_copy(k.deg[:, :], infop[:, :, 1]))
            dve.sem_inc(deg_pos, 1)
            c(dve.tensor_copy(k.node[:, :], infop[:, :, 2]))
            c(dve.tensor_copy(tmp[:, :], infop[:, :, 2]))
            c(dve.tensor_scalar(k.nodec[:, :], tmp[:, :], float(N - 1), None, ALU.min))
            c(dve.tensor_single_scalar(k.row0[:, :], infop[:, :, 0], 6, ALU.arith_shift_right))
            c(dve.tensor_single_scalar(k.shift[:, :], infop[:, :, 0], CH - 1, ALU.bitwise_and))
            dve.wait_ge(md_ready, 1)
            for unit, count, first in ((J, k.groups, k.group0), (CH, k.chunks, k.chunk0)):
                c(dve.tensor_scalar(ti[:, :], md[:, :], float(unit - 1), None, ALU.add))
                c(dve.tensor_single_scalar(ti[:, :], ti[:, :], {J: 2, CH: 6}[unit], ALU.arith_shift_right))
                c(dve.tensor_scalar(tot[:, :], ti[:, :], 3.0 if unit == J else 1.0, None, ALU.max))
                c(dve.tensor_copy(count[:, :], tot[:, :]))
                c(dve.tensor_tensor_scan(tmp[:, :], k.ones[:, 0:T], tot[:, :], 0.0, ALU.mult, ALU.add))
                if unit == J:
                    c(dve.tensor_copy(k.total[:, 0:1], tmp[:, T - 1:T]))
                    c(dve.tensor_scalar(ti[:, 0:1], tmp[:, T - 1:T], float(R - 1), None, ALU.add))
                    c(dve.tensor_single_scalar(k.total[:, 1:2], ti[:, 0:1], 2, ALU.arith_shift_right))
                    c(dve.tensor_scalar(k.empty[:, :], tot[:, :], float(J), None, ALU.mult))
                    c(dve.tensor_tensor(k.empty[:, :], k.empty[:, :], k.deg[:, :], ALU.subtract))
                    c(dve.tensor_reduce(rank[:, 0:NB],
                                        tot[:, :].rearrange("p (b u) -> p b u", u=B7), AX.X, ALU.max))
                    c(dve.tensor_copy(k.bgroups[:, :], rank[:, 0:NB]))
                    c(dve.tensor_tensor_scan(key[:, 0:NB], k.ones[:, 0:NB], rank[:, 0:NB], 0.0, ALU.mult, ALU.add))
                    c(dve.tensor_tensor(key[:, 0:NB], key[:, 0:NB], rank[:, 0:NB], ALU.subtract))
                    c(dve.tensor_copy(k.bgroup0[:, :], key[:, 0:NB]))
                c(dve.tensor_tensor(tmp[:, :], tmp[:, :], tot[:, :], ALU.subtract))
                c(dve.tensor_copy(first[:, :], tmp[:, :]))


def build_slots(k, src_rows, weight_rows, slot_src, slot_weight):
    nc = k.nc
    with ExitStack() as st:
        s = k.sub(st)
        rid = s.sb("rid", [P, 2], I32)
        ridf = s.sb("ridf", [P, 2])
        raw = s.sb("raw", [P, 2, 2 * CH], I32)
        tmp = s.sb("tmp", [P, 2, 2 * CH], I32)
        mask = s.sb("mask", [P, T, 6, 2], I32)
        bit = s.sb("bit", [P, T], I32)
        mrow = s.sb("mrow", [P, 6, 2], I32)
        left = s.sb("left", [P, 1])
        valid = s.sb("valid", [P, CH])
        outs = s.sb("outs", [P, CH], I32)
        outw = s.sb("outw", [P, CH], I32)
        blank = s.sb("blank", [P, CH], I32)
        chain_s, rid_ready, rows_in, out_ready, written, w_sem, turns, turns2, last = (k.sem(x) for x in (
            "slchain", "rid_ready", "rows_in", "out_ready", "written", "w_sem", "slt", "slt2", "last"))
        block = st.enter_context(k.block())

        def table(tab, g):
            return tab[ds(g, GC), :, :].rearrange("g p j -> p g j")

        def tile(x):
            return x[:, :].rearrange("p (g j) -> p g j", j=J)

        @block.gpsimd
        def _(pool):
            with pool.Fori(0, T) as t:
                n = pool.value_load(k.chunks[0:1, ds(t, 1)], min_val=1, max_val=EROWS)
                with pool.Fori(0, n):
                    take(pool, rid_ready)
                    for half in range(2):
                        at = bass.IndirectOffsetOnAxis(rid[:, half:half + 1], 0)
                        pool.indirect_dma_start(raw[:, 0, half * CH:(half + 1) * CH], None, src_rows,
                                                at).then_inc(rows_in, 16)
                        pool.indirect_dma_start(raw[:, 1, half * CH:(half + 1) * CH], None, weight_rows,
                                                at).then_inc(rows_in, 16)

        @block.vector
        def _(dve):
            c = Chain(dve, chain_s)
            hold = Hold(dve, turns)
            c(dve.memset(blank[:, :], DUMMY))
            for b in range(6):
                c(dve.tensor_single_scalar(bit[:, :], k.shift[:, :], 5 - b, ALU.arith_shift_right))
                c(dve.tensor_single_scalar(bit[:, :], bit[:, :], 1, ALU.bitwise_and))
                c(dve.tensor_scalar(mask[:, :, b, 0], bit[:, :], -1.0, None, ALU.mult))
                c(dve.tensor_scalar(mask[:, :, b, 1], bit[:, :], -1.0, None, ALU.add))
            c.reset()
            dve.sem_inc(written, 1)
            with dve.Fori(0, T) as t:
                n = dve.value_load(k.chunks[0:1, ds(t, 1)], min_val=1, max_val=EROWS)
                c0 = dve.value_load(k.chunk0[0:1, ds(t, 1)], min_val=0, max_val=EROWS)
                c(dve.tensor_copy(ridf[:, 0:1], k.row0[:, ds(t, 1)]))
                c(dve.tensor_scalar(ridf[:, 1:2], ridf[:, 0:1], 1.0, None, ALU.add))
                c(dve.tensor_copy(left[:, :], k.deg[:, ds(t, 1)]))
                c(dve.tensor_copy(mrow[:, :, :], mask[:, ds(t, 1)].rearrange("p t b m -> p (t b) m")))
                c.reset()
                with dve.Fori(c0, c0 + n) as g:
                    c(dve.tensor_scalar(rid[:, :], ridf[:, :], float(EROWS - 1), None, ALU.min))
                    c(dve.tensor_scalar(ridf[:, :], ridf[:, :], 1.0, None, ALU.add))
                    dve.sem_inc(rid_ready, 1)
                    hold(rows_in, 64 * (g + 1))
                    for b in range(6):
                        step = 32 >> b
                        wide = {32: 96, 16: 80, 8: 72, 4: 68, 2: 66, 1: 65}[step]
                        c(dve.tensor_single_scalar(tmp[:, :, 0:wide], raw[:, :, 0:wide], mrow[:, b, 1:2],
                                                   ALU.bitwise_and))
                        c(dve.scalar_tensor_tensor(raw[:, :, 0:wide], raw[:, :, step:step + wide],
                                                   mrow[:, b, 0:1], tmp[:, :, 0:wide],
                                                   ALU.bitwise_and, ALU.bitwise_or))
                    take(dve, written)
                    c(dve.tensor_scalar(valid[:, :], k.ramp[:, 0:CH], left[:, 0:1], None, ALU.is_lt))
                    c(dve.tensor_scalar(left[:, :], left[:, :], float(-CH), None, ALU.add))
                    c(dve.scalar_tensor_tensor(valid[:, :], raw[:, 0, 0:CH], float(-DUMMY), valid[:, :],
                                               ALU.add, ALU.mult))
                    c(dve.tensor_scalar(outs[:, :], valid[:, :], float(DUMMY), None, ALU.add))
                    c(dve.tensor_copy(outw[:, :], raw[:, 1, 0:CH]))
                    c.reset()
                    dve.sem_inc(out_ready, 1)

        @block.sync
        def _(sp):
            hold = Hold(sp, turns2)
            with sp.Fori(0, T) as t:
                n = sp.value_load(k.chunks[0:1, ds(t, 1)], min_val=1, max_val=EROWS)
                c0 = sp.value_load(k.chunk0[0:1, ds(t, 1)], min_val=0, max_val=EROWS)
                g0 = sp.value_load(k.group0[0:1, ds(t, 1)], min_val=0, max_val=GMAX - 2 * GC)
                with sp.Fori(c0, c0 + n) as g:
                    at = (g0 + (g - c0) * GC).with_bounds(min_val=0, max_val=GMAX - 2 * GC)
                    take(sp, out_ready)
                    sp.dma_start(table(slot_src, at), tile(outs)).then_inc(w_sem, 16)
                    sp.dma_start(table(slot_weight, at), tile(outw)).then_inc(w_sem, 16)
                    hold(w_sem, 32 * (g + 1))
                    sp.sem_inc(written, 1)
            g = sp.value_load(k.total[0:1, 0:1], min_val=0, max_val=GMAX - 2 * GC)
            sp.dma_start(table(slot_src, g), tile(blank)).then_inc(last, 16)
            sp.dma_start(table(slot_weight, g), tile(blank)).then_inc(last, 16)
            sp.wait_ge(last, 32)


def gather_rows(k, table, dst3, index):
    with ExitStack() as st:
        got = k.sem("got")
        block = st.enter_context(k.block())

        @block.gpsimd
        def _(pool):
            for t in range(T):
                pool.indirect_dma_start(dst3[:, t, :], None, table,
                                        bass.IndirectOffsetOnAxis(index[:, t:t + 1], 0)).then_inc(got, 16)
            pool.wait_ge(got, 16 * T)


def scatter_table(k, table, src3, width, dummy):
    with ExitStack() as st:
        s = k.sub(st)
        row = s.sb("dummy", [1, width])
        out, ready, dout, ch = k.sem("tab_out"), k.sem("dummy_ready"), k.sem("dummy_out"), k.sem("dch")
        block = st.enter_context(k.block())

        @block.vector
        def _(dve):
            c = Chain(dve, ch)
            c(dve.memset(row[:, :], 0.0))
            if dummy is not None:
                c(dve.memset(dummy(row), -BIG))
            dve.sem_inc(ready, 1)

        @block.sync
        def _(sp):
            sp.wait_ge(ready, 1)
            sp.dma_start(table[DUMMY:DUMMY + 1, :], row[:, :]).then_inc(dout, 16)
            sp.wait_ge(dout, 16)

        @block.gpsimd
        def _(pool):
            for t in range(T):
                pool.indirect_dma_start(table, bass.IndirectOffsetOnAxis(k.node[:, t:t + 1], 0),
                                        src3[:, t, 0:width], None).then_inc(out, 16)
            pool.wait_ge(out, 16 * T)


def dense_rows(k, src, products):
    nc = k.nc
    with ExitStack() as st:
        s = k.sub(st)
        stage, xt = s.sb("stage", [P, W7]), s.sb("xt", [P, W7])
        tp, acc = s.ps("tp", [P, 2, 512]), s.ps("acc", [P, 3, 512])
        staged, turned, xt_ready, mm_done, acc_free, ch = (k.sem(x) for x in (
            "staged", "turned", "xt_ready", "mm_done", "acc_free", "drchain"))
        block = st.enter_context(k.block())

        @block.vector
        def _(dve):
            c = Chain(dve, ch)
            with dve.Fori(0, NB) as b:
                c(dve.tensor_copy(stage[:, :].rearrange("p (u c) -> p u c", u=B7), src[:, ds(b * B7, B7), :]))
                dve.sem_inc(staged, 1)
                for w, width, store in products:
                    take(dve, mm_done)
                    for u, n in split(B7, 3):
                        store(dve, c, acc[:, u // 3, 0:n * width].rearrange("p (u c) -> p u c", u=n),
                              b * B7 + u, n)
                    dve.sem_inc(acc_free, 1)
                c.reset()

        @block.tensor
        def _(pe):
            with pe.Fori(0, NB):
                take(pe, staged)
                for u in range(B7):
                    mm = pe.transpose(tp[:, u // 4, (u % 4) * P:(u % 4 + 1) * P], stage[:, u * P:(u + 1) * P],
                                      k.ident[:, :])
                mm.then_inc(turned, 1)
                take(pe, xt_ready)
                for w, width, store in products:
                    for u in range(B7):
                        mm = pe.matmul(acc[:, u // 3, (u % 3) * width:(u % 3 + 1) * width],
                                       xt[:, u * P:(u + 1) * P], w, start=True, stop=True)
                    mm.then_inc(mm_done, 1)
                    take(pe, acc_free)

        @block.scalar
        def _(act):
            with act.Fori(0, NB):
                take(act, turned)
                act.activation(xt[:, 0:512], tp[:, 0, :], ACT.Copy)
                act.activation(xt[:, 512:W7], tp[:, 1, 0:W7 - 512], ACT.Copy).then_inc(xt_ready, 1)


def transpose_blocks(k, src, dst):
    nc = k.nc
    with ExitStack() as st:
        s = k.sub(st)
        stage = s.sb("stage", [P, W7])
        tp = s.ps("tp", [P, 2, 512])
        staged, turned, ch, ach = k.sem("tstaged"), k.sem("tturned"), k.sem("tchain"), k.sem("tachain")
        block = st.enter_context(k.block())

        @block.vector
        def _(dve):
            c = Chain(dve, ch)
            with dve.Fori(0, NB) as b:
                c(dve.tensor_copy(stage[:, :], src[:, ds(b * W7, W7)]))
                c.reset()
                dve.sem_inc(staged, 1)
                take(dve, turned)
                c(dve.tensor_copy(dst[:, ds(b * W7, 512)], tp[:, 0, :]))
                c(dve.tensor_copy(dst[:, ds(b * W7 + 512, W7 - 512)], tp[:, 1, 0:W7 - 512]))
                c.reset()

        @block.tensor
        def _(pe):
            with pe.Fori(0, NB):
                take(pe, staged)
                for u in range(B7):
                    mm = pe.transpose(tp[:, u // 4, (u % 4) * P:(u % 4 + 1) * P], stage[:, u * P:(u + 1) * P],
                                      k.ident[:, :])
                mm.then_inc(turned, 1)


def layernorm(k, src, dst, eps, scale=None, shift=None):
    nc = k.nc
    with ExitStack() as st:
        s = k.sub(st)
        stats = s.sb("stats", [P, T, 6])
        mean, var, tmp, epst = s.sb("mean", [P, T]), s.sb("var", [P, T]), s.sb("t", [P, T]), s.sb("eps", [P, 1])
        ch, var_ready, std_ready = k.sem("lnchain"), k.sem("var_ready"), k.sem("std_ready")
        block = st.enter_context(k.block())

        @block.vector
        def _(dve):
            c = Chain(dve, ch)
            with dve.Fori(0, T) as t:
                c(dve.bn_stats(flat2(stats[:, ds(t, 1), :]), flat2(src[:, ds(t, 1), :])))
                c.reset()
            c(dve.tensor_tensor(mean[:, :], stats[:, :, 1], stats[:, :, 4], ALU.add))
            c(dve.tensor_scalar(mean[:, :], mean[:, :], 0.5, None, ALU.mult))
            c(dve.tensor_tensor(var[:, :], stats[:, :, 2], stats[:, :, 5], ALU.add))
            c(dve.tensor_tensor(tmp[:, :], stats[:, :, 1], stats[:, :, 4], ALU.subtract))
            c(dve.scalar_tensor_tensor(tmp[:, :], tmp[:, :], 0.25, tmp[:, :], ALU.mult, ALU.mult))
            c(dve.scalar_tensor_tensor(var[:, :], var[:, :], 1.0 / D, tmp[:, :], ALU.mult, ALU.add))
            c(dve.memset(epst[:, :], eps))
            dve.sem_inc(var_ready, 1)
            c(dve.tensor_tensor(dst, src, mean[:, :].unsqueeze(2).broadcast_to([P, T, D]), ALU.subtract))
            dve.wait_ge(std_ready, 1)
            c(dve.reciprocal(tmp[:, :], var[:, :]))
            c(dve.tensor_tensor(dst, dst, tmp[:, :].unsqueeze(2).broadcast_to([P, T, D]), ALU.mult))
            if scale is not None:
                c(dve.tensor_tensor(dst, dst, scale.unsqueeze(1).broadcast_to([P, T, D]), ALU.mult))
                c(dve.tensor_tensor(dst, dst, shift.unsqueeze(1).broadcast_to([P, T, D]), ALU.add))

        @block.scalar
        def _(act):
            act.wait_ge(var_ready, 1)
            act.activation(var[:, :], var[:, :], ACT.Sqrt, bias=epst[:, 0:1]).then_inc(std_ready, 1)


def add_rows(k, dst, a, b):
    with ExitStack() as st:
        block = st.enter_context(k.block())

        @block.vector
        def _(dve):
            dve.tensor_tensor(dst, a, b, ALU.add)


def load(k, pairs):
    with ExitStack() as st:
        got = k.sem("loaded")
        block = st.enter_context(k.block())

        @block.sync
        def _(sp):
            for dst, src in pairs:
                sp.dma_start(dst, src).then_inc(got, 16)
            sp.wait_ge(got, 16 * len(pairs))


class Gather:

    def __init__(self, k, s, table, width, slot_src):
        self.k, self.table, self.width, self.slots = k, table, width, slot_src
        self.ring = s.sb("ring", [P, R * J, width])
        self.index = s.sb("index", [P, R * J], I32)
        self.landed, self.used = k.sem("landed"), k.sem("used")
        self.g_sem = [k.sem(f"group{r}_in") for r in range(R)]
        self.i_sem = [k.sem(f"index{h}_in") for h in range(2)]
        self.turns, self.sp_turns = k.sem("pool_turns"), k.sem("sp_turns")

    def pool(self, pool):
        hold = Hold(pool, self.turns)
        n = pool.value_load(self.k.total[0:1, 1:2], min_val=1, max_val=GMAX // R)
        with pool.Fori(0, n) as i:
            for r in range(R):
                if r % 2 == 0:
                    hold(self.i_sem[r // 2], 16 * (i + 1))
                hold(self.used, R * i + r + 1)
                for j in range(J):
                    at = r * J + j
                    pool.indirect_dma_start(self.ring[:, at, :], None, self.table,
                                            bass.IndirectOffsetOnAxis(self.index[:, at:at + 1], 0)
                                            ).then_inc(self.g_sem[r], 16)

    def load_index(self, sp, half, group):
        sp.dma_start(self.index[:, half * 2 * J:(half + 1) * 2 * J].rearrange("p (g j) -> p g j", j=J),
                     self.slots[ds(group, 2), :, :].rearrange("g p j -> p g j")).then_inc(self.i_sem[half], 16)

    def sync(self, sp):
        n = sp.value_load(self.k.total[0:1, 1:2], min_val=1, max_val=GMAX // R)
        for half in range(2):
            self.load_index(sp, half, 2 * half)
        with sp.Fori(0, n) as i:
            for r in range(R):
                sp.wait_ge(self.g_sem[r], 16 * J * (i + 1))
                sp.sem_inc(self.landed, 1)
                if r % 2 == 1:
                    self.load_index(sp, r // 2, (R * (i + 1) + r - 1).with_bounds(min_val=0, max_val=GMAX - 2))
        hold = Hold(sp, self.sp_turns)
        for half in range(2):
            hold(self.i_sem[half], 16 * (n + 1))

    def group(self, g):
        return self.ring[:, ds((g % R) * J, J), :]


def tiles_loop(k, eng):
    def bounds(t):
        n = eng.value_load(k.groups[0:1, ds(t, 1)], min_val=3, max_val=GMAX)
        g0 = eng.value_load(k.group0[0:1, ds(t, 1)], min_val=0, max_val=GMAX)
        return g0, n
    return bounds


def attention_pass(k, table, slot_src, width, heads, dim, own, scores, start, finish, extra):
    VB = heads * (dim + 1)
    with ExitStack() as st:
        s = k.sub(st)
        ga = Gather(k, s, table, width, slot_src)
        e5, x5 = (s.sb(x, [P, J + 1, heads]) for x in ("e5", "x5"))
        p5 = s.sb("p5", [P, J + 1, heads])
        warm = s.sb("warm", [P, 1])
        prod = s.sb("prod", [P, J + 1, VB])
        acc = s.sb("acc", [P, VB])
        rden, newmax = s.sb("rden", [P, heads]), s.sb("newmax", [P, heads])
        work = extra(s)
        ch, e_ready, p_ready = (k.sem(x) for x in ("atchain", "e_ready", "p_ready"))
        block = st.enter_context(k.block())
        block.gpsimd(ga.pool)
        block.sync(ga.sync)

        def by_head(ap):
            return ap.rearrange("p s (h c) -> p s h c", h=heads)

        @block.vector
        def _(dve):
            c = Chain(dve, ch)
            dve.sem_inc(ga.used, R)
            bounds = tiles_loop(k, dve)

            def weigh_rows(g):
                dve.wait_ge(p_ready, g + 1)
                dve.tensor_tensor(by_head(prod[:, 0:J, :]), by_head(ga.group(g)[:, :, 0:VB]),
                                  p5[:, 0:J, :].unsqueeze(3).broadcast_to([P, J, heads, dim + 1]),
                                  ALU.mult).then_inc(ga.used, 1)

            def weigh_sum():
                return c.go(dve.tensor_tensor(by_head(prod[:, J:J + 1, :]),
                                              acc[:, :].rearrange("p (s h c) -> p s h c", s=1, h=heads),
                                              p5[:, J:J + 1, :].unsqueeze(3).broadcast_to([P, 1, heads, dim + 1]),
                                              ALU.mult))

            def add_up():
                return dve.tensor_reduce(acc[:, :], prod[:, :, :].rearrange("p s c -> p c s"), AX.X, ALU.add)

            def take_maximum():
                return c.go(dve.tensor_reduce(newmax[:, :], e5[:, :, :].rearrange("p s h -> p h s"), AX.X, ALU.max))

            def off_maximum():
                return dve.tensor_tensor(x5[:, :, :], e5[:, :, :],
                                         newmax[:, :].unsqueeze(1).broadcast_to([P, J + 1, heads]),
                                         ALU.subtract).then_inc(e_ready, 1)

            with dve.Fori(0, T) as t:
                g0, n = bounds(t)
                start(dve, c, t, acc, e5[:, J, :], work)
                dve.wait_ge(ga.landed, g0 + 1)
                for f in scores(dve, ga.group(g0), e5[:, 0:J, :], work):
                    c(f())
                c.until(take_maximum())
                off_maximum()
                c.reset()
                with dve.Fori(g0 + 1, g0 + n) as g:
                    dve.wait_ge(ga.landed, g + 1)
                    first, second = scores(dve, ga.group(g), e5[:, 0:J, :], work)
                    scored = c.go(first())
                    weigh_rows(g - 1)
                    c.until(scored)
                    scored = c.go(second())
                    weighed = weigh_sum()
                    c.until(scored)
                    highest = take_maximum()
                    c.until(weighed)
                    add_up()
                    c.until(highest)
                    off_maximum()
                    c.until(highest)
                    c.reset()
                weigh_rows(g0 + n - 1)
                c.until(weigh_sum())
                c(add_up())
                a3 = acc[:, :].rearrange("p (h c) -> p h c", h=heads)
                c(dve.tensor_scalar(rden[:, :], a3[:, :, dim], 1e-16, None, ALU.add))
                c(dve.reciprocal(rden[:, :], rden[:, :]))
                c(dve.tensor_tensor(k.out[:, ds(t, 1), :].rearrange("p t (h c) -> p (t h) c", h=heads),
                                    a3[:, :, 0:dim], rden[:, :].unsqueeze(2).broadcast_to([P, heads, dim]),
                                    ALU.mult))
                finish(dve, c, t)
                c.reset()

        @block.scalar
        def _(act):
            n = act.value_load(k.total[0:1, 0:1], min_val=1, max_val=GMAX)
            act.activation(warm[:, :], k.ones[:, 0:1], ACT.Exp)
            with act.Fori(0, n):
                take(act, e_ready)
                act.activation(p5[:, :, :], x5[:, :, :], ACT.Exp)
                act.activation(e5[:, J, :], newmax[:, :], ACT.Copy).then_inc(p_ready, 1)


def gat_conv(k, x, W, a_src, a_dst, bias, table, slot_src, elu):
    H, C = 4, 32
    VB = H * (C + 1)
    with ExitStack() as st:
        s = k.sub(st)
        wext = s.sb("wext", [P, D + 2 * H])
        arow, brow = s.sb("arow", [P, 2, D]), s.sb("brow", [P, D])
        tmp = s.sb("tmp", [P, D])
        own = s.sb("own", [P, T, VB + 2 * H])
        load(k, [(wext[:, 0:D], W), (arow[:, 0, :], rows(a_src.rearrange("h c -> (h c)"))),
                 (arow[:, 1, :], rows(a_dst.rearrange("h c -> (h c)"))), (brow[:, :], rows(bias))])
        with ExitStack() as st2:
            ch = k.sem("wchain")
            block = st2.enter_context(k.block())

            @block.vector
            def _(dve):
                c = Chain(dve, ch)
                for i in range(2):
                    c(dve.tensor_tensor(tmp[:, :], wext[:, 0:D], arow[:, i, :], ALU.mult))
                    c(dve.tensor_reduce(wext[:, D + i * H:D + (i + 1) * H],
                                        tmp[:, :].rearrange("p (h c) -> p h c", h=H), AX.X, ALU.add))
                c(dve.memset(own[:, :, :], 1.0))

        def store(dve, c, ps, t, n):
            c(dve.tensor_copy(own[:, ds(t, n), 0:VB].rearrange("p u (h c) -> p u h c", h=H)[:, :, :, 0:C],
                              ps[:, :, 0:D].rearrange("p u (h c) -> p u h c", h=H)))
            c(dve.tensor_copy(own[:, ds(t, n), VB:VB + 2 * H], ps[:, :, D:D + 2 * H]))

        dense_rows(k, x, [(wext[:, :], D + 2 * H, store)])
        scatter_table(k, table, own, VB + H, lambda row: row[:, VB:VB + H])

        def extra(s2):
            return s2.sb("ad", [P, H]), s2.sb("es", [P, J, H])

        def start(dve, c, t, acc, m, work):
            ad, _ = work
            o = own[:, ds(t, 1), :].rearrange("p t c -> p (t c)")
            c(dve.tensor_copy(acc[:, :], o[:, 0:VB]))
            c(dve.tensor_copy(ad[:, :], o[:, VB + H:VB + 2 * H]))
            c(dve.tensor_tensor(m, o[:, VB:VB + H], ad[:, :], ALU.add))
            c(dve.scalar_tensor_tensor(m, m, 0.2, m, ALU.mult, ALU.max))

        def scores(dve, g, e, work):
            ad, es = work
            return (lambda: dve.tensor_tensor(es[:, :, :], g[:, :, VB:VB + H],
                                              ad[:, :].unsqueeze(1).broadcast_to([P, J, H]), ALU.add),
                    lambda: dve.scalar_tensor_tensor(e, es[:, :, :], 0.2, es[:, :, :], ALU.mult, ALU.max))

        def finish(dve, c, t):
            o = k.out[:, ds(t, 1), :].rearrange("p t c -> p (t c)")
            c(dve.tensor_tensor(o, o, brow[:, :], ALU.add))

        attention_pass(k, table, slot_src, VB + H, H, C, own, scores, start, finish, extra)
    if elu:
        with ExitStack() as st:
            s = k.sub(st)
            neg = s.sb("neg", [P, NP])
            ch, n_ready, e_ready = k.sem("eluchain"), k.sem("neg_ready"), k.sem("exp_ready")
            block = st.enter_context(k.block())
            o = flat2(k.out[:, :, :])

            @block.vector
            def _(dve):
                c = Chain(dve, ch)
                c(dve.tensor_scalar(neg[:, :], o, 0.0, None, ALU.min))
                dve.sem_inc(n_ready, 1)
                dve.wait_ge(e_ready, 1)
                c(dve.tensor_scalar(neg[:, :], neg[:, :], -1.0, None, ALU.add))
                c(dve.scalar_tensor_tensor(o, o, 0.0, neg[:, :], ALU.max, ALU.add))

            @block.scalar
            def _(act):
                act.wait_ge(n_ready, 1)
                act.activation(neg[:, :], neg[:, :], ACT.Exp).then_inc(e_ready, 1)


def scatter_weights(k, dense, slot_src, slot_weight):
    nc = k.nc
    with ExitStack() as st:
        s = k.sub(st)
        sl, wl = s.sb("sl", [P, B7, J], I32), s.sb("wl", [P, B7, J])
        slot, valid = s.sb("slot", [P, B7, J]), s.sb("valid", [P, B7, J])
        nexti, nextw = s.sb("nexti", [P, B7, J], I32), s.sb("nextw", [P, B7, J])
        flat, wv = s.sb("flat", [P, B7, J], I32), s.sb("wv", [P, B7, J])
        posb, pos13 = s.sb("posb", [P, B7], I32), s.sb("pos13", [P, T], I32)
        degb = s.sb("degb", [P, B7])
        slots_in, slots_free, flat_ready, scattered, ch, dt, pt, st_ = (k.sem(x) for x in (
            "slots_in", "slots_free", "flat_ready", "scattered", "swchain", "sw_dt", "sw_pt", "sw_st"))
        done = [k.sem(f"added{u}") for u in range(B7)]
        block = st.enter_context(k.block())

        def bounds(eng, b):
            n = eng.value_load(k.bgroups[0:1, ds(b, 1)], min_val=1, max_val=GMAX)
            j0 = eng.value_load(k.bgroup0[0:1, ds(b, 1)], min_val=0, max_val=GMAX)
            return j0, n

        @block.sync
        def _(sp):
            with sp.Fori(0, NB) as b:
                j0, n = bounds(sp, b)
                g0 = [sp.value_load(k.group0[0:1, ds(b * B7 + u, 1)], min_val=0, max_val=GMAX)
                      for u in range(B7)]
                with sp.Fori(j0, j0 + n) as jj:
                    take(sp, slots_free)
                    for u in range(B7):
                        at = ds((g0[u] + (jj - j0)).with_bounds(min_val=0, max_val=GMAX - 1), 1)
                        sp.dma_start(sl[:, u, :], slot_src[at, :, :].rearrange("g p j -> (g p) j")
                                     ).then_inc(slots_in, 16)
                        sp.dma_start(wl[:, u, :], slot_weight[at, :, :].bitcast(F32).rearrange("g p j -> (g p) j")
                                     ).then_inc(slots_in, 16)

        @block.vector
        def _(dve):
            c = Chain(dve, ch)
            hold = Hold(dve, dt)
            c(dve.tensor_single_scalar(pos13[:, :], k.pos[:, :], 13, ALU.logical_shift_left))
            c.reset()
            dve.sem_inc(slots_free, 1)
            dve.sem_inc(scattered, 1)
            with dve.Fori(0, NB) as b:
                j0, n = bounds(dve, b)
                c(dve.tensor_copy(degb[:, :], k.deg[:, ds(b * B7, B7)]))
                c(dve.tensor_copy(posb[:, :], pos13[:, ds(b * B7, B7)]))
                c(dve.tensor_copy(slot[:, :, :], k.ramp[:, 0:J].unsqueeze(1).broadcast_to([P, B7, J])))
                c.reset()
                with dve.Fori(j0, j0 + n) as jj:
                    hold(slots_in, 16 * 2 * B7 * (jj + 1))
                    c(dve.tensor_tensor(valid[:, :, :], slot[:, :, :],
                                        degb[:, :].unsqueeze(2).broadcast_to([P, B7, J]), ALU.is_lt))
                    c(dve.tensor_scalar(slot[:, :, :], slot[:, :, :], float(J), None, ALU.add))
                    c(dve.scalar_tensor_tensor(valid[:, :, :], sl[:, :, :], float(-DUMMY), valid[:, :, :],
                                               ALU.add, ALU.mult))
                    c(dve.tensor_scalar(nexti[:, :, :], valid[:, :, :], float(DUMMY), None, ALU.add))
                    c(dve.tensor_tensor(nexti[:, :, :], nexti[:, :, :],
                                        posb[:, :].unsqueeze(2).broadcast_to([P, B7, J]), ALU.bitwise_or))
                    c(dve.tensor_copy(nextw[:, :, :], wl[:, :, :]))
                    dve.sem_inc(slots_free, 1)
                    take(dve, scattered)
                    c(dve.tensor_copy(flat[:, :, :], nexti[:, :, :]))
                    c(dve.tensor_copy(wv[:, :, :], nextw[:, :, :]))
                    dve.sem_inc(flat_ready, 1)
                    c.reset()

        @block.gpsimd
        def _(pool):
            hold = Hold(pool, pt)
            with pool.Fori(0, NB) as b:
                j0, n = bounds(pool, b)
                with pool.Fori(j0, j0 + n) as jj:
                    take(pool, flat_ready)
                    for j in range(J):
                        for u in range(B7):
                            if j:
                                hold(done[u], 16 * (J * jj + j))
                            pool.indirect_dma_start(
                                dense, bass.IndirectOffsetOnAxis(flat[:, u, j:j + 1], 0), wv[:, u, j:j + 1],
                                None, compute_op=ALU.add).then_inc(done[u], 16)
                    for u in range(B7):
                        hold(done[u], 16 * (J * jj + J))
                    pool.sem_inc(scattered, 1)


def sum_by_source(k, x, dense, fnt):
    nc = k.nc
    HALF, UN = NP // 2, 4
    MM = 448
    with ExitStack() as st:
        s = k.sub(st)
        mat = s.sb("mat", [P, UN, HALF])
        xs = s.sb("xs", [P, UN, D])
        acc = s.ps("fsum", [P, HALF // MM, 512])
        m_in = [k.sem(f"mat{u}_in") for u in range(UN)]
        m_free, x_ready = [k.sem(f"mfree{u}") for u in range(UN)], [k.sem(f"xs_ready{u}") for u in range(UN)]
        x_free = [k.sem(f"xs_free{u}") for u in range(UN)]
        ch, acc_done, acc_out, turns = (k.sem(x) for x in ("sschain", "acc_done", "acc_out", "ss_turns"))
        block = st.enter_context(k.block())
        view = dense.rearrange("(t p c) o -> t p (c o)", p=P, c=PITCH)
        IT = (T - 1) // UN

        @block.sync
        def _(sp):
            for h in range(2):
                def fetch(t, u):
                    take(sp, m_free[u])
                    sp.dma_start(mat[:, u, :], view[ds(t, 1), :, h * HALF:(h + 1) * HALF]
                                 .rearrange("t p c -> (t p) c")).then_inc(m_in[u], 16)
                fetch(0, 0)
                with sp.Fori(0, IT) as i:
                    for u in range(UN):
                        fetch(1 + UN * i + u, (u + 1) % UN)

        @block.vector
        def _(dve):
            c = Chain(dve, ch)
            for u in range(UN):
                dve.sem_inc(m_free[u], 1)
                dve.sem_inc(x_free[u], 1)
            for h in range(2):
                def stage(t, u):
                    take(dve, x_free[u])
                    c(dve.tensor_copy(xs[:, u, :], flat2(x[:, ds(t, 1), :])))
                    dve.sem_inc(x_ready[u], 1)
                stage(0, 0)
                c.reset()
                with dve.Fori(0, IT) as i:
                    for u in range(UN):
                        stage(1 + UN * i + u, (u + 1) % UN)
                    c.reset()
                dve.wait_ge(acc_done, h + 1)
                for m in range(HALF // MM):
                    c(dve.tensor_copy(fnt[:, h * HALF + m * MM:h * HALF + (m + 1) * MM], acc[:, m, 0:MM]))
                c.reset()
                dve.sem_inc(acc_out, 1)

        @block.tensor
        def _(pe):
            hold = Hold(pe, turns)
            for h in range(2):
                def product(u, count, start):
                    hold(m_in[u], count)
                    take(pe, x_ready[u])
                    for m in range(HALF // MM):
                        mm = pe.matmul(acc[:, m, 0:MM], xs[:, u, :], mat[:, u, m * MM:(m + 1) * MM],
                                       start=start, stop=start, skip_group_check=True)
                    mm.then_inc(m_free[u], 1)
                if h:
                    pe.wait_ge(acc_out, 1)
                each = [IT + (u == 0) for u in range(UN)]
                product_free(pe, product, 0, 16 * (h * each[0] + 1), True, x_free)
                with pe.Fori(0, IT) as i:
                    for u in range(UN):
                        v = (u + 1) % UN
                        product_free(pe, product, v, 16 * (h * each[v] + (v == 0) + 1) + 16 * i, False, x_free)
                pe.drain().then_inc(acc_done, 1)


def product_free(pe, product, u, count, start, x_free):
    product(u, count, start)
    pe.drain().then_inc(x_free[u], 1)


def residual_layer(k, x, w_self_t, b_self, w_neigh_t, b_neigh, scale, offset, dense, slot_src, slot_weight,
                   by_node):
    scatter_weights(k, dense, slot_src, slot_weight)
    with ExitStack() as st:
        s = k.sub(st)
        ws, wn = s.sb("ws", [P, D]), s.sb("wn", [P, D])
        br, sc, of = s.sb("br", [P, 2, D]), s.sb("sc", [P, 2 * D]), s.sb("of", [P, 2 * D])
        own = s.sb("selfrows", [P, T, D])
        load(k, [(ws[:, :], w_self_t), (wn[:, :], w_neigh_t), (br[:, 0, :], rows(b_self)),
                 (br[:, 1, :], rows(b_neigh)), (sc[:, :], rows(scale)), (of[:, :], rows(offset))])

        def store(dst, bias):
            def f(dve, c, ps, t, n):
                o = dst[:, ds(t, n), :]
                c(dve.tensor_tensor(o, ps, bias.unsqueeze(1).broadcast_to([P, n, D]), ALU.add))
                c(dve.tensor_scalar(o, o, 0.0, None, ALU.max))
            return f

        dense_rows(k, x, [(ws[:, :], D, store(own, br[:, 0, :]))])
        layernorm(k, own[:, :, :], own[:, :, :], 1e-9, sc[:, 0:D], of[:, 0:D])
        with ExitStack() as st2:
            s2 = k.sub(st2)
            fnt = s2.sb("fnt", [P, NP])
            sum_by_source(k, x, dense, fnt)
            transpose_blocks(k, fnt, flat2(k.out[:, :, :]))
        dense_rows(k, k.out[:, :, :], [(wn[:, :], D, store(k.out, br[:, 1, :]))])
        layernorm(k, k.out[:, :, :], k.out[:, :, :], 1e-9, sc[:, D:2 * D], of[:, D:2 * D])
        with ExitStack() as st3:
            done = k.sem("by_node_out")
            block = st3.enter_context(k.block())

            @block.sync
            def _(sp):
                sp.dma_start(by_node.rearrange("(t p) c -> p t c", p=P), k.out[:, :, :]).then_inc(done, 16)
                sp.wait_ge(done, 16)
        gather_rows(k, by_node, k.out[:, :, :], k.node)
        add_rows(k, k.out[:, :, :], k.out[:, :, :], own[:, :, :])
        add_rows(k, k.out[:, :, :], k.out[:, :, :], x)
    layernorm(k, k.out[:, :, :], x, 1e-5)


def dense_cols(k, src, weights, store, blocks=1):
    nc = k.nc
    with ExitStack() as st:
        s = k.sub(st)
        acc = s.ps("dcacc", [P, len(weights), 512])
        done, free, ch = k.sem("dc_done"), k.sem("dc_free"), k.sem("dcchain")
        block = st.enter_context(k.block())

        @block.tensor
        def _(pe):
            with pe.Fori(0, NBLK) as i:
                take(pe, free)
                for o, ws in enumerate(weights):
                    for b, w in enumerate(ws):
                        mm = pe.matmul(acc[:, o, 0:BLK], w, src[b][:, ds(i * BLK, BLK)], start=(b == 0),
                                       stop=(b == len(ws) - 1))
                mm.then_inc(done, 1)

        @block.vector
        def _(dve):
            c = Chain(dve, ch)
            dve.sem_inc(free, 1)
            with dve.Fori(0, NBLK) as i:
                take(dve, done)
                for o in range(len(weights)):
                    store(dve, c, acc[:, o, 0:BLK], i, o)
                c.reset()
                dve.sem_inc(free, 1)


def scale_shift(dve, c, act_std, mean, var, gamma, beta, scale, shift):
    act_std()
    c(dve.reciprocal(scale, var))
    c(dve.tensor_tensor(scale, scale, gamma, ALU.mult))
    c(dve.tensor_tensor(shift, mean, scale, ALU.mult))
    c(dve.tensor_tensor(shift, beta, shift, ALU.subtract))


def batchnorm_cols(k, a, gamma, beta):
    nc = k.nc
    with ExitStack() as st:
        s = k.sub(st)
        parts = split(N, 512)
        stats, mv, sc, sh, ep = (s.sb(x, sh_) for x, sh_ in (("stats", [P, len(parts), 6]), ("mv", [P, 2]),
                                                            ("sc", [P, 1]), ("sh", [P, 1]), ("ep", [P, 1])))
        ch, v_ready, s_ready = k.sem("bnchain"), k.sem("bn_var"), k.sem("bn_std")
        block = st.enter_context(k.block())

        @block.vector
        def _(dve):
            c = Chain(dve, ch)
            c(dve.memset(ep[:, :], 1e-5))
            for i, (at, n) in enumerate(parts):
                c(dve.bn_stats(stats[:, i, :], a[:, at:at + n]))
            c(dve.bn_aggr(mv[:, :], stats[:, :, :]))

            def std():
                dve.sem_inc(v_ready, 1)
                dve.wait_ge(s_ready, 1)
            scale_shift(dve, c, std, mv[:, 0:1], mv[:, 1:2], gamma, beta, sc[:, :], sh[:, :])
            c(dve.tensor_scalar(a[:, :], a[:, :], sc[:, 0:1], sh[:, 0:1], ALU.mult, ALU.add))

        @block.scalar
        def _(act):
            act.wait_ge(v_ready, 1)
            act.activation(mv[:, 1:2], mv[:, 1:2], ACT.Sqrt, bias=ep[:, 0:1]).then_inc(s_ready, 1)


def attention_layer(k, x, w, table, slot_src):
    H, C = 8, 16
    VB = H * (C + 1)
    F = 512
    with ExitStack() as st:
        s = k.sub(st)
        with ExitStack() as st1:
            s1 = k.sub(st1)
            wq, wk, wv = (s1.sb(n, [P, D]) for n in ("wq", "wk", "wv"))
            qb = s1.sb("qb", [P, D])
            kv = s1.sb("kv", [P, T, 2 * VB])
            q = s1.sb("q", [P, T, VB])
            load(k, [(wq[:, :], w["q_w"]), (wk[:, :], w["k_w"]), (wv[:, :], w["v_w"]), (qb[:, :], rows(w["q_b"]))])
            with ExitStack() as st2:
                block = st2.enter_context(k.block())

                @block.vector
                def _(dve):
                    dve.memset(kv[:, :, 0:VB], 1.0)
                    dve.memset(kv[:, :, VB:2 * VB], 0.0)
                    dve.memset(q[:, :, :], 1.0)

            def heads(ap):
                return ap.rearrange("p u (h c) -> p u h c", h=H)

            def store_v(dve, c, ps, t, n):
                c(dve.tensor_copy(heads(kv[:, ds(t, n), 0:VB])[:, :, :, 0:C], heads(ps)))

            def store_k(dve, c, ps, t, n):
                c(dve.tensor_copy(heads(kv[:, ds(t, n), VB:2 * VB])[:, :, :, 0:C], heads(ps)))

            def store_q(dve, c, ps, t, n):
                for u in range(n):
                    qq = q[:, ds(t + u, 1), :].rearrange("p u (h c) -> p (u h) c", h=H)[:, :, 0:C]
                    c(dve.tensor_tensor(qq, ps[:, u, :].rearrange("p (h c) -> p h c", h=H),
                                        qb[:, :].rearrange("p (h c) -> p h c", h=H), ALU.add))
                    c(dve.tensor_scalar(qq, qq, float(C) ** -0.5, None, ALU.mult))

            dense_rows(k, x, [(wv[:, :], D, store_v), (wk[:, :], D, store_k), (wq[:, :], D, store_q)])
            scatter_table(k, table, kv, 2 * VB,
                          lambda row: row[:, VB:2 * VB].rearrange("p (h c) -> p h c", h=H)[:, :, C:C + 1])

            def extra(s2):
                return s2.sb("qt", [P, VB]), s2.sb("qk", [P, J, VB])

            def start(dve, c, t, acc, m, work):
                qt, qk = work
                o = kv[:, ds(t, 1), :].rearrange("p t c -> p (t c)")
                c(dve.tensor_copy(acc[:, :], o[:, 0:VB]))
                c(dve.tensor_copy(qt[:, :], flat2(q[:, ds(t, 1), :])))
                c(dve.tensor_tensor(qk[:, 0, :], o[:, VB:2 * VB], qt[:, :], ALU.mult))
                c(dve.tensor_reduce(m, qk[:, 0, :].rearrange("p (h c) -> p h c", h=H), AX.X, ALU.add))

            def scores(dve, g, e, work):
                qt, qk = work
                return (lambda: dve.tensor_tensor(qk[:, :, :], g[:, :, VB:2 * VB],
                                                  qt[:, :].unsqueeze(1).broadcast_to([P, J, VB]), ALU.mult),
                        lambda: dve.tensor_reduce(e, qk[:, :, :].rearrange("p s (h c) -> p s h c", h=H), AX.X,
                                                  ALU.add))

            attention_pass(k, table, slot_src, 2 * VB, H, C, kv, scores, start, lambda *a: None, extra)
        wo, l1, l2 = s.sb("wo", [P, D]), s.sb("l1", [P, F]), s.sb("l2", [P, F // P, D])
        vec = s.sb("vec", [P, 16])
        xt, st_ = s.sb("xt2", [P, NP]), s.sb("ot2", [P, NP])
        names = ("out_b", "g1", "b1", "lin2_b", "g2", "b2")
        load(k, [(wo[:, :], w["out_w"]), (l1[:, :], w["lin1_w"]),
                 (l2[:, :, :], w["lin2_w"].rearrange("(f p) d -> p f d", p=P)),
                 (vec[:, 8:12], w["lin1_b"])] +
             [(vec[:, i:i + 1], w[n]) for i, n in enumerate(names)])
        col = {n: vec[:, i:i + 1] for i, n in enumerate(names)}
        transpose_blocks(k, flat2(x), xt)
        transpose_blocks(k, flat2(k.out[:, :, :]), st_)

        def add_attn(dve, c, ps, i, o):
            a = xt[:, ds(i * BLK, BLK)]
            c(dve.scalar_tensor_tensor(a, ps, col["out_b"], a, ALU.add, ALU.add))

        dense_cols(k, [st_], [[wo[:, :]]], add_attn)
        batchnorm_cols(k, xt, col["g1"], col["b1"])
        with ExitStack() as st3:
            s3 = k.sub(st3)
            hid = [s3.sb(f"hid{f}", [P, NP]) for f in range(F // P - 2)] + [st_]
            hid.append(k.out[:, :, :].rearrange("p t c -> p (t c)"))

            def hidden(dve, c, ps, i, o):
                h = hid[o][:, ds(i * BLK, BLK)]
                c(dve.tensor_scalar(h, ps, vec[:, 8 + o:9 + o], None, ALU.add))
                c(dve.scalar_tensor_tensor(h, h, 0.01, h, ALU.mult, ALU.max))

            def add_ff(dve, c, ps, i, o):
                a = xt[:, ds(i * BLK, BLK)]
                c(dve.scalar_tensor_tensor(a, ps, col["lin2_b"], a, ALU.add, ALU.add))

            dense_cols(k, [xt], [[l1[:, f * P:(f + 1) * P]] for f in range(F // P)], hidden)
            dense_cols(k, hid, [[l2[:, f, :] for f in range(F // P)]], add_ff)
        batchnorm_cols(k, xt, col["g2"], col["b2"])
        transpose_blocks(k, xt, flat2(k.out[:, :, :]))
        add_rows(k, k.out[:, :, :], k.out[:, :, :], x)
    layernorm(k, k.out[:, :, :], x, 1e-5)


def edge_mlp_layer(k, x, w, table, slot_src, kept, empty_dram, cnt_dram, out):
    nc = k.nc
    with ExitStack() as st:
        s = k.sub(st)
        th, ph, fc = s.sb("th", [P, D]), s.sb("ph", [P, D]), s.sb("fc", [P, D])
        vec = s.sb("vec3", [P, 4])
        at = s.sb("at", [P, NP])
        sums = s.sb("sums", [P, 8])
        coef = s.sb("coef", [P, 4])
        load(k, [(th[:, :], w["theta_w"]), (ph[:, :], w["phi_w"]), (fc[:, :], w["fc1_w"])] +
             [(vec[:, i:i + 1], w[n]) for i, n in enumerate(("bn0_g", "bn0_b", "bn1_g", "bn1_b"))])
        with ExitStack() as st1:
            block = st1.enter_context(k.block())
            ch1 = k.sem("l3c")

            @block.vector
            def _(dve):
                c = Chain(dve, ch1)
                c(dve.tensor_tensor(ph[:, :], ph[:, :], th[:, :], ALU.subtract))

        def store_b(dve, c, ps, t, n):
            c(dve.tensor_copy(k.out[:, ds(t, n), :], ps))

        dense_rows(k, x, [(ph[:, :], D, store_b)])
        scatter_table(k, table, k.out, D, None)
        degr, empr = s.sb("degr", [P, NP]), s.sb("empr", [P, NP])
        with ExitStack() as st1:
            s1 = k.sub(st1)
            tt = s1.sb("tt", [T, 2, P])
            pt = s1.ps("pt", [T, 2, P])
            a_, b_, c_ = k.sem("dr_t"), k.sem("dr_c"), k.sem("dr_o")
            d_ = k.sem("dr_i")
            block = st1.enter_context(k.block())

            @block.tensor
            def _(pe):
                pe.transpose(pt[:, 0, :], k.deg[:, :], k.ident[:, :])
                pe.transpose(pt[:, 1, :], k.empty[:, :], k.ident[:, :]).then_inc(a_, 1)

            @block.vector
            def _(dve):
                dve.wait_ge(a_, 1)
                dve.tensor_copy(tt[:, :, :], pt[:, :, :]).then_inc(b_, 1)

            @block.sync
            def _(sp):
                sp.wait_ge(b_, 1)
                sp.dma_start(cnt_dram.rearrange("(t p) -> t p", p=P), tt[:, 0, :]).then_inc(c_, 16)
                sp.dma_start(empty_dram.rearrange("(t p) -> t p", p=P), tt[:, 1, :]).then_inc(c_, 16)
                sp.wait_ge(c_, 32)
                sp.dma_start(degr[:, :], rows(cnt_dram)).then_inc(d_, 16)
                sp.dma_start(empr[:, :], rows(empty_dram)).then_inc(d_, 16)
                sp.wait_ge(d_, 32)

        hT = s.sb("hT", [P, NP])
        transpose_blocks(k, flat2(x), hT)

        def store_a(dve, c, ps, i, o):
            c(dve.tensor_copy(at[:, ds(i * BLK, BLK)], ps))

        dense_cols(k, [hT], [[th[:, :]]], store_a)

        sbt = hT

        edge_stats(k, table, slot_src, sbt, sums, kept)
        edge_bn0(k, at, sbt, degr, sums, vec, coef)
        edge_kept(k, at, fc, coef, sums, None, kept)
        edge_regather(k, table, slot_src, at, fc, coef, sums, None)
        edge_dummy(k, at, fc, coef, sums, empr, vec, hT, False)
        agg = k.out[:, :, :].rearrange("p t c -> p (t c)")
        edge_kept(k, at, fc, coef, sums, agg, kept)
        edge_regather(k, table, slot_src, at, fc, coef, sums, agg)
        edge_dummy(k, at, fc, coef, sums, empr, vec, hT, True)
        with ExitStack() as st1:
            ch = k.sem("l3e")
            block = st1.enter_context(k.block())

            @block.vector
            def _(dve):
                c = Chain(dve, ch)
                c(dve.tensor_tensor(agg, agg, hT[:, :], ALU.subtract))
                c(dve.tensor_scalar(degr[:, :], degr[:, :], 1.0, None, ALU.max))
                c(dve.reciprocal(degr[:, :], degr[:, :]))
                c(dve.tensor_tensor(hT[:, :], agg, degr[:, :], ALU.mult))
        transpose_blocks(k, hT, agg)
        with ExitStack() as st1:
            ch = k.sem("l3f")
            block = st1.enter_context(k.block())
            o, xx = k.out[:, :, :], x

            @block.vector
            def _(dve):
                c = Chain(dve, ch)
                c(dve.tensor_tensor(o, o, xx, ALU.add))
                c(dve.scalar_tensor_tensor(o, o, 0.0, xx, ALU.max, ALU.add))
    layernorm(k, k.out[:, :, :], k.out[:, :, :], 1e-5)
    with ExitStack() as st:
        done = k.sem("out_written")
        block = st.enter_context(k.block())

        @block.gpsimd
        def _(pool):
            for t in range(T):
                n = P if t < T - 1 else LAST
                pool.indirect_dma_start(out, bass.IndirectOffsetOnAxis(k.node[0:n, t:t + 1], 0),
                                        k.out[0:n, t, :], None).then_inc(done, 16)
            pool.wait_ge(done, 16 * T)


def rounds(k, eng):
    return eng.value_load(k.total[0:1, 1:2], min_val=1, max_val=GMAX // R)


def edge_stats(k, table, slot_src, sbt, sums, kept):
    with ExitStack() as st:
        s = k.sub(st)
        ga = Gather(k, s, table, D, slot_src)
        tb, sq = s.sb("tb", [P, R, J * P]), s.sb("sq", [P, R, J * P])
        part, total = s.sb("part", [P, R]), s.sb("sqtotal", [P, 1])
        bsum = s.sb("bsum", [P, D])
        bacc = s.sb("bacc", [P, D])
        bt = s.ps("bt", [P, R, 512])
        turns, aturns, pturns, ch, copied, read, used, clear = (k.sem(n) for n in (
            "turns", "aturns", "pturns", "ch", "copied", "read", "tb_used", "tb_clear"))
        stored = [k.sem(f"stored{r}") for r in range(R)]
        block = st.enter_context(k.block())
        block.gpsimd(ga.pool)
        block.sync(ga.sync)

        @block.vector
        def _(dve):
            c = Chain(dve, ch)
            hold = Hold(dve, turns)
            for sem in (ga.used, read, used):
                dve.sem_inc(sem, R)
            c(dve.memset(tb[:, :, :], 0.0))
            dve.sem_inc(clear, 1)
            c(dve.memset(total[:, :], 0.0))
            c.reset()
            bounds = tiles_loop(k, dve)
            with dve.Fori(0, T) as t:
                g0, n = bounds(t)
                c(dve.memset(bacc[:, :], 0.0))
                c.reset()
                with dve.Fori(g0, g0 + n) as g:
                    hold(read, g + 1 + R)
                    c(dve.tensor_reduce(bsum[:, :], tb[:, ds(g % R, 1), :].rearrange(
                        "p r (j c) -> p (r c) j", j=J), AX.X, ALU.add))
                    c.go(dve.tensor_tensor(total[:, :], total[:, :], part[:, ds(g % R, 1)], ALU.add))
                    c(dve.tensor_tensor(bacc[:, :], bacc[:, :], bsum[:, :], ALU.add))
                    dve.sem_inc(used, 1)
                    c.reset()
                c(dve.tensor_copy(sbt[:, ds(t * P, P)], bacc[:, :]))
                c.reset()
            c(dve.tensor_copy(sums[:, 0:1], total[:, :]))

        @block.tensor
        def _(pe):
            hold = Hold(pe, pturns)
            with pe.Fori(0, rounds(k, pe)) as i:
                for r in range(R):
                    hold(ga.landed, R * i + r + 1)
                    hold(read, R * i + r + 1)
                    for j in range(J):
                        mm = pe.transpose(bt[:, r, j * P:(j + 1) * P], ga.ring[:, r * J + j, :], k.ident[:, :])
                    mm.then_inc(ga.used, 1)

        @block.scalar
        def _(act):
            hold = Hold(act, aturns)

            def store(r, group):
                act.dma_start(kept[ds(group, 1), :, :].rearrange("g p c -> (g p) c"),
                              tb[:, r, :]).then_inc(stored[r], 16)

            act.wait_ge(clear, 1)
            for r in range(R):
                store(r, CAP + r)
            n = rounds(k, act)
            with act.Fori(0, n) as i:
                for r in range(R):
                    hold(ga.used, R * i + r + 1 + R)
                    hold(used, R * i + r + 1)
                    hold(stored[r], 16 * (i + 1))
                    act.activation(tb[:, r, :], bt[:, r, :], ACT.Copy).then_inc(copied, 1)
                    act.activation(sq[:, r, :], bt[:, r, :], ACT.Square,
                                   accum_out=part[:, r:r + 1]).then_inc(read, 1)
                    hold(copied, R * i + r + 1)
                    store(r, ((R * i + r) % CAP).with_bounds(min_val=0, max_val=CAP - 1))
            for r in range(R):
                hold(stored[r], 16 * (n + 1))


def finish_bn(k, sums, mean_col, sq_col, gamma, beta, scale, shift):
    with ExitStack() as st:
        s = k.sub(st)
        m, v, t, ep = (s.sb(n, [P, 1]) for n in ("m", "v", "t", "ep"))
        ch, a_, b_ = k.sem("fbch"), k.sem("fba"), k.sem("fbb")
        block = st.enter_context(k.block())

        @block.vector
        def _(dve):
            c = Chain(dve, ch)
            c(dve.memset(ep[:, :], 1e-5))
            c(dve.tensor_scalar(m[:, :], sums[:, mean_col:mean_col + 1], 1.0 / E, None, ALU.mult))
            c(dve.tensor_scalar(v[:, :], sums[:, sq_col:sq_col + 1], 1.0 / E, None, ALU.mult))
            c(dve.tensor_tensor(t[:, :], m[:, :], m[:, :], ALU.mult))
            c(dve.tensor_tensor(v[:, :], v[:, :], t[:, :], ALU.subtract))
            c(dve.tensor_scalar(v[:, :], v[:, :], 0.0, None, ALU.max))

            def std():
                dve.sem_inc(a_, 1)
                dve.wait_ge(b_, 1)
            scale_shift(dve, c, std, m[:, :], v[:, :], gamma, beta, scale, shift)

        @block.scalar
        def _(act):
            act.wait_ge(a_, 1)
            act.activation(v[:, :], v[:, :], ACT.Sqrt, bias=ep[:, 0:1]).then_inc(b_, 1)


def edge_bn0(k, at, sbt, degr, sums, vec, coef):
    with ExitStack() as st:
        s = k.sub(st)
        da, junk = s.sb("da", [P, NP]), s.sb("junk3", [P, NP])
        ch = k.sem("bn0ch")
        with ExitStack() as st1:
            block = st1.enter_context(k.block())

            @block.vector
            def _(dve):
                c = Chain(dve, ch)
                c(dve.tensor_tensor(da[:, :], degr[:, :], at[:, :], ALU.mult))
                c(dve.tensor_reduce(sums[:, 1:2], da[:, :], AX.X, ALU.add))
                c(dve.tensor_reduce(sums[:, 2:3], sbt[:, :], AX.X, ALU.add))
                c(dve.tensor_tensor(sums[:, 4:5], sums[:, 1:2], sums[:, 2:3], ALU.add))
                c(dve.scalar_tensor_tensor(junk[:, :], sbt[:, :], 2.0, da[:, :], ALU.mult, ALU.add))
                c(dve.tensor_tensor(junk[:, :], junk[:, :], at[:, :], ALU.mult))
                c(dve.tensor_reduce(sums[:, 3:4], junk[:, :], AX.X, ALU.add))
                c(dve.tensor_tensor(sums[:, 5:6], sums[:, 0:1], sums[:, 3:4], ALU.add))
        finish_bn(k, sums, 4, 5, vec[:, 0:1], vec[:, 1:2], coef[:, 0:1], coef[:, 1:2])
        ch2 = k.sem("bn0ch2")
        with ExitStack() as st1:
            block = st1.enter_context(k.block())

            @block.vector
            def _(dve):
                c = Chain(dve, ch2)
                c(dve.tensor_scalar(at[:, :], at[:, :], coef[:, 0:1], coef[:, 1:2], ALU.mult, ALU.add))
                c(dve.memset(sums[:, :], 0.0))


def edge_kept(k, at, fc, coef, sums, agg, kept):
    with ExitStack() as st:
        s = k.sub(st)
        W = J * P
        tb, pre, r4, z = (s.sb(n, [P, R, W]) for n in ("tb", "pre", "r4", "z"))
        att = s.sb("att", [P, D])
        part = s.sb("part", [P, 2, CAP])
        zsum, zacc = s.sb("zsum", [P, D]), s.sb("zacc", [P, D])
        e1 = s.ps("e1", [P, R, 512])
        landed, made, relued, product, posted, zused, ch, vt, at_, pt, st_, gt, zero = (k.sem(n) for n in (
            "landed", "pre_made", "relued", "product", "posted", "z_used", "ch", "vt", "at_", "pt", "st_", "gt",
            "part_zero"))
        loaded = [k.sem(f"tb{r}_in") for r in range(R)]
        block = st.enter_context(k.block())

        def when(eng):
            return eng.If(rounds(k, eng) <= CAP // R)

        def slot(ring, g):
            return ring[:, ds(g % R, 1), :].rearrange("p r c -> p (r c)")

        @block.sync
        def _(sp):
            hold = Hold(sp, st_)
            with when(sp):
                with sp.Fori(0, rounds(k, sp)) as i:
                    for r in range(R):
                        g = (R * i + r).with_bounds(min_val=0, max_val=CAP - 1)
                        hold(made, R * i + r + 1)
                        sp.dma_start(tb[:, r, :], kept[ds(g, 1), :, :].rearrange("g p c -> (g p) c")
                                     ).then_inc(loaded[r], 16)

        @block.gpsimd
        def _(pool):
            with when(pool):
                with pool.Fori(0, rounds(k, pool)) as i:
                    for r in range(R):
                        pool.wait_ge(loaded[r], 16 * (i + 1))
                        pool.sem_inc(landed, 1)

        @block.vector
        def _(dve):
            c = Chain(dve, ch)
            hold = Hold(dve, vt)
            with when(dve):
                for sem in (made, relued, posted, zused):
                    dve.sem_inc(sem, R)
                c(dve.memset(part[:, :, :], 0.0))
                c.reset()
                dve.sem_inc(zero, 1)
                bounds = tiles_loop(k, dve)

                def take_tile(t):
                    c(dve.tensor_copy(att[:, :], at[:, ds(t * P, P)]))
                    c.reset()

                def scale_shift_rows(g):
                    hold(landed, g + 1)
                    dve.wait_ge(relued, g + 1)
                    dve.scalar_tensor_tensor(
                        slot(pre, g).rearrange("p (j c) -> p j c", j=J),
                        slot(tb, g).rearrange("p (j c) -> p j c", j=J), coef[:, 0:1],
                        att[:, :].unsqueeze(1).broadcast_to([P, J, D]), ALU.mult, ALU.add).then_inc(made, 1)

                def add_group(g):
                    hold(posted, g + 1 + R)
                    c(dve.tensor_reduce(zsum[:, :], slot(z, g).rearrange("p (j c) -> p c j", j=J), AX.X, ALU.add))
                    dve.sem_inc(zused, 1)
                    c(dve.tensor_tensor(zacc[:, :], zacc[:, :], zsum[:, :], ALU.add))
                    c.reset()

                if agg is None:
                    with dve.Fori(0, T) as t:
                        g0, n = bounds(t)
                        take_tile(t)
                        with dve.Fori(g0, g0 + n) as g:
                            scale_shift_rows(g)
                        dve.wait_ge(made, g0 + n + R)
                        c.go(dve.memset(zacc[:, :], 0.0))
                        c.until(c.n)
                        c.reset()
                    total = dve.value_load(k.total[0:1, 0:1], min_val=1, max_val=GMAX)
                    hold(posted, total + R)
                    for q in range(2):
                        c(dve.tensor_reduce(sums[:, q:q + 1], part[:, q, :], AX.X, ALU.add))
                else:
                    take_tile(0)
                    for g in range(2):
                        scale_shift_rows(g)

                    def tile(t, last):
                        g0, n = bounds(t)
                        c(dve.memset(zacc[:, :], 0.0))
                        c.reset()
                        with dve.Fori(g0, g0 + n - 2) as g:
                            scale_shift_rows(g + 2)
                            add_group(g)
                        if not last:
                            hold(made, g0 + n + R)
                            take_tile(t + 1)
                        for q in range(2):
                            if not last:
                                scale_shift_rows(g0 + n + q)
                            add_group(g0 + n - 2 + q)
                        c(dve.tensor_copy(agg[:, ds(t * P, P)], zacc[:, :]))
                        c.reset()

                    with dve.Fori(0, T - 1) as t:
                        tile(t, False)
                    tile(T - 1, True)

        @block.tensor
        def _(pe):
            hold = Hold(pe, pt)
            with when(pe):
                n = pe.value_load(k.total[0:1, 0:1], min_val=1, max_val=GMAX)
                with pe.Fori(0, n) as g:
                    hold(relued, g + 1 + R)
                    hold(posted, g + 1)
                    pe.matmul(slot(e1, g), fc[:, :], slot(r4, g), start=True, stop=True).then_inc(product, 1)

        @block.scalar
        def _(act):
            hold = Hold(act, at_)
            with when(act):
                act.wait_ge(zero, 1)
                n = act.value_load(k.total[0:1, 0:1], min_val=2, max_val=GMAX)

                def first(g):
                    hold(made, g + 1 + R)
                    gg = g if isinstance(g, int) else g.with_bounds(min_val=0, max_val=CAP - 1)
                    more = {"accum_out": part[:, 0, ds(gg, 1)]} if agg is None else {}
                    act.activation(slot(r4, g), slot(pre, g), ACT.Relu, **more).then_inc(relued, 1)

                def second(g):
                    hold(product, g + 1)
                    hold(zused, g + 1)
                    gg = g.with_bounds(min_val=0, max_val=CAP - 1)
                    if agg is None:
                        act.activation(slot(z, g), slot(e1, g), ACT.Square,
                                       accum_out=part[:, 1, ds(gg, 1)]).then_inc(posted, 1)
                        act.sem_inc(zused, 1)
                    else:
                        act.activation(slot(z, g), slot(e1, g), ACT.Relu, bias=coef[:, 3:4],
                                       scale=coef[:, 2:3]).then_inc(posted, 1)

                first(0)
                with act.Fori(1, n) as g:
                    first(g)
                    second(g - 1)
                second(n - 1)


def edge_regather(k, table, slot_src, at, fc, coef, sums, agg):
    nc = k.nc
    with ExitStack() as st:
        s = k.sub(st)
        ga = Gather(k, s, table, D, slot_src)
        stage = s.sb("mstage", [P, J, D])
        att, pre, r, z = s.sb("att", [P, D]), s.sb("pre", [P, J, D]), s.sb("r", [P, J, D]), s.sb("z", [P, J, D])
        part, total = s.sb("part", [P, 2]), s.sb("tot2", [P, 2])
        zsum, zacc = s.sb("zsum", [P, D]), s.sb("zacc", [P, D])
        bt, e1 = s.ps("bt", [P, 512]), s.ps("e1", [P, 512])
        staged, turned, pre_ready, r_ready, e1_ready, z_ready, e1_free, turns, ch, ach = (
            k.sem(n) for n in ("staged", "turned", "pre_ready", "r_ready", "e1_ready", "z_ready", "e1_free",
                               "turns", "ch", "ach"))
        block = st.enter_context(k.block())

        def program(eng_name):
            def wrap(f):
                def g(eng):
                    with eng.If(rounds(k, eng) > CAP // R):
                        f(eng)
                eng_name(g)
            return wrap

        program(block.gpsimd)(ga.pool)
        program(block.sync)(ga.sync)

        @program(block.vector)
        def _(dve):
            c = Chain(dve, ch)
            hold = Hold(dve, turns)
            dve.sem_inc(ga.used, R)
            c(dve.memset(total[:, :], 0.0))
            c.reset()
            bounds = tiles_loop(k, dve)
            with dve.Fori(0, T) as t:
                g0, n = bounds(t)
                c(dve.tensor_copy(att[:, :], at[:, ds(t * P, P)]))
                if agg is not None:
                    c(dve.memset(zacc[:, :], 0.0))
                c.reset()
                with dve.Fori(g0, g0 + n) as g:
                    hold(ga.landed, g + 1)
                    c(dve.tensor_copy(stage[:, :, :], ga.group(g)))
                    dve.sem_inc(ga.used, 1)
                    dve.sem_inc(staged, 1)
                    take(dve, turned)
                    c(dve.scalar_tensor_tensor(pre[:, :, :], bt[:, :].rearrange("p (j c) -> p j c", j=J),
                                               coef[:, 0:1], att[:, :].unsqueeze(1).broadcast_to([P, J, D]),
                                               ALU.mult, ALU.add))
                    dve.sem_inc(pre_ready, 1)
                    take(dve, z_ready)
                    if agg is None:
                        c(dve.tensor_tensor(total[:, :], total[:, :], part[:, :], ALU.add))
                    else:
                        c(dve.tensor_reduce(zsum[:, :], z[:, :, :].rearrange("p j c -> p c j"), AX.X, ALU.add))
                        c(dve.tensor_tensor(zacc[:, :], zacc[:, :], zsum[:, :], ALU.add))
                    c.reset()
                if agg is not None:
                    c(dve.tensor_copy(agg[:, ds(t * P, P)], zacc[:, :]))
                    c.reset()
            if agg is None:
                c(dve.tensor_copy(sums[:, 0:2], total[:, :]))

        @program(block.tensor)
        def _(pe):
            n = pe.value_load(k.total[0:1, 0:1], min_val=1, max_val=GMAX)
            with pe.Fori(0, n):
                take(pe, staged)
                for j in range(J):
                    mm = pe.transpose(bt[:, j * P:(j + 1) * P], stage[:, j, :], k.ident[:, :])
                mm.then_inc(turned, 1)
                take(pe, r_ready)
                pe.matmul(e1[:, :], fc[:, :], r[:, :, :].rearrange("p j c -> p (j c)"), start=True,
                          stop=True).then_inc(e1_ready, 1)

        @program(block.scalar)
        def _(act):
            n = act.value_load(k.total[0:1, 0:1], min_val=1, max_val=GMAX)
            with act.Fori(0, n):
                take(act, pre_ready)
                rf, pf, zf = (a[:, :, :].rearrange("p j c -> p (j c)") for a in (r, pre, z))
                if agg is None:
                    act.activation(rf, pf, ACT.Relu, accum_out=part[:, 0:1]).then_inc(r_ready, 1)
                    take(act, e1_ready)
                    act.activation(zf, e1[:, :], ACT.Square, accum_out=part[:, 1:2]).then_inc(z_ready, 1)
                else:
                    act.activation(rf, pf, ACT.Relu).then_inc(r_ready, 1)
                    take(act, e1_ready)
                    act.activation(zf, e1[:, :], ACT.Relu, bias=coef[:, 3:4], scale=coef[:, 2:3]).then_inc(z_ready, 1)


def edge_dummy(k, at, fc, coef, sums, empr, vec, spare, final):
    nc = k.nc
    with ExitStack() as st:
        s = k.sub(st)
        e1 = s.sb("e1a", [P, NP])
        r = spare

        with ExitStack() as st1:
            ch = k.sem("edch")
            block = st1.enter_context(k.block())

            @block.vector
            def _(dve):
                c = Chain(dve, ch)
                c(dve.tensor_scalar(r[:, :], at[:, :], 0.0, None, ALU.max))

        def store(dve, c, ps, i, o):
            c(dve.tensor_copy(e1[:, ds(i * BLK, BLK)], ps))

        dense_cols(k, [r], [[fc[:, :]]], store)
        with ExitStack() as st1:
            ch = k.sem("edch2")
            mm_r, mm_d = k.sem("edr"), k.sem("edd")
            ps = k.sub(st1).ps("fcr", [P, 512])
            block = st1.enter_context(k.block())

            @block.vector
            def _(dve):
                c = Chain(dve, ch)
                if final:
                    c(dve.tensor_scalar(e1[:, :], e1[:, :], coef[:, 2:3], coef[:, 3:4], ALU.mult, ALU.add))
                    c(dve.scalar_tensor_tensor(spare[:, :], e1[:, :], 0.0, empr[:, :], ALU.max, ALU.mult))
                else:
                    c(dve.tensor_tensor(r[:, :], r[:, :], empr[:, :], ALU.mult))
                    c(dve.tensor_reduce(sums[:, 2:3], r[:, :], AX.X, ALU.add))
                    c(dve.tensor_tensor(sums[:, 0:1], sums[:, 0:1], sums[:, 2:3], ALU.subtract))
                    dve.sem_inc(mm_r, 1)
                    c(dve.tensor_tensor(r[:, :], e1[:, :], empr[:, :], ALU.mult))
                    c(dve.tensor_tensor(r[:, :], r[:, :], e1[:, :], ALU.mult))
                    c(dve.tensor_reduce(sums[:, 3:4], r[:, :], AX.X, ALU.add))
                    c(dve.tensor_tensor(sums[:, 5:6], sums[:, 1:2], sums[:, 3:4], ALU.subtract))
                    dve.wait_ge(mm_d, 1)
                    c(dve.tensor_copy(sums[:, 4:5], ps[:, 0:1]))

            @block.tensor
            def _(pe):
                if not final:
                    pe.wait_ge(mm_r, 1)
                    pe.matmul(ps[:, 0:1], fc[:, :], sums[:, 0:1], start=True, stop=True).then_inc(mm_d, 1)
        if not final:
            finish_bn(k, sums, 4, 5, vec[:, 2:3], vec[:, 3:4], coef[:, 2:3], coef[:, 3:4])


def build(nc, a, out):
    def dram(name, shape, dt=F32):
        return nc.dram_tensor(name, shape, dt, kind="Internal").ap()

    with ExitStack() as whole:
        k = Kit(nc)
        m = k.sub(whole)
        k.ident, k.ones, k.before = (m.sb(n, [P, P]) for n in ("ident", "ones", "before"))
        k.ramp = m.sb("ramp", [P, P])
        k.pos, k.posf = m.sb("pos", [P, T], I32), m.sb("posf", [P, T])
        k.deg, k.empty = m.sb("deg", [P, T]), m.sb("empty", [P, T])
        k.node, k.nodec, k.row0, k.shift = (m.sb(n, [P, T], I32) for n in ("node", "nodec", "row0", "shift"))
        k.groups, k.group0, k.chunks, k.chunk0 = (m.sb(n, [P, T], I32) for n in (
            "groups", "group0", "chunks", "chunk0"))
        k.bgroups, k.bgroup0 = m.sb("bgroups", [P, NB], I32), m.sb("bgroup0", [P, NB], I32)
        k.total = m.sb("total", [P, 2], I32)
        k.out = m.sb("layer_out", [P, T, D])
        xs = m.sb("x_state", [P, T, D])
        x = xs[:, :, :]

        dense = dram("dense_weights", (NP * PITCH, 1))
        slot_src, slot_weight = dram("slot_src", (GMAX, P, J), I32), dram("slot_weight", (GMAX, P, J), I32)
        keys, info = dram("keys", (NP,)), dram("info", (NP, 4), I32)
        gat_table = dram("gat_table", (NP + 1, 136))
        kv_table = dram("kv_table", (NP + 1, 272))
        b_table = dram("b_table", (NP + 1, D))
        by_node = dram("by_node", (NP, D))
        kept = dram("kept", (CAP + R, P, J * P))
        empty_row, cnt_row = dram("empty_row", (NP,)), dram("cnt_row", (NP,))

        make_constants(k)
        order_nodes(k, a["dst"], keys, info, dense)
        build_slots(k, a["src"], a["edge_weight"], slot_src, slot_weight)
        gather_rows(k, a["x"], x, k.nodec)
        gat_conv(k, x, a["L0_gnn_W1"], a["L0_gnn_a1_src"], a["L0_gnn_a1_dst"], a["L0_gnn_b1"], gat_table,
                 slot_src, True)
        gat_conv(k, k.out[:, :, :], a["L0_gnn_W2"], a["L0_gnn_a2_src"], a["L0_gnn_a2_dst"], a["L0_gnn_b2"],
                 gat_table, slot_src, False)
        add_rows(k, k.out[:, :, :], k.out[:, :, :], x)
        layernorm(k, k.out[:, :, :], x, 1e-5)
        residual_layer(k, x, a["L1_gnn_W_self"], a["L1_gnn_b_self"], a["L1_gnn_W_neigh"], a["L1_gnn_b_neigh"],
                       a["L1_gnn_scale"], a["L1_gnn_offset"], dense, slot_src, slot_weight, by_node)
        attention_layer(k, x, {n[7:]: v for n, v in a.items() if n.startswith("L2_gnn_")}, kv_table, slot_src)
        edge_mlp_layer(k, x, {n[7:]: v for n, v in a.items() if n.startswith("L3_gnn_")}, b_table, slot_src,
                       kept, empty_row, cnt_row, out)


TRANSPOSED = ("L1_gnn_W_self", "L1_gnn_W_neigh", "L2_gnn_q_w", "L2_gnn_k_w", "L2_gnn_v_w", "L2_gnn_out_w",
              "L2_gnn_lin1_w", "L2_gnn_lin2_w", "L3_gnn_theta_w", "L3_gnn_phi_w", "L3_gnn_fc1_w")
COLUMNS = ("L2_gnn_out_b", "L2_gnn_g1", "L2_gnn_b1", "L2_gnn_lin2_b", "L2_gnn_g2", "L2_gnn_b2",
           "L3_gnn_bn0_g", "L3_gnn_bn0_b", "L3_gnn_bn1_g", "L3_gnn_bn1_b")


def kernel(**inputs):
    import numpy as _np
    import concourse.bacc as _bacc
    from concourse import mybir as _mybir
    from concourse.bass_utils import run_bass_kernel_spmd as _run

    nc = _bacc.Bacc("TRN2", target_bir_lowering=False, num_devices=1)
    arrays, args = {}, {}
    for name, value in inputs.items():
        v = _np.asarray(value)
        if name == "dst":
            v = _np.concatenate([v, _np.full(P * ECOLS - E, NP, v.dtype)]).reshape(P, ECOLS)
        elif name in ("src", "edge_weight"):
            v = _np.concatenate([v, _np.zeros(EROWS * CH - E, v.dtype)]).reshape(EROWS, CH)
            if name == "edge_weight":
                v = v.view(_np.int32)
        elif name in TRANSPOSED:
            v = v.T
        elif name in COLUMNS:
            v = v.reshape(-1, 1)
        elif name == "L2_gnn_lin1_b":
            v = v.reshape(-1, P).T
        v = _np.ascontiguousarray(v)
        arrays[f"in_{name}_dram"] = v
        args[name] = nc.dram_tensor(f"in_{name}_dram", v.shape, _mybir.dt.from_np(v.dtype),
                                    kind="ExternalInput").ap()
    out = nc.dram_tensor("out_0_dram", (N, D), _mybir.dt.float32, kind="ExternalOutput").ap()
    build(nc, args, out)
    r = _run(nc, [arrays], core_ids=[0])
    return r.results[0]["out_0_dram"]
```

```python
from contextlib import ExitStack, contextmanager

import concourse.bass as bass
from concourse import mybir

F32 = mybir.dt.float32
BF16 = mybir.dt.bfloat16
I32 = mybir.dt.int32
ALU = mybir.AluOpType
ACT = mybir.ActivationFunctionType
AX = mybir.AxisListType
RMAX = bass.bass_isa.ReduceOp.max
ds = bass.ds

P = 128
N = 6250
E = 206250
T = -(-N // P)
NP = T * P
LAST = N - (T - 1) * P
DUMMY = NP
D = 128
B7 = 7
NB = T // B7
W7 = B7 * P
J = 4
R = 4
CH = 64
GC = CH // J
EROWS = -(-E // CH) + 3
HK = 16
HSTEPS = 2 * (-(-E // (P * HK * 2)))
ECOLS = HSTEPS * HK
GMAX = E // J + 3 * T + T * GC + 2 * GC
CAP = 512
PITCH = 8192
FILL = NP + P
BIG = 1e30
BLK = 448
NBLK = NP // BLK


class Memory:

    def __init__(self, kit, stage):
        self.kit, self.stage = kit, stage

    def sb(self, s, shape, dt=F32):
        return self.stage.enter_context(self.kit.nc.sbuf_tensor(self.kit.name(s), shape, dt))

    def ps(self, s, shape, dt=F32):
        return self.stage.enter_context(self.kit.nc.psum_tensor(self.kit.name(s), shape, dt))


class Kit:

    def __init__(self, nc):
        self.nc, self.count, self.live = nc, 0, []

    def sub(self, stage):
        return Memory(self, stage)

    def name(self, s):
        self.count += 1
        return f"{s}_{self.count}"

    def sem(self, s):
        self.live.append(self.nc.alloc_semaphore(name=self.name(s)))
        return self.live[-1]

    @contextmanager
    def block(self):
        with self.nc.Block() as b:
            yield b
        self.nc.clear_and_free_semaphores(self.live)
        self.live.clear()
        self.nc.all_engine_barrier()


def take(eng, sem, n=1):
    eng.wait_ge(sem, n)
    eng.sem_clear(sem)


class Hold:

    def __init__(self, eng, turns):
        self.eng, self.turns = eng, turns

    def __call__(self, sem, count):
        self.eng.wait_ge(sem, count)
        self.eng.sem_inc(self.turns, 1)


class Chain:

    def __init__(self, eng, sem):
        self.eng, self.sem, self.n = eng, sem, 0

    def __call__(self, ins):
        self.n += 1
        ins.then_inc(self.sem, 1)
        self.eng.wait_ge(self.sem, self.n)

    def go(self, ins):
        self.n += 1
        ins.then_inc(self.sem, 1)
        return self.n

    def until(self, n):
        self.eng.wait_ge(self.sem, n)

    def reset(self):
        if self.n:
            self.eng.sem_clear(self.sem)
        self.n = 0


def rows(ap1d, parts=P):
    return ap1d.partition_broadcast(parts)


def flat2(ap):
    return ap.rearrange("p t c -> p (t c)")


def split(total, step):
    return [(i, min(step, total - i)) for i in range(0, total, step)]


def make_constants(k):
    with ExitStack() as st:
        id0 = k.sem("id0")
        block = st.enter_context(k.block())

        @block.vector
        def _(dve):
            dve.memset(k.ones[:, :], 1.0)

        @block.gpsimd
        def _(pool):
            pool.memset(k.ident[:, :], 0.0).then_inc(id0, 1)
            pool.memset(k.before[:, :], 0.0).then_inc(id0, 1)
            pool.wait_ge(id0, 2)
            pool.affine_select(out=k.ident[:, :], in_=k.ident[:, :], compare_op=ALU.not_equal, fill=1.0,
                               base=0, pattern=[[-1, P]], channel_multiplier=1)
            pool.affine_select(out=k.before[:, :], in_=k.before[:, :], compare_op=ALU.is_ge, fill=1.0,
                               base=0, pattern=[[-1, P]], channel_multiplier=1)
            pool.iota(k.ramp[:, :], [[1, P]], base=0, channel_multiplier=0,
                      allow_small_or_imprecise_dtypes=True)
            pool.iota(k.pos[:, :], [[P, T]], base=0, channel_multiplier=1)
            pool.iota(k.posf[:, :], [[P, T]], base=0, channel_multiplier=1,
                      allow_small_or_imprecise_dtypes=True)


def order_nodes(k, dst_cols, keys_dram, info_dram, dense):
    with ExitStack() as st:
        s = k.sub(st)
        dst = s.sb("dst", [P, ECOLS], I32)
        zero = s.sb("zero", [P, FILL])
        zeroed, cleared, ach, keys_ready, signs_ready = (k.sem(x) for x in (
            "zeroed", "cleared", "ordach", "keys_ready", "signs_ready"))
        low_i = s.sb("low_i", [P, ECOLS], I32)
        low, high = s.sb("low", [P, ECOLS], BF16), s.sb("high", [P, ECOLS], BF16)
        ramp = s.sb("rampb", [P, P], BF16)
        hot_low = s.sb("hot_low", [P, 2, HK, P], BF16)
        hot_high = s.sb("hot_high", [P, 2, HK, T], BF16)
        deg = s.sb("deg_n", [P, T])
        tot = s.sb("tot", [P, T])
        key, keyrow = s.sb("key", [P, T]), s.sb("keyrow", [P, NP])
        junk, junk_a = s.sb("junk", [P, NP], BF16), s.sb("junk_a", [P, NP], BF16)
        TV = T // 2 + 1
        below, signs = s.sb("below", [P, T]), s.sb("signs", [P, T - TV])
        rank, ranki = s.sb("rank", [P, T]), s.sb("ranki", [P, T], I32)
        tmp = s.sb("tmp", [P, T])
        info = s.sb("info", [P, T, 4], I32)
        infop = s.sb("infop", [P, T, 4], I32)
        md = s.sb("md", [P, T])
        ti = s.sb("ti", [P, T], I32)
        hist, pre, tots = s.ps("hist", [P, T]), s.ps("pre", [P, T]), s.ps("tots", [P, T])
        loaded, hot, free = k.sem("dst_loaded"), [k.sem("hot0"), k.sem("hot1")], [k.sem("hf0"), k.sem("hf1")]
        chain_s, key_out, key_in, key_ready = (k.sem(x) for x in ("ordchain", "key_out", "key_in", "key_ready"))
        deg_ready, pre_ready, info_ready, info_out, info_in = (k.sem(x) for x in (
            "deg_ready", "pre_ready", "info_ready", "info_out", "info_in"))
        infos_out, deg_pos, md_ready, z_ready, z_done = (k.sem(x) for x in (
            "infos_out", "deg_pos", "md_ready", "z_ready", "z_done"))
        block = st.enter_context(k.block())

        @block.scalar
        def _(act):
            act.wait_ge(zeroed, 1)
            view = dense.rearrange("(t p c) o -> t p (c o)", p=P, c=PITCH)
            with act.Fori(0, T) as t:
                act.dma_start(view[ds(t, 1), :, 0:FILL].rearrange("t p c -> (t p) c"),
                              zero[:, :]).then_inc(cleared, 16)
            c = Chain(act, ach)
            act.wait_ge(keys_ready, 1)
            with act.Fori(0, T - TV) as t:
                c(act.activation(junk_a[:, :], keyrow[:, :], ACT.Sign, bias=below[:, ds(t, 1)],
                                 accum_out=signs[:, ds(t, 1)]))
                c.reset()
            act.sem_inc(signs_ready, 1)
            act.wait_ge(cleared, 16 * T)

        @block.sync
        def _(sp):
            sp.dma_start(dst[:, :], dst_cols).then_inc(loaded, 16)
            sp.wait_ge(key_ready, 1)
            sp.dma_start(keys_dram.rearrange("(p t) -> p t", p=P), key[:, :]).then_inc(key_out, 16)
            sp.wait_ge(key_out, 16)
            sp.dma_start(keyrow[:, :], rows(keys_dram)).then_inc(key_in, 16)
            sp.wait_ge(infos_out, 1)
            sp.dma_start(infop[:, :, :], info_dram.rearrange("(t p) k -> p t k", p=P)).then_inc(info_in, 16)

        @block.tensor
        def _(pe):
            pe.wait_ge(z_ready, 1)
            pe.matmul(hist[:, :], hot_low[:, 0, 0, :], hot_high[:, 0, 0, :], start=True, stop=False,
                      skip_group_check=True).then_inc(z_done, 1)
            with pe.Fori(0, HSTEPS // 2):
                for u in range(2):
                    take(pe, hot[u])
                    for c in range(HK):
                        mm = pe.matmul(hist[:, :], hot_low[:, u, c, :], hot_high[:, u, c, :], start=False,
                                       stop=False, skip_group_check=True)
                    mm.then_inc(free[u], 1)
            pe.wait_ge(deg_ready, 1)
            pe.matmul(pre[:, :], k.before[:, :], deg[:, :], start=True, stop=True)
            pe.matmul(tots[:, :], k.ones[:, :], deg[:, :], start=True, stop=True).then_inc(pre_ready, 1)

        @block.gpsimd
        def _(pool):
            pool.wait_ge(info_ready, 1)
            for t in range(T):
                pool.indirect_dma_start(info_dram, bass.IndirectOffsetOnAxis(ranki[:, t:t + 1], 0),
                                        info[:, t, :], None).then_inc(info_out, 16)
            pool.wait_ge(info_out, 16 * T)
            pool.sem_inc(infos_out, 1)
            pool.wait_ge(deg_pos, 1)
            pool.partition_all_reduce(md[:, :], k.deg[:, :], P, RMAX).then_inc(md_ready, 1)

        @block.vector
        def _(dve):
            c = Chain(dve, chain_s)
            dve.memset(zero[:, :], 0.0).then_inc(zeroed, 1)
            c(dve.memset(hot_low[:, 0, 0, :], 0.0))
            c(dve.memset(hot_high[:, 0, 0, :], 0.0))
            dve.sem_inc(z_ready, 1)
            c(dve.tensor_copy(ramp[:, :], k.ramp[:, :]))
            dve.wait_ge(loaded, 16)
            c(dve.tensor_single_scalar(low_i[:, :], dst[:, :], P - 1, ALU.bitwise_and))
            c(dve.tensor_copy(low[:, :], low_i[:, :]))
            c(dve.tensor_single_scalar(low_i[:, :], dst[:, :], 7, ALU.arith_shift_right))
            c(dve.tensor_copy(high[:, :], low_i[:, :]))
            c.reset()
            dve.wait_ge(z_done, 1)
            for u in range(2):
                dve.sem_inc(free[u], 1)
            with dve.Fori(0, HSTEPS // 2) as i:
                for u in range(2):
                    take(dve, free[u])
                    lo = low[:, ds((2 * i + u) * HK, HK)].unsqueeze(2).broadcast_to([P, HK, P])
                    hi = high[:, ds((2 * i + u) * HK, HK)].unsqueeze(2).broadcast_to([P, HK, T])
                    c(dve.tensor_tensor(hot_low[:, u], lo, ramp[:, :].unsqueeze(1).broadcast_to([P, HK, P]),
                                        ALU.is_equal))
                    c(dve.tensor_tensor(hot_high[:, u], hi, ramp[:, 0:T].unsqueeze(1).broadcast_to([P, HK, T]),
                                        ALU.is_equal))
                    dve.sem_inc(hot[u], 1)
                c.reset()
            for u in range(2):
                dve.wait_ge(free[u], 1)
            c(dve.tensor_copy(deg[:, :], hist[:, :]))
            dve.sem_inc(deg_ready, 1)
            dve.wait_ge(pre_ready, 1)
            c(dve.tensor_copy(tot[:, :], tots[:, :]))
            c(dve.tensor_tensor_scan(tmp[:, :], k.ones[:, 0:T], tot[:, :], 0.0, ALU.mult, ALU.add))
            c(dve.tensor_tensor(tmp[:, :], tmp[:, :], tot[:, :], ALU.subtract))
            c(dve.tensor_tensor(tmp[:, :], tmp[:, :], pre[:, :], ALU.add))
            c(dve.memset(info[:, :, :], 0))
            c(dve.tensor_copy(info[:, :, 0], tmp[:, :]))
            c(dve.tensor_copy(info[:, :, 1], deg[:, :]))
            c(dve.tensor_copy(info[:, :, 2], k.pos[:, :]))
            c(dve.tensor_scalar(key[:, :], deg[:, :], 1023.0, 8192.0, ALU.min, ALU.mult))
            c(dve.tensor_tensor(key[:, :], key[:, :], k.posf[:, :], ALU.add))
            c(dve.tensor_scalar(tmp[:, :], k.posf[:, :], float(N), -16384.0, ALU.is_ge, ALU.mult))
            c(dve.tensor_tensor(key[:, :], key[:, :], tmp[:, :], ALU.add))
            dve.sem_inc(key_ready, 1)
            c(dve.tensor_scalar(below[:, :], key[:, :], -1.0, None, ALU.mult))
            dve.wait_ge(key_in, 16)
            dve.sem_inc(keys_ready, 1)
            c.reset()
            with dve.Fori(T - TV, T) as t:
                c(dve.tensor_scalar(junk[:, :], keyrow[:, :], key[:, ds(t, 1)], 0.0, ALU.is_gt, ALU.add,
                                    accum_out=rank[:, ds(t, 1)]))
                c.reset()
            dve.wait_ge(signs_ready, 1)
            c(dve.tensor_scalar(rank[:, 0:T - TV], signs[:, :], float(NP - 1), 0.5, ALU.add, ALU.mult))
            c(dve.tensor_copy(ranki[:, :], rank[:, :]))
            dve.sem_inc(info_ready, 1)
            dve.wait_ge(info_in, 16)
            c(dve.tensor_copy(k.deg[:, :], infop[:, :, 1]))
            dve.sem_inc(deg_pos, 1)
            c(dve.tensor_copy(k.node[:, :], infop[:, :, 2]))
            c(dve.tensor_copy(tmp[:, :], infop[:, :, 2]))
            c(dve.tensor_scalar(k.nodec[:, :], tmp[:, :], float(N - 1), None, ALU.min))
            c(dve.tensor_single_scalar(k.row0[:, :], infop[:, :, 0], 6, ALU.arith_shift_right))
            c(dve.tensor_single_scalar(k.shift[:, :], infop[:, :, 0], CH - 1, ALU.bitwise_and))
            dve.wait_ge(md_ready, 1)
            for unit, count, first in ((J, k.groups, k.group0), (CH, k.chunks, k.chunk0)):
                c(dve.tensor_scalar(ti[:, :], md[:, :], float(unit - 1), None, ALU.add))
                c(dve.tensor_single_scalar(ti[:, :], ti[:, :], {J: 2, CH: 6}[unit], ALU.arith_shift_right))
                c(dve.tensor_scalar(tot[:, :], ti[:, :], 3.0 if unit == J else 1.0, None, ALU.max))
                c(dve.tensor_copy(count[:, :], tot[:, :]))
                c(dve.tensor_tensor_scan(tmp[:, :], k.ones[:, 0:T], tot[:, :], 0.0, ALU.mult, ALU.add))
                if unit == J:
                    c(dve.tensor_copy(k.total[:, 2:3], tmp[:, T - 1:T]))
                    c(dve.tensor_scalar(ti[:, 0:1], tmp[:, T - 1:T], float(R - 1), None, ALU.add))
                    c(dve.tensor_single_scalar(k.total[:, 1:2], ti[:, 0:1], 2, ALU.arith_shift_right))
                    c(dve.tensor_single_scalar(k.total[:, 0:1], k.total[:, 1:2], 2, ALU.arith_shift_left))
                    c(dve.tensor_scalar(k.total[:, 4:5], k.total[:, 1:2], -1.0, None, ALU.add))
                    c(dve.tensor_reduce(rank[:, 0:NB],
                                        tot[:, :].rearrange("p (b u) -> p b u", u=B7), AX.X, ALU.max))
                    c(dve.tensor_copy(k.bgroups[:, :], rank[:, 0:NB]))
                    c(dve.tensor_tensor_scan(key[:, 0:NB], k.ones[:, 0:NB], rank[:, 0:NB], 0.0, ALU.mult, ALU.add))
                    c(dve.tensor_scalar(ti[:, 0:1], key[:, NB - 1:NB], -1.0, None, ALU.add))
                    c(dve.tensor_single_scalar(k.total[:, 3:4], ti[:, 0:1], 1, ALU.arith_shift_right))
                    c(dve.tensor_tensor(key[:, 0:NB], key[:, 0:NB], rank[:, 0:NB], ALU.subtract))
                    c(dve.tensor_copy(k.bgroup0[:, :], key[:, 0:NB]))
                c(dve.tensor_tensor(tmp[:, :], tmp[:, :], tot[:, :], ALU.subtract))
                c(dve.tensor_copy(first[:, :], tmp[:, :]))
                if unit == J:
                    c(dve.tensor_copy(rank[:, 0:1], k.total[:, 0:1]))
                    c(dve.tensor_tensor(tot[:, T - 1:T], rank[:, 0:1], tmp[:, T - 1:T], ALU.subtract))
                    c(dve.tensor_copy(count[:, T - 1:T], tot[:, T - 1:T]))
                    c(dve.tensor_scalar(k.empty[:, :], tot[:, :], float(J), None, ALU.mult))
                    c(dve.tensor_tensor(k.empty[:, :], k.empty[:, :], k.deg[:, :], ALU.subtract))


def build_slots(k, edge_rows, slot_src, slot_weight):
    with ExitStack() as st:
        s = k.sub(st)
        rid = s.sb("rid", [P, 1], I32)
        room, cur = s.sb("room", [P, T]), s.sb("cur", [P, 1])
        top, less = s.sb("top", [P, 1]), s.sb("less", [P, 1])
        raw = s.sb("raw", [P, 2, 2 * CH], I32)
        work = s.sb("work", [P, 2, 3 * CH // 2], I32)
        tmp = s.sb("tmp", [P, 2, 2 * CH], I32)
        mask = s.sb("mask", [P, T, 6, 2], I32)
        bit = s.sb("bit", [P, T], I32)
        mrow = s.sb("mrow", [P, 6, 2], I32)
        left = s.sb("left", [P, 1])
        valid = s.sb("valid", [P, CH])
        outs = s.sb("outs", [P, CH], I32)
        outw = s.sb("outw", [P, CH], I32)
        blank = s.sb("blank", [P, CH], I32)
        chain_s, rid_ready, rid_free, raw_free, room_ready, rows_in, out_ready, written, w_sem, turns, turns2, \
            turns3, ach, last = (k.sem(x) for x in (
                "slchain", "rid_ready", "rid_free", "raw_free", "room_ready", "rows_in", "out_ready", "written",
                "w_sem", "slt", "slt2", "slt3", "slach", "last"))
        block = st.enter_context(k.block())

        def table(tab, g):
            return tab[ds(g, GC), :, :].rearrange("g p j -> p g j")

        def tile(x):
            return x[:, :].rearrange("p (g j) -> p g j", j=J)

        @block.gpsimd
        def _(pool):
            with pool.Fori(0, T) as t:
                n = pool.value_load(k.chunks[0:1, ds(t, 1)], min_val=1, max_val=EROWS)
                with pool.Fori(0, n):
                    take(pool, rid_ready)
                    take(pool, raw_free)
                    pool.indirect_dma_start(raw[:, :, :].rearrange("p k c -> p (k c)"), None, edge_rows,
                                            bass.IndirectOffsetOnAxis(rid[:, 0:1], 0)).then_inc(rows_in, 16)

        @block.vector
        def _(dve):
            c = Chain(dve, chain_s)
            hold = Hold(dve, turns)
            c(dve.memset(blank[:, :], DUMMY))
            for b in range(6):
                c(dve.tensor_single_scalar(bit[:, :], k.shift[:, :], 5 - b, ALU.arith_shift_right))
                c(dve.tensor_single_scalar(bit[:, :], bit[:, :], 1, ALU.bitwise_and))
                c(dve.tensor_scalar(mask[:, :, b, 0], bit[:, :], -1.0, None, ALU.mult))
                c(dve.tensor_scalar(mask[:, :, b, 1], bit[:, :], -1.0, None, ALU.add))
            c.reset()
            c(dve.tensor_copy(room[:, :], k.row0[:, :]))
            c(dve.tensor_scalar(room[:, :], room[:, :], -1.0, float(EROWS - 1), ALU.mult, ALU.add))
            c(dve.memset(top[:, :], float(EROWS - 1)))
            c(dve.memset(less[:, :], -1.0))
            c.reset()
            for sem in (room_ready, raw_free, rid_free, written):
                dve.sem_inc(sem, 1)
            with dve.Fori(0, T) as t:
                n = dve.value_load(k.chunks[0:1, ds(t, 1)], min_val=1, max_val=EROWS)
                c0 = dve.value_load(k.chunk0[0:1, ds(t, 1)], min_val=0, max_val=EROWS)
                c(dve.tensor_copy(left[:, :], k.deg[:, ds(t, 1)]))
                c(dve.tensor_copy(mrow[:, :, :], mask[:, ds(t, 1)].rearrange("p t b m -> p (t b) m")))
                c.reset()
                with dve.Fori(c0, c0 + n) as g:
                    hold(rows_in, 16 * (g + 1))
                    dve.sem_inc(rid_free, 1)
                    inside = c.go(dve.tensor_scalar(valid[:, :], k.ramp[:, 0:CH], left[:, 0:1], None, ALU.is_lt))
                    moved = [0, 0]
                    for b in range(6):
                        step = 32 >> b
                        wide = {32: 96, 16: 80, 8: 72, 4: 68, 2: 66, 1: 65}[step]
                        src = work if b else raw
                        stay = []
                        for x in range(2):
                            if b:
                                c.until(moved[x])
                            stay.append(c.go(dve.tensor_single_scalar(
                                tmp[:, x, 0:wide], src[:, x, 0:wide], mrow[:, b, 1:2], ALU.bitwise_and)))
                        for x in range(2):
                            c.until(stay[x])
                            moved[x] = c.go(dve.scalar_tensor_tensor(
                                work[:, x, 0:wide], src[:, x, step:step + wide], mrow[:, b, 0:1],
                                tmp[:, x, 0:wide], ALU.bitwise_and, ALU.bitwise_or))
                        if b == 0:
                            c.until(inside)
                            c.go(dve.tensor_scalar(left[:, :], left[:, :], float(-CH), None, ALU.add))
                            c.until(moved[1])
                            dve.sem_inc(raw_free, 1)
                    take(dve, written)
                    c.until(moved[1])
                    c.go(dve.tensor_copy(outw[:, :], work[:, 1, 0:CH]))
                    c(dve.scalar_tensor_tensor(valid[:, :], work[:, 0, 0:CH], float(-DUMMY), valid[:, :],
                                               ALU.add, ALU.mult))
                    c(dve.tensor_scalar(outs[:, :], valid[:, :], float(DUMMY), None, ALU.add))
                    c.reset()
                    dve.sem_inc(out_ready, 1)

        @block.scalar
        def _(act):
            c = Chain(act, ach)
            hold = Hold(act, turns3)
            act.wait_ge(room_ready, 1)
            with act.Fori(0, T) as t:
                n = act.value_load(k.chunks[0:1, ds(t, 1)], min_val=1, max_val=EROWS)
                c0 = act.value_load(k.chunk0[0:1, ds(t, 1)], min_val=0, max_val=EROWS)
                c(act.activation(cur[:, :], room[:, ds(t, 1)], ACT.Relu))
                c.reset()
                with act.Fori(c0, c0 + n) as g:
                    hold(rid_free, g + 1)
                    c(act.activation(rid[:, :], cur[:, :], ACT.Relu, bias=top[:, 0:1], scale=-1.0))
                    act.sem_inc(rid_ready, 1)
                    c(act.activation(cur[:, :], cur[:, :], ACT.Relu, bias=less[:, 0:1]))
                    c.reset()

        @block.sync
        def _(sp):
            hold = Hold(sp, turns2)
            with sp.Fori(0, T) as t:
                n = sp.value_load(k.chunks[0:1, ds(t, 1)], min_val=1, max_val=EROWS)
                c0 = sp.value_load(k.chunk0[0:1, ds(t, 1)], min_val=0, max_val=EROWS)
                g0 = sp.value_load(k.group0[0:1, ds(t, 1)], min_val=0, max_val=GMAX - 2 * GC)
                with sp.Fori(c0, c0 + n) as g:
                    at = (g0 + (g - c0) * GC).with_bounds(min_val=0, max_val=GMAX - 2 * GC)
                    take(sp, out_ready)
                    sp.dma_start(table(slot_src, at), tile(outs)).then_inc(w_sem, 16)
                    sp.dma_start(table(slot_weight, at), tile(outw)).then_inc(w_sem, 16)
                    hold(w_sem, 32 * (g + 1))
                    sp.sem_inc(written, 1)
            g = sp.value_load(k.total[0:1, 2:3], min_val=0, max_val=GMAX - 2 * GC)
            sp.dma_start(table(slot_src, g), tile(blank)).then_inc(last, 16)
            sp.dma_start(table(slot_weight, g), tile(blank)).then_inc(last, 16)
            sp.wait_ge(last, 32)


def gather_rows(k, table, dst3, index):
    with ExitStack() as st:
        got = k.sem("got")
        block = st.enter_context(k.block())

        @block.gpsimd
        def _(pool):
            for t in range(T):
                pool.indirect_dma_start(dst3[:, t, :], None, table,
                                        bass.IndirectOffsetOnAxis(index[:, t:t + 1], 0)).then_inc(got, 16)
            pool.wait_ge(got, 16 * T)


def dense_rows(k, src, products, table=None, rows_out=None, width=0, dummy=None):
    with ExitStack() as st:
        s = k.sub(st)
        stage, xt = s.sb("stage", [P, W7]), s.sb("xt", [P, W7])
        tp, acc = s.ps("tp", [P, 2, 512]), s.ps("acc", [P, 2, 3, 512])
        staged, stage_free, turned, xt_ready, xt_free, ch = (k.sem(x) for x in (
            "staged", "stage_free", "turned", "xt_ready", "xt_free", "drchain"))
        mm_done, acc_free = ([k.sem(f"{x}{q}") for q in range(2)] for x in ("mm_done", "acc_free"))
        row = s.sb("dummy", [1, max(width, 1)])
        batch_done, out, ready, dout = (k.sem(x) for x in ("batch_done", "tab_out", "dummy_ready", "dummy_out"))
        block = st.enter_context(k.block())

        @block.vector
        def _(dve):
            c = Chain(dve, ch)

            def bring(b):
                c(dve.tensor_copy(stage[:, :].rearrange("p (u c) -> p u c", u=B7), src[:, ds(b * B7, B7), :]))
                dve.sem_inc(staged, 1)

            def store_batch(b):
                for i, (w, width, store) in enumerate(products):
                    take(dve, mm_done[i % 2])
                    if i == len(products) - 1:
                        dve.sem_inc(xt_free, 1)
                    for u, n in split(B7, 3):
                        store(dve, c, acc[:, i % 2, u // 3, 0:n * width].rearrange("p (u c) -> p u c", u=n),
                              b * B7 + u, n)
                    dve.sem_inc(acc_free[i % 2], 1)
                dve.sem_inc(batch_done, 1)
                c.reset()

            c(dve.memset(row[:, :], 0.0))
            if dummy is not None:
                c(dve.memset(dummy(row), -BIG))
            dve.sem_inc(ready, 1)
            for sem in (xt_free, acc_free[0], acc_free[1]):
                dve.sem_inc(sem, 1)
            bring(0)
            c.reset()
            with dve.Fori(0, NB - 1) as b:
                take(dve, stage_free)
                bring(b + 1)
                store_batch(b)
            store_batch(NB - 1)

        @block.tensor
        def _(pe):
            def turn():
                take(pe, staged)
                for u in range(B7):
                    mm = pe.transpose(tp[:, u // 4, (u % 4) * P:(u % 4 + 1) * P], stage[:, u * P:(u + 1) * P],
                                      k.ident[:, :])
                mm.then_inc(turned, 1)

            def multiply():
                for i, (w, width, store) in enumerate(products):
                    take(pe, acc_free[i % 2])
                    for u in range(B7):
                        mm = pe.matmul(acc[:, i % 2, u // 3, (u % 3) * width:(u % 3 + 1) * width],
                                       xt[:, u * P:(u + 1) * P], w, start=True, stop=True)
                    mm.then_inc(mm_done[i % 2], 1)

            turn()
            with pe.Fori(0, NB - 1):
                take(pe, xt_ready)
                turn()
                multiply()
            take(pe, xt_ready)
            multiply()

        @block.scalar
        def _(act):
            with act.Fori(0, NB):
                take(act, turned)
                act.sem_inc(stage_free, 1)
                take(act, xt_free)
                act.activation(xt[:, 0:512], tp[:, 0, :], ACT.Copy)
                act.activation(xt[:, 512:W7], tp[:, 1, 0:W7 - 512], ACT.Copy).then_inc(xt_ready, 1)

        if table is not None:
            @block.sync
            def _(sp):
                sp.wait_ge(ready, 1)
                sp.dma_start(table[DUMMY:DUMMY + 1, :], row[:, :]).then_inc(dout, 16)
                sp.wait_ge(dout, 16)

            @block.gpsimd
            def _(pool):
                for t in range(T):
                    if t % B7 == 0:
                        pool.wait_ge(batch_done, t // B7 + 1)
                    pool.indirect_dma_start(table, bass.IndirectOffsetOnAxis(k.node[:, t:t + 1], 0),
                                            rows_out[:, t, 0:width], None).then_inc(out, 16)
                pool.wait_ge(out, 16 * T)


def transpose_blocks(k, src, dst):
    with ExitStack() as st:
        s = k.sub(st)
        stage = s.sb("stage", [P, W7])
        tp = s.ps("tp", [P, 2, 512])
        staged, stage_free, turned, tp_free, ch, ach = (k.sem(x) for x in (
            "tstaged", "tstage_free", "tturned", "tp_free", "tchain", "tachain"))
        block = st.enter_context(k.block())

        @block.vector
        def _(dve):
            c = Chain(dve, ch)
            dve.sem_inc(stage_free, 1)
            dve.sem_inc(tp_free, 1)
            with dve.Fori(0, NB) as b:
                take(dve, stage_free)
                c(dve.tensor_copy(stage[:, :], src[:, ds(b * W7, W7)]))
                c.reset()
                dve.sem_inc(staged, 1)

        @block.tensor
        def _(pe):
            with pe.Fori(0, NB):
                take(pe, staged)
                take(pe, tp_free)
                for u in range(B7):
                    mm = pe.transpose(tp[:, u // 4, (u % 4) * P:(u % 4 + 1) * P], stage[:, u * P:(u + 1) * P],
                                      k.ident[:, :])
                mm.then_inc(turned, 1)

        @block.scalar
        def _(act):
            c = Chain(act, ach)
            with act.Fori(0, NB) as b:
                take(act, turned)
                act.sem_inc(stage_free, 1)
                c.go(act.activation(dst[:, ds(b * W7, 512)], tp[:, 0, :], ACT.Copy))
                c(act.activation(dst[:, ds(b * W7 + 512, W7 - 512)], tp[:, 1, 0:W7 - 512], ACT.Copy))
                c.reset()
                act.sem_inc(tp_free, 1)


def layernorm(k, src, dst, eps, scale=None, shift=None):
    with ExitStack() as st:
        s = k.sub(st)
        stats = s.sb("stats", [P, T, 6])
        mean, var, tmp, epst = s.sb("mean", [P, T]), s.sb("var", [P, T]), s.sb("t", [P, T]), s.sb("eps", [P, 1])
        ch, var_ready, std_ready = k.sem("lnchain"), k.sem("var_ready"), k.sem("std_ready")
        block = st.enter_context(k.block())

        @block.vector
        def _(dve):
            c = Chain(dve, ch)
            with dve.Fori(0, NB) as b:
                for u in range(B7):
                    each = ds(b * B7 + u, 1)
                    last = c.go(dve.bn_stats(flat2(stats[:, each, :]), flat2(src[:, each, :])))
                c.until(last)
                c.reset()
            c(dve.tensor_tensor(mean[:, :], stats[:, :, 1], stats[:, :, 4], ALU.add))
            c(dve.tensor_scalar(mean[:, :], mean[:, :], 0.5, None, ALU.mult))
            c(dve.tensor_tensor(var[:, :], stats[:, :, 2], stats[:, :, 5], ALU.add))
            c(dve.tensor_tensor(tmp[:, :], stats[:, :, 1], stats[:, :, 4], ALU.subtract))
            c(dve.scalar_tensor_tensor(tmp[:, :], tmp[:, :], 0.25, tmp[:, :], ALU.mult, ALU.mult))
            c(dve.scalar_tensor_tensor(var[:, :], var[:, :], 1.0 / D, tmp[:, :], ALU.mult, ALU.add))
            c(dve.memset(epst[:, :], eps))
            dve.sem_inc(var_ready, 1)
            c(dve.tensor_tensor(dst, src, mean[:, :].unsqueeze(2).broadcast_to([P, T, D]), ALU.subtract))
            dve.wait_ge(std_ready, 1)
            c(dve.reciprocal(tmp[:, :], var[:, :]))
            c(dve.tensor_tensor(dst, dst, tmp[:, :].unsqueeze(2).broadcast_to([P, T, D]), ALU.mult))
            if scale is not None:
                c(dve.tensor_tensor(dst, dst, scale.unsqueeze(1).broadcast_to([P, T, D]), ALU.mult))
                c(dve.tensor_tensor(dst, dst, shift.unsqueeze(1).broadcast_to([P, T, D]), ALU.add))

        @block.scalar
        def _(act):
            act.wait_ge(var_ready, 1)
            act.activation(var[:, :], var[:, :], ACT.Sqrt, bias=epst[:, 0:1]).then_inc(std_ready, 1)


def add_rows(k, dst, a, b):
    with ExitStack() as st:
        block = st.enter_context(k.block())

        @block.vector
        def _(dve):
            dve.tensor_tensor(dst, a, b, ALU.add)


def load(k, pairs):
    with ExitStack() as st:
        got = k.sem("loaded")
        block = st.enter_context(k.block())

        @block.sync
        def _(sp):
            for dst, src in pairs:
                sp.dma_start(dst, src).then_inc(got, 16)
            sp.wait_ge(got, 16 * len(pairs))


class Gather:

    def __init__(self, k, s, table, width, slot_src):
        self.k, self.table, self.width, self.slots = k, table, width, slot_src
        self.ring = s.sb("ring", [P, R * J, width])
        self.index = s.sb("index", [P, R * J], I32)
        self.landed, self.used = k.sem("landed"), k.sem("used")
        self.g_sem = [k.sem(f"group{r}_in") for r in range(R)]
        self.i_sem = [k.sem(f"index{h}_in") for h in range(2)]
        self.turns, self.sp_turns = k.sem("pool_turns"), k.sem("sp_turns")

    def pool(self, pool):
        hold = Hold(pool, self.turns)
        n = pool.value_load(self.k.total[0:1, 1:2], min_val=1, max_val=GMAX // R)
        with pool.Fori(0, n) as i:
            for r in range(R):
                if r % 2 == 0:
                    hold(self.i_sem[r // 2], 16 * (i + 1))
                hold(self.used, R * i + r + 1)
                for j in range(J):
                    at = r * J + j
                    pool.indirect_dma_start(self.ring[:, at, :], None, self.table,
                                            bass.IndirectOffsetOnAxis(self.index[:, at:at + 1], 0)
                                            ).then_inc(self.g_sem[r], 16)

    def load_index(self, sp, half, group):
        sp.dma_start(self.index[:, half * 2 * J:(half + 1) * 2 * J].rearrange("p (g j) -> p g j", j=J),
                     self.slots[ds(group, 2), :, :].rearrange("g p j -> p g j")).then_inc(self.i_sem[half], 16)

    def sync(self, sp):
        n = sp.value_load(self.k.total[0:1, 1:2], min_val=1, max_val=GMAX // R)
        for half in range(2):
            self.load_index(sp, half, 2 * half)
        with sp.Fori(0, n) as i:
            for r in range(R):
                sp.wait_ge(self.g_sem[r], 16 * J * (i + 1))
                sp.sem_inc(self.landed, 1)
                if r % 2 == 1:
                    self.load_index(sp, r // 2, (R * (i + 1) + r - 1).with_bounds(min_val=0, max_val=GMAX - 2))
        hold = Hold(sp, self.sp_turns)
        for half in range(2):
            hold(self.i_sem[half], 16 * (n + 1))

    def group(self, g):
        return self.ring[:, ds((g % R) * J, J), :]


def tiles_loop(k, eng):
    def bounds(t):
        n = eng.value_load(k.groups[0:1, ds(t, 1)], min_val=3, max_val=GMAX)
        g0 = eng.value_load(k.group0[0:1, ds(t, 1)], min_val=0, max_val=GMAX)
        return g0, n
    return bounds


def attention_pass(k, table, slot_src, width, heads, dim, scores, start, finish, extra):
    VB = heads * (dim + 1)
    with ExitStack() as st:
        s = k.sub(st)
        ga = Gather(k, s, table, width, slot_src)
        e5, x5 = (s.sb(x, [P, J + 1, heads]) for x in ("e5", "x5"))
        p5 = s.sb("p5", [P, J + 1, heads])
        warm = s.sb("warm", [P, 1])
        prod = s.sb("prod", [P, J + 1, VB])
        acc = s.sb("acc", [P, VB])
        rden, newmax = s.sb("rden", [P, heads]), s.sb("newmax", [P, heads])
        work = extra(s)
        ch, e_ready, p_ready = (k.sem(x) for x in ("atchain", "e_ready", "p_ready"))
        block = st.enter_context(k.block())
        block.gpsimd(ga.pool)
        block.sync(ga.sync)

        def by_head(ap):
            return ap.rearrange("p s (h c) -> p s h c", h=heads)

        @block.vector
        def _(dve):
            c = Chain(dve, ch)
            dve.sem_inc(ga.used, R)
            bounds = tiles_loop(k, dve)

            def weigh_rows(g):
                dve.wait_ge(p_ready, g + 1)
                dve.tensor_tensor(by_head(prod[:, 0:J, :]), by_head(ga.group(g)[:, :, 0:VB]),
                                  p5[:, 0:J, :].unsqueeze(3).broadcast_to([P, J, heads, dim + 1]),
                                  ALU.mult).then_inc(ga.used, 1)

            def weigh_sum():
                return c.go(dve.tensor_tensor(by_head(prod[:, J:J + 1, :]),
                                              acc[:, :].rearrange("p (s h c) -> p s h c", s=1, h=heads),
                                              p5[:, J:J + 1, :].unsqueeze(3).broadcast_to([P, 1, heads, dim + 1]),
                                              ALU.mult))

            def add_up():
                return dve.tensor_reduce(acc[:, :], prod[:, :, :].rearrange("p s c -> p c s"), AX.X, ALU.add)

            def take_maximum():
                return c.go(dve.tensor_reduce(newmax[:, :], e5[:, :, :].rearrange("p s h -> p h s"), AX.X, ALU.max))

            def off_maximum():
                return dve.tensor_tensor(x5[:, :, :], e5[:, :, :],
                                         newmax[:, :].unsqueeze(1).broadcast_to([P, J + 1, heads]),
                                         ALU.subtract).then_inc(e_ready, 1)

            with dve.Fori(0, T) as t:
                g0, n = bounds(t)
                start(dve, c, t, acc, e5[:, J, :], work)
                dve.wait_ge(ga.landed, g0 + 1)
                for f in scores(dve, ga.group(g0), e5[:, 0:J, :], work):
                    c(f())
                c.until(take_maximum())
                off_maximum()
                c.reset()
                with dve.Fori(g0 + 1, g0 + n) as g:
                    dve.wait_ge(ga.landed, g + 1)
                    first, second = scores(dve, ga.group(g), e5[:, 0:J, :], work)
                    scored = c.go(first())
                    weigh_rows(g - 1)
                    c.until(scored)
                    scored = c.go(second())
                    weighed = weigh_sum()
                    c.until(scored)
                    highest = take_maximum()
                    c.until(weighed)
                    add_up()
                    c.until(highest)
                    off_maximum()
                    c.until(highest)
                    c.reset()
                weigh_rows(g0 + n - 1)
                c.until(weigh_sum())
                c(add_up())
                a3 = acc[:, :].rearrange("p (h c) -> p h c", h=heads)
                c(dve.tensor_scalar(rden[:, :], a3[:, :, dim], 1e-16, None, ALU.add))
                c(dve.reciprocal(rden[:, :], rden[:, :]))
                c(dve.tensor_tensor(k.out[:, ds(t, 1), :].rearrange("p t (h c) -> p (t h) c", h=heads),
                                    a3[:, :, 0:dim], rden[:, :].unsqueeze(2).broadcast_to([P, heads, dim]),
                                    ALU.mult))
                finish(dve, c, t)
                c.reset()

        @block.scalar
        def _(act):
            n = act.value_load(k.total[0:1, 0:1], min_val=1, max_val=GMAX)
            act.activation(warm[:, :], k.ones[:, 0:1], ACT.Exp)
            with act.Fori(0, n):
                take(act, e_ready)
                act.activation(p5[:, :, :], x5[:, :, :], ACT.Exp)
                act.activation(e5[:, J, :], newmax[:, :], ACT.Copy).then_inc(p_ready, 1)


def gat_conv(k, x, W, a_src, a_dst, bias, table, slot_src, elu):
    H, C = 4, 32
    VB = H * (C + 1)
    with ExitStack() as st:
        s = k.sub(st)
        wext = s.sb("wext", [P, D + 2 * H])
        arow, brow = s.sb("arow", [P, 2, D]), s.sb("brow", [P, D])
        tmp = s.sb("tmp", [P, D])
        own = s.sb("own", [P, T, VB + 2 * H])
        load(k, [(wext[:, 0:D], W), (arow[:, 0, :], rows(a_src.rearrange("h c -> (h c)"))),
                 (arow[:, 1, :], rows(a_dst.rearrange("h c -> (h c)"))), (brow[:, :], rows(bias))])
        with ExitStack() as st2:
            ch = k.sem("wchain")
            block = st2.enter_context(k.block())

            @block.vector
            def _(dve):
                c = Chain(dve, ch)
                for i in range(2):
                    c(dve.tensor_tensor(tmp[:, :], wext[:, 0:D], arow[:, i, :], ALU.mult))
                    c(dve.tensor_reduce(wext[:, D + i * H:D + (i + 1) * H],
                                        tmp[:, :].rearrange("p (h c) -> p h c", h=H), AX.X, ALU.add))
                c(dve.memset(own[:, :, :], 1.0))

        def store(dve, c, ps, t, n):
            c(dve.tensor_copy(own[:, ds(t, n), 0:VB].rearrange("p u (h c) -> p u h c", h=H)[:, :, :, 0:C],
                              ps[:, :, 0:D].rearrange("p u (h c) -> p u h c", h=H)))
            c(dve.tensor_copy(own[:, ds(t, n), VB:VB + 2 * H], ps[:, :, D:D + 2 * H]))

        dense_rows(k, x, [(wext[:, :], D + 2 * H, store)], table, own, VB + H,
                   lambda row: row[:, VB:VB + H])

        def extra(s2):
            return s2.sb("ad", [P, H]), s2.sb("es", [P, J, H])

        def start(dve, c, t, acc, m, work):
            ad, _ = work
            o = own[:, ds(t, 1), :].rearrange("p t c -> p (t c)")
            c(dve.tensor_copy(acc[:, :], o[:, 0:VB]))
            c(dve.tensor_copy(ad[:, :], o[:, VB + H:VB + 2 * H]))
            c(dve.tensor_tensor(m, o[:, VB:VB + H], ad[:, :], ALU.add))
            c(dve.scalar_tensor_tensor(m, m, 0.2, m, ALU.mult, ALU.max))

        def scores(dve, g, e, work):
            ad, es = work
            return (lambda: dve.tensor_tensor(es[:, :, :], g[:, :, VB:VB + H],
                                              ad[:, :].unsqueeze(1).broadcast_to([P, J, H]), ALU.add),
                    lambda: dve.scalar_tensor_tensor(e, es[:, :, :], 0.2, es[:, :, :], ALU.mult, ALU.max))

        def finish(dve, c, t):
            o = k.out[:, ds(t, 1), :].rearrange("p t c -> p (t c)")
            c(dve.tensor_tensor(o, o, brow[:, :], ALU.add))

        attention_pass(k, table, slot_src, VB + H, H, C, scores, start, finish, extra)
    if elu:
        with ExitStack() as st:
            s = k.sub(st)
            neg = s.sb("neg", [P, NP])
            ch, n_ready, e_ready = k.sem("eluchain"), k.sem("neg_ready"), k.sem("exp_ready")
            block = st.enter_context(k.block())
            o = flat2(k.out[:, :, :])

            @block.vector
            def _(dve):
                c = Chain(dve, ch)
                c(dve.tensor_scalar(neg[:, :], o, 0.0, None, ALU.min))
                dve.sem_inc(n_ready, 1)
                dve.wait_ge(e_ready, 1)
                c(dve.tensor_scalar(neg[:, :], neg[:, :], -1.0, None, ALU.add))
                c(dve.scalar_tensor_tensor(o, o, 0.0, neg[:, :], ALU.max, ALU.add))

            @block.scalar
            def _(act):
                act.wait_ge(n_ready, 1)
                act.activation(neg[:, :], neg[:, :], ACT.Exp).then_inc(e_ready, 1)


def scatter_weights(k, dense, slot_src, slot_weight):
    with ExitStack() as st:
        s = k.sub(st)
        sl, wl = s.sb("sl", [P, B7, J], I32), s.sb("wl", [P, B7, J])
        slot, valid = s.sb("slot", [P, B7, J]), s.sb("valid", [P, B7, J])
        flat, wv = s.sb("flat", [P, 2, B7, J], I32), s.sb("wv", [P, 2, B7, J])
        posb, pos13 = s.sb("posb", [P, B7], I32), s.sb("pos13", [P, T], I32)
        degb, none = s.sb("degb", [P, B7]), s.sb("none", [P, B7, J])
        slots_in, slots_free, flat_ready, flat_free, ch, dt, pt = (k.sem(x) for x in (
            "slots_in", "slots_free", "flat_ready", "flat_free", "swchain", "sw_dt", "sw_pt"))
        done = [k.sem(f"added{u}") for u in range(B7)]
        block = st.enter_context(k.block())

        def bounds(eng, b):
            n = eng.value_load(k.bgroups[0:1, ds(b, 1)], min_val=1, max_val=GMAX)
            j0 = eng.value_load(k.bgroup0[0:1, ds(b, 1)], min_val=0, max_val=GMAX)
            return j0, n

        @block.sync
        def _(sp):
            with sp.Fori(0, NB) as b:
                j0, n = bounds(sp, b)
                g0 = [sp.value_load(k.group0[0:1, ds(b * B7 + u, 1)], min_val=0, max_val=GMAX)
                      for u in range(B7)]
                with sp.Fori(j0, j0 + n) as jj:
                    take(sp, slots_free)
                    for u in range(B7):
                        at = ds((g0[u] + (jj - j0)).with_bounds(min_val=0, max_val=GMAX - 1), 1)
                        sp.dma_start(sl[:, u, :], slot_src[at, :, :].rearrange("g p j -> (g p) j")
                                     ).then_inc(slots_in, 16)
                        sp.dma_start(wl[:, u, :], slot_weight[at, :, :].bitcast(F32).rearrange("g p j -> (g p) j")
                                     ).then_inc(slots_in, 16)

        @block.vector
        def _(dve):
            c = Chain(dve, ch)
            hold = Hold(dve, dt)
            c(dve.memset(none[:, :, :], 0.0))
            c(dve.tensor_single_scalar(pos13[:, :], k.pos[:, :], 13, ALU.logical_shift_left))
            c.reset()
            dve.sem_inc(slots_free, 1)
            dve.sem_inc(flat_free, 2)
            with dve.Fori(0, NB) as b:
                j0, n = bounds(dve, b)
                c(dve.tensor_copy(degb[:, :], k.deg[:, ds(b * B7, B7)]))
                c(dve.tensor_copy(posb[:, :], pos13[:, ds(b * B7, B7)]))
                c(dve.tensor_copy(slot[:, :, :], k.ramp[:, 0:J].unsqueeze(1).broadcast_to([P, B7, J])))
                c.reset()
                with dve.Fori(j0, j0 + n) as jj:
                    hold(slots_in, 16 * 2 * B7 * (jj + 1))
                    hold(flat_free, jj + 1)
                    fl, wf = (x[:, ds(jj % 2, 1)].rearrange("p q u j -> p (q u) j") for x in (flat, wv))
                    c(dve.tensor_tensor(valid[:, :, :], slot[:, :, :],
                                        degb[:, :].unsqueeze(2).broadcast_to([P, B7, J]), ALU.is_lt))
                    c(dve.tensor_scalar(slot[:, :, :], slot[:, :, :], float(J), None, ALU.add))
                    c(dve.scalar_tensor_tensor(valid[:, :, :], sl[:, :, :], float(-DUMMY), valid[:, :, :],
                                               ALU.add, ALU.mult))
                    c(dve.tensor_scalar(fl, valid[:, :, :], float(DUMMY), None, ALU.add))
                    c(dve.tensor_tensor(fl, fl, posb[:, :].unsqueeze(2).broadcast_to([P, B7, J]),
                                        ALU.bitwise_or))
                    c(dve.tensor_copy(wf, wl[:, :, :]))
                    dve.sem_inc(slots_free, 1)
                    dve.sem_inc(flat_ready, 1)
                    c.reset()
            j0, n = bounds(dve, NB - 1)
            total = j0 + n
            pairs = dve.value_load(k.total[0:1, 3:4], min_val=1, max_val=GMAX)
            with dve.If(pairs * 2 + 2 > total):
                with dve.Fori(total, pairs * 2 + 2) as jj:
                    hold(flat_free, jj + 1)
                    fl, wf = (x[:, ds(jj % 2, 1)].rearrange("p q u j -> p (q u) j") for x in (flat, wv))
                    c(dve.tensor_scalar(fl, posb[:, :].unsqueeze(2).broadcast_to([P, B7, J]), DUMMY, None,
                                        ALU.bitwise_or))
                    c(dve.tensor_copy(wf, none[:, :, :]))
                    dve.sem_inc(flat_ready, 1)
                    c.reset()

        @block.gpsimd
        def _(pool):
            hold = Hold(pool, pt)

            def add_slot(step, first_step, pair):
                q, j = step // J % 2, step % J
                for u in range(B7):
                    if not first_step:
                        hold(done[u], 16 * (2 * J * pair + step))
                    pool.indirect_dma_start(
                        dense, bass.IndirectOffsetOnAxis(flat[:, q, u, j:j + 1], 0), wv[:, q, u, j:j + 1],
                        None, compute_op=ALU.add).then_inc(done[u], 16)

            def rest_of_pair(pair):
                for step in range(1, 2 * J):
                    if step == J:
                        hold(flat_ready, 2 * pair + 2)
                    add_slot(step, False, pair)
                    if step == J:
                        pool.sem_inc(flat_free, 1)

            pairs = pool.value_load(k.total[0:1, 3:4], min_val=1, max_val=GMAX)
            pool.wait_ge(flat_ready, 1)
            add_slot(0, True, 0)
            with pool.Fori(0, pairs) as i:
                rest_of_pair(i)
                hold(flat_ready, 2 * i + 3)
                add_slot(2 * J, False, i)
                pool.sem_inc(flat_free, 1)
            rest_of_pair(pairs)
            for u in range(B7):
                hold(done[u], 16 * 2 * J * (pairs + 1))


def sum_by_source(k, x, dense, fnt):
    HALF, UN = NP // 2, 4
    MM = 448
    with ExitStack() as st:
        s = k.sub(st)
        mat = s.sb("mat", [P, UN, HALF])
        xs = s.sb("xs", [P, UN, D])
        acc = s.ps("fsum", [P, HALF // MM, 512])
        m_in = [k.sem(f"mat{u}_in") for u in range(UN)]
        m_free, x_ready = [k.sem(f"mfree{u}") for u in range(UN)], [k.sem(f"xs_ready{u}") for u in range(UN)]
        x_free = [k.sem(f"xs_free{u}") for u in range(UN)]
        ch, acc_done, acc_out, turns = (k.sem(x) for x in ("sschain", "acc_done", "acc_out", "ss_turns"))
        block = st.enter_context(k.block())
        view = dense.rearrange("(t p c) o -> t p (c o)", p=P, c=PITCH)
        IT = (T - 1) // UN

        @block.sync
        def _(sp):
            for h in range(2):
                def fetch(t, u):
                    take(sp, m_free[u])
                    sp.dma_start(mat[:, u, :], view[ds(t, 1), :, h * HALF:(h + 1) * HALF]
                                 .rearrange("t p c -> (t p) c")).then_inc(m_in[u], 16)
                fetch(0, 0)
                with sp.Fori(0, IT) as i:
                    for u in range(UN):
                        fetch(1 + UN * i + u, (u + 1) % UN)

        @block.vector
        def _(dve):
            c = Chain(dve, ch)
            for u in range(UN):
                dve.sem_inc(m_free[u], 1)
                dve.sem_inc(x_free[u], 1)
            for h in range(2):
                def stage(t, u):
                    take(dve, x_free[u])
                    c(dve.tensor_copy(xs[:, u, :], flat2(x[:, ds(t, 1), :])))
                    dve.sem_inc(x_ready[u], 1)
                stage(0, 0)
                c.reset()
                with dve.Fori(0, IT) as i:
                    for u in range(UN):
                        stage(1 + UN * i + u, (u + 1) % UN)
                    c.reset()
                dve.wait_ge(acc_done, h + 1)
                for m in range(HALF // MM):
                    c(dve.tensor_copy(fnt[:, h * HALF + m * MM:h * HALF + (m + 1) * MM], acc[:, m, 0:MM]))
                c.reset()
                dve.sem_inc(acc_out, 1)

        @block.tensor
        def _(pe):
            hold = Hold(pe, turns)
            for h in range(2):
                def multiply(u, count, start):
                    hold(m_in[u], count)
                    take(pe, x_ready[u])
                    for m in range(HALF // MM):
                        mm = pe.matmul(acc[:, m, 0:MM], xs[:, u, :], mat[:, u, m * MM:(m + 1) * MM],
                                       start=start, stop=start, skip_group_check=True)
                    mm.then_inc(m_free[u], 1)
                    pe.drain().then_inc(x_free[u], 1)
                if h:
                    pe.wait_ge(acc_out, 1)
                each = [IT + (u == 0) for u in range(UN)]
                multiply(0, 16 * (h * each[0] + 1), True)
                with pe.Fori(0, IT) as i:
                    for u in range(UN):
                        v = (u + 1) % UN
                        multiply(v, 16 * (h * each[v] + (v == 0) + 1) + 16 * i, False)
                pe.drain().then_inc(acc_done, 1)


def residual_layer(k, x, w_self_t, b_self, w_neigh_t, b_neigh, scale, offset, dense, slot_src, slot_weight,
                   by_node):
    scatter_weights(k, dense, slot_src, slot_weight)
    with ExitStack() as st:
        s = k.sub(st)
        ws, wn = s.sb("ws", [P, D]), s.sb("wn", [P, D])
        br, sc, of = s.sb("br", [P, 2, D]), s.sb("sc", [P, 2 * D]), s.sb("of", [P, 2 * D])
        own = s.sb("selfrows", [P, T, D])
        load(k, [(ws[:, :], w_self_t), (wn[:, :], w_neigh_t), (br[:, 0, :], rows(b_self)),
                 (br[:, 1, :], rows(b_neigh)), (sc[:, :], rows(scale)), (of[:, :], rows(offset))])

        def store(dst, bias):
            def f(dve, c, ps, t, n):
                o = dst[:, ds(t, n), :]
                c(dve.tensor_tensor(o, ps, bias.unsqueeze(1).broadcast_to([P, n, D]), ALU.add))
                c(dve.tensor_scalar(o, o, 0.0, None, ALU.max))
            return f

        dense_rows(k, x, [(ws[:, :], D, store(own, br[:, 0, :]))])
        layernorm(k, own[:, :, :], own[:, :, :], 1e-9, sc[:, 0:D], of[:, 0:D])
        with ExitStack() as st2:
            s2 = k.sub(st2)
            fnt = s2.sb("fnt", [P, NP])
            sum_by_source(k, x, dense, fnt)
            transpose_blocks(k, fnt, flat2(k.out[:, :, :]))
        dense_rows(k, k.out[:, :, :], [(wn[:, :], D, store(k.out, br[:, 1, :]))])
        layernorm(k, k.out[:, :, :], k.out[:, :, :], 1e-9, sc[:, D:2 * D], of[:, D:2 * D])
        with ExitStack() as st3:
            done = k.sem("by_node_out")
            block = st3.enter_context(k.block())

            @block.sync
            def _(sp):
                sp.dma_start(by_node.rearrange("(t p) c -> p t c", p=P), k.out[:, :, :]).then_inc(done, 16)
                sp.wait_ge(done, 16)
        gather_rows(k, by_node, k.out[:, :, :], k.node)
        add_rows(k, k.out[:, :, :], k.out[:, :, :], own[:, :, :])
        add_rows(k, k.out[:, :, :], k.out[:, :, :], x)
    layernorm(k, k.out[:, :, :], x, 1e-5)


def dense_cols(k, src, weights, store):
    with ExitStack() as st:
        s = k.sub(st)
        acc = s.ps("dcacc", [P, 2, len(weights), 512])
        ch = k.sem("dcchain")
        done, free = ([k.sem(f"{x}{u}") for u in range(2)] for x in ("dc_done", "dc_free"))
        block = st.enter_context(k.block())

        @block.tensor
        def _(pe):
            with pe.Fori(0, NBLK // 2) as i:
                for u in range(2):
                    take(pe, free[u])
                    for o, ws in enumerate(weights):
                        for b, w in enumerate(ws):
                            mm = pe.matmul(acc[:, u, o, 0:BLK], w, src[b][:, ds((2 * i + u) * BLK, BLK)],
                                           start=(b == 0), stop=(b == len(ws) - 1))
                    mm.then_inc(done[u], 1)

        @block.vector
        def _(dve):
            c = Chain(dve, ch)
            for u in range(2):
                dve.sem_inc(free[u], 1)
            with dve.Fori(0, NBLK // 2) as i:
                for u in range(2):
                    take(dve, done[u])
                    for o in range(len(weights)):
                        store(dve, c, acc[:, u, o, 0:BLK], 2 * i + u, o)
                    dve.sem_inc(free[u], 1)
                c.reset()


def scale_shift(dve, c, act_std, mean, var, gamma, beta, scale, shift):
    act_std()
    c(dve.reciprocal(scale, var))
    c(dve.tensor_tensor(scale, scale, gamma, ALU.mult))
    c(dve.tensor_tensor(shift, mean, scale, ALU.mult))
    c(dve.tensor_tensor(shift, beta, shift, ALU.subtract))


def batchnorm_cols(k, a, gamma, beta):
    with ExitStack() as st:
        s = k.sub(st)
        parts = split(N, 512)
        stats, mv, sc, sh, ep = (s.sb(x, sh_) for x, sh_ in (("stats", [P, len(parts), 6]), ("mv", [P, 2]),
                                                            ("sc", [P, 1]), ("sh", [P, 1]), ("ep", [P, 1])))
        ch, v_ready, s_ready = k.sem("bnchain"), k.sem("bn_var"), k.sem("bn_std")
        block = st.enter_context(k.block())

        @block.vector
        def _(dve):
            c = Chain(dve, ch)
            c(dve.memset(ep[:, :], 1e-5))
            for i, (at, n) in enumerate(parts):
                c(dve.bn_stats(stats[:, i, :], a[:, at:at + n]))
            c(dve.bn_aggr(mv[:, :], stats[:, :, :]))

            def std():
                dve.sem_inc(v_ready, 1)
                dve.wait_ge(s_ready, 1)
            scale_shift(dve, c, std, mv[:, 0:1], mv[:, 1:2], gamma, beta, sc[:, :], sh[:, :])
            c(dve.tensor_scalar(a[:, :], a[:, :], sc[:, 0:1], sh[:, 0:1], ALU.mult, ALU.add))

        @block.scalar
        def _(act):
            act.wait_ge(v_ready, 1)
            act.activation(mv[:, 1:2], mv[:, 1:2], ACT.Sqrt, bias=ep[:, 0:1]).then_inc(s_ready, 1)


def attention_layer(k, x, w, table, slot_src):
    H, C = 8, 16
    VB = H * (C + 1)
    F = 512
    with ExitStack() as st:
        s = k.sub(st)
        with ExitStack() as st1:
            s1 = k.sub(st1)
            wq, wk, wv = (s1.sb(n, [P, D]) for n in ("wq", "wk", "wv"))
            qb = s1.sb("qb", [P, D])
            kv = s1.sb("kv", [P, T, 2 * VB])
            q = s1.sb("q", [P, T, VB])
            load(k, [(wq[:, :], w["q_w"]), (wk[:, :], w["k_w"]), (wv[:, :], w["v_w"]), (qb[:, :], rows(w["q_b"]))])
            with ExitStack() as st2:
                block = st2.enter_context(k.block())

                @block.vector
                def _(dve):
                    dve.memset(kv[:, :, 0:VB], 1.0)
                    dve.memset(kv[:, :, VB:2 * VB], 0.0)
                    dve.memset(q[:, :, :], 1.0)

            def heads(ap):
                return ap.rearrange("p u (h c) -> p u h c", h=H)

            def store_v(dve, c, ps, t, n):
                c(dve.tensor_copy(heads(kv[:, ds(t, n), 0:VB])[:, :, :, 0:C], heads(ps)))

            def store_k(dve, c, ps, t, n):
                c(dve.tensor_copy(heads(kv[:, ds(t, n), VB:2 * VB])[:, :, :, 0:C], heads(ps)))

            def store_q(dve, c, ps, t, n):
                for u in range(n):
                    qq = q[:, ds(t + u, 1), :].rearrange("p u (h c) -> p (u h) c", h=H)[:, :, 0:C]
                    c(dve.tensor_tensor(qq, ps[:, u, :].rearrange("p (h c) -> p h c", h=H),
                                        qb[:, :].rearrange("p (h c) -> p h c", h=H), ALU.add))
                    c(dve.tensor_scalar(qq, qq, float(C) ** -0.5, None, ALU.mult))

            dense_rows(k, x, [(wv[:, :], D, store_v), (wk[:, :], D, store_k), (wq[:, :], D, store_q)], table, kv, 2 * VB,
                          lambda row: row[:, VB:2 * VB].rearrange("p (h c) -> p h c", h=H)[:, :, C:C + 1])

            def extra(s2):
                return s2.sb("qt", [P, VB]), s2.sb("qk", [P, J, VB])

            def start(dve, c, t, acc, m, work):
                qt, qk = work
                o = kv[:, ds(t, 1), :].rearrange("p t c -> p (t c)")
                c(dve.tensor_copy(acc[:, :], o[:, 0:VB]))
                c(dve.tensor_copy(qt[:, :], flat2(q[:, ds(t, 1), :])))
                c(dve.tensor_tensor(qk[:, 0, :], o[:, VB:2 * VB], qt[:, :], ALU.mult))
                c(dve.tensor_reduce(m, qk[:, 0, :].rearrange("p (h c) -> p h c", h=H), AX.X, ALU.add))

            def scores(dve, g, e, work):
                qt, qk = work
                return (lambda: dve.tensor_tensor(qk[:, :, :], g[:, :, VB:2 * VB],
                                                  qt[:, :].unsqueeze(1).broadcast_to([P, J, VB]), ALU.mult),
                        lambda: dve.tensor_reduce(e, qk[:, :, :].rearrange("p s (h c) -> p s h c", h=H), AX.X,
                                                  ALU.add))

            attention_pass(k, table, slot_src, 2 * VB, H, C, scores, start, lambda *a: None, extra)
        wo, l1, l2 = s.sb("wo", [P, D]), s.sb("l1", [P, F]), s.sb("l2", [P, F // P, D])
        vec = s.sb("vec", [P, 16])
        xt, st_ = s.sb("xt2", [P, NP]), s.sb("ot2", [P, NP])
        names = ("out_b", "g1", "b1", "lin2_b", "g2", "b2")
        load(k, [(wo[:, :], w["out_w"]), (l1[:, :], w["lin1_w"]),
                 (l2[:, :, :], w["lin2_w"].rearrange("(f p) d -> p f d", p=P)),
                 (vec[:, 8:12], w["lin1_b"])] +
             [(vec[:, i:i + 1], w[n]) for i, n in enumerate(names)])
        col = {n: vec[:, i:i + 1] for i, n in enumerate(names)}
        transpose_blocks(k, flat2(x), xt)
        transpose_blocks(k, flat2(k.out[:, :, :]), st_)

        def add_attn(dve, c, ps, i, o):
            a = xt[:, ds(i * BLK, BLK)]
            c(dve.scalar_tensor_tensor(a, ps, col["out_b"], a, ALU.add, ALU.add))

        dense_cols(k, [st_], [[wo[:, :]]], add_attn)
        batchnorm_cols(k, xt, col["g1"], col["b1"])
        with ExitStack() as st3:
            s3 = k.sub(st3)
            hid = [s3.sb(f"hid{f}", [P, NP]) for f in range(F // P - 2)] + [st_]
            hid.append(k.out[:, :, :].rearrange("p t c -> p (t c)"))

            def hidden(dve, c, ps, i, o):
                h = hid[o][:, ds(i * BLK, BLK)]
                c(dve.tensor_scalar(h, ps, vec[:, 8 + o:9 + o], None, ALU.add))
                c(dve.scalar_tensor_tensor(h, h, 0.01, h, ALU.mult, ALU.max))

            def add_ff(dve, c, ps, i, o):
                a = xt[:, ds(i * BLK, BLK)]
                c(dve.scalar_tensor_tensor(a, ps, col["lin2_b"], a, ALU.add, ALU.add))

            dense_cols(k, [xt], [[l1[:, f * P:(f + 1) * P]] for f in range(F // P)], hidden)
            dense_cols(k, hid, [[l2[:, f, :] for f in range(F // P)]], add_ff)
        batchnorm_cols(k, xt, col["g2"], col["b2"])
        transpose_blocks(k, xt, flat2(k.out[:, :, :]))
        add_rows(k, k.out[:, :, :], k.out[:, :, :], x)
    layernorm(k, k.out[:, :, :], x, 1e-5)


def edge_mlp_layer(k, x, w, table, slot_src, kept, running, empty_dram, cnt_dram, out):
    with ExitStack() as st:
        s = k.sub(st)
        th, ph, fc = s.sb("th", [P, D]), s.sb("ph", [P, D]), s.sb("fc", [P, D])
        vec = s.sb("vec3", [P, 4])
        at = s.sb("at", [P, NP])
        sums = s.sb("sums", [P, 8])
        coef = s.sb("coef", [P, 4])
        load(k, [(th[:, :], w["theta_w"]), (ph[:, :], w["phi_w"]), (fc[:, :], w["fc1_w"])] +
             [(vec[:, i:i + 1], w[n]) for i, n in enumerate(("bn0_g", "bn0_b", "bn1_g", "bn1_b"))])
        with ExitStack() as st1:
            block = st1.enter_context(k.block())
            ch1 = k.sem("l3c")

            @block.vector
            def _(dve):
                c = Chain(dve, ch1)
                c(dve.tensor_tensor(ph[:, :], ph[:, :], th[:, :], ALU.subtract))

        def store_b(dve, c, ps, t, n):
            c(dve.tensor_copy(k.out[:, ds(t, n), :], ps))

        dense_rows(k, x, [(ph[:, :], D, store_b)], table, k.out, D)
        degr, empr = s.sb("degr", [P, NP]), s.sb("empr", [P, NP])
        with ExitStack() as st1:
            s1 = k.sub(st1)
            tt = s1.sb("tt", [T, 2, P])
            pt = s1.ps("pt", [T, 2, P])
            a_, b_, c_ = k.sem("dr_t"), k.sem("dr_c"), k.sem("dr_o")
            d_, e_ = k.sem("dr_i"), k.sem("dr_ch")
            block = st1.enter_context(k.block())

            @block.tensor
            def _(pe):
                pe.transpose(pt[:, 0, :], k.deg[:, :], k.ident[:, :])
                pe.transpose(pt[:, 1, :], k.empty[:, :], k.ident[:, :]).then_inc(a_, 1)

            @block.vector
            def _(dve):
                c = Chain(dve, e_)
                dve.wait_ge(a_, 1)
                c(dve.tensor_copy(tt[:, :, :], pt[:, :, :]))
                c(dve.tensor_scalar(tt[:, 0, :], tt[:, 0, :], 1.0, None, ALU.max))
                c(dve.reciprocal(tt[:, 0, :], tt[:, 0, :]))
                dve.sem_inc(b_, 1)

            @block.sync
            def _(sp):
                sp.wait_ge(b_, 1)
                sp.dma_start(cnt_dram.rearrange("(t p) -> t p", p=P), tt[:, 0, :]).then_inc(c_, 16)
                sp.dma_start(empty_dram.rearrange("(t p) -> t p", p=P), tt[:, 1, :]).then_inc(c_, 16)
                sp.wait_ge(c_, 32)
                sp.dma_start(degr[:, :], rows(cnt_dram)).then_inc(d_, 16)
                sp.dma_start(empr[:, :], rows(empty_dram)).then_inc(d_, 16)
                sp.wait_ge(d_, 32)

        hT = s.sb("hT", [P, NP])
        transpose_blocks(k, flat2(x), hT)

        def store_a(dve, c, ps, i, o):
            c(dve.tensor_copy(at[:, ds(i * BLK, BLK)], ps))

        dense_cols(k, [hT], [[th[:, :]]], store_a)

        goes_on = s.sb("goes_on", [P, CAP])
        edge_stats(k, table, slot_src, at, sums, kept, goes_on)
        edge_bn0(k, at, empr, sums, vec, coef)
        edge_kept(k, fc, coef, sums, None, kept, goes_on, running)
        edge_regather(k, table, slot_src, at, fc, coef, sums, None)
        edge_dummy(k, at, fc, coef, sums, empr, vec, hT, False)
        agg = k.out[:, :, :].rearrange("p t c -> p (t c)")
        edge_kept(k, fc, coef, sums, agg, kept, goes_on, running)
        edge_regather(k, table, slot_src, at, fc, coef, sums, agg)
        edge_dummy(k, at, fc, coef, sums, empr, vec, hT, True)
        with ExitStack() as st1:
            ch = k.sem("l3e")
            block = st1.enter_context(k.block())

            @block.vector
            def _(dve):
                c = Chain(dve, ch)
                c(dve.tensor_tensor(agg, agg, hT[:, :], ALU.subtract))
                c(dve.tensor_tensor(hT[:, :], agg, degr[:, :], ALU.mult))
        transpose_blocks(k, hT, agg)
        with ExitStack() as st1:
            ch = k.sem("l3f")
            block = st1.enter_context(k.block())
            o, xx = k.out[:, :, :], x

            @block.vector
            def _(dve):
                c = Chain(dve, ch)
                c(dve.tensor_tensor(o, o, xx, ALU.add))
                c(dve.scalar_tensor_tensor(o, o, 0.0, xx, ALU.max, ALU.add))
    layernorm(k, k.out[:, :, :], k.out[:, :, :], 1e-5)
    with ExitStack() as st:
        done = k.sem("out_written")
        block = st.enter_context(k.block())

        @block.gpsimd
        def _(pool):
            for t in range(T):
                n = P if t < T - 1 else LAST
                pool.indirect_dma_start(out, bass.IndirectOffsetOnAxis(k.node[0:n, t:t + 1], 0),
                                        k.out[0:n, t, :], None).then_inc(done, 16)
            pool.wait_ge(done, 16 * T)


def rounds(k, eng):
    return eng.value_load(k.total[0:1, 1:2], min_val=1, max_val=GMAX // R)


def edge_stats(k, table, slot_src, at, sums, kept, goes_on):
    with ExitStack() as st:
        s = k.sub(st)
        ga = Gather(k, s, table, D, slot_src)
        tb = s.sb("tb", [P, R, J * P])
        att, zero = s.sb("att", [P, D]), s.sb("zero1", [P, 1])
        stats, acc = s.sb("stats", [P, 6]), StatSums(s)
        bt = s.ps("bt", [P, R, 512])
        turns, aturns, pturns, ch, copied, read, free = (k.sem(n) for n in (
            "turns", "aturns", "pturns", "ch", "copied", "read", "tb_free"))
        stored = [k.sem(f"stored{r}") for r in range(R)]
        block = st.enter_context(k.block())
        block.gpsimd(ga.pool)
        block.sync(ga.sync)

        @block.vector
        def _(dve):
            c = Chain(dve, ch)
            hold = Hold(dve, turns)
            for sem in (ga.used, read):
                dve.sem_inc(sem, R)
            c(dve.memset(tb[:, :, :], 0.0))
            dve.sem_inc(copied, 1)
            acc.clear(dve, c)
            c(dve.memset(goes_on[:, :], 1.0))
            c(dve.memset(zero[:, :], 0.0))
            c.reset()
            bounds = tiles_loop(k, dve)
            with dve.Fori(0, T) as t:
                g0, n = bounds(t)
                c(dve.tensor_copy(att[:, :], at[:, ds(t * P, P)]))
                c(dve.tensor_copy(goes_on[:, ds((g0 % CAP).with_bounds(min_val=0, max_val=CAP - 1), 1)],
                                  zero[:, :]))
                c.reset()
                with dve.Fori(g0, g0 + n) as g:
                    slot = tb[:, ds(g % R, 1), :].rearrange("p r c -> p (r c)")
                    hold(ga.used, g + 1 + R)
                    hold(free, g + 1)
                    c(dve.tensor_tensor(slot.rearrange("p (j c) -> p j c", j=J),
                                        bt[:, ds(g % R, 1), :].rearrange("p r (j c) -> p (r j) c", j=J),
                                        att[:, :].unsqueeze(1).broadcast_to([P, J, D]), ALU.add))
                    dve.sem_inc(copied, 1)
                    dve.sem_inc(read, 1)
                    c(dve.bn_stats(stats[:, :], slot))
                    acc.add(dve, c, stats)
                    c.reset()
            acc.finish(dve, c, sums[:, 0:1], sums[:, 1:2])

        @block.tensor
        def _(pe):
            hold = Hold(pe, pturns)
            with pe.Fori(0, rounds(k, pe)) as i:
                for r in range(R):
                    hold(ga.landed, R * i + r + 1)
                    hold(read, R * i + r + 1)
                    for j in range(J):
                        mm = pe.transpose(bt[:, r, j * P:(j + 1) * P], ga.ring[:, r * J + j, :], k.ident[:, :])
                    mm.then_inc(ga.used, 1)

        @block.scalar
        def _(act):
            hold = Hold(act, aturns)

            def store(r, group):
                act.dma_start(kept[ds(group, 1), :, :].rearrange("g p c -> (g p) c"),
                              tb[:, r, :]).then_inc(stored[r], 16)

            act.wait_ge(copied, 1)
            for r in range(R):
                store(r, CAP + r)
            n = rounds(k, act)
            with act.Fori(0, n) as i:
                for r in range(R):
                    hold(stored[r], 16 * (i + 1))
                    act.sem_inc(free, 1)
                    hold(copied, R * i + r + 2)
                    store(r, ((R * i + r) % CAP).with_bounds(min_val=0, max_val=CAP - 1))
            for r in range(R):
                hold(stored[r], 16 * (n + 1))


class StatSums:

    def __init__(self, s):
        self.sum6, self.msq, self.sq = s.sb("sum6", [P, 6]), s.sb("msq", [P, 2]), s.sb("sq2", [P, 2])

    def clear(self, dve, c):
        c.go(dve.memset(self.sum6[:, :], 0.0))
        c(dve.memset(self.msq[:, :], 0.0))

    def add(self, dve, c, stats):
        means = stats[:, :].rearrange("p (h v) -> p h v", v=3)[:, :, 1]
        c.go(dve.tensor_tensor(self.sum6[:, :], self.sum6[:, :], stats[:, :], ALU.add))
        c(dve.tensor_tensor(self.sq[:, :], means, means, ALU.mult))
        c(dve.tensor_tensor(self.msq[:, :], self.msq[:, :], self.sq[:, :], ALU.add))

    def finish(self, dve, c, total, squares):
        half = float(J * P // 2)
        s6 = self.sum6
        c(dve.tensor_tensor(total, s6[:, 1:2], s6[:, 4:5], ALU.add))
        c(dve.tensor_scalar(total, total, half, None, ALU.mult))
        c(dve.tensor_tensor(squares, self.msq[:, 0:1], self.msq[:, 1:2], ALU.add))
        c(dve.scalar_tensor_tensor(squares, squares, half, s6[:, 2:3], ALU.mult, ALU.add))
        c(dve.tensor_tensor(squares, squares, s6[:, 5:6], ALU.add))


def finish_bn(k, sums, mean_col, sq_col, gamma, beta, scale, shift):
    with ExitStack() as st:
        s = k.sub(st)
        m, v, t, ep = (s.sb(n, [P, 1]) for n in ("m", "v", "t", "ep"))
        ch, a_, b_ = k.sem("fbch"), k.sem("fba"), k.sem("fbb")
        block = st.enter_context(k.block())

        @block.vector
        def _(dve):
            c = Chain(dve, ch)
            c(dve.memset(ep[:, :], 1e-5))
            c(dve.tensor_scalar(m[:, :], sums[:, mean_col:mean_col + 1], 1.0 / E, None, ALU.mult))
            c(dve.tensor_scalar(v[:, :], sums[:, sq_col:sq_col + 1], 1.0 / E, None, ALU.mult))
            c(dve.tensor_tensor(t[:, :], m[:, :], m[:, :], ALU.mult))
            c(dve.tensor_tensor(v[:, :], v[:, :], t[:, :], ALU.subtract))
            c(dve.tensor_scalar(v[:, :], v[:, :], 0.0, None, ALU.max))

            def std():
                dve.sem_inc(a_, 1)
                dve.wait_ge(b_, 1)
            scale_shift(dve, c, std, m[:, :], v[:, :], gamma, beta, scale, shift)

        @block.scalar
        def _(act):
            act.wait_ge(a_, 1)
            act.activation(v[:, :], v[:, :], ACT.Sqrt, bias=ep[:, 0:1]).then_inc(b_, 1)


def edge_bn0(k, at, empr, sums, vec, coef):
    with ExitStack() as st:
        s = k.sub(st)
        ea, junk = s.sb("ea", [P, NP]), s.sb("junk3", [P, NP])
        ch = k.sem("bn0ch")
        with ExitStack() as st1:
            block = st1.enter_context(k.block())

            @block.vector
            def _(dve):
                c = Chain(dve, ch)
                c(dve.tensor_tensor(ea[:, :], empr[:, :], at[:, :], ALU.mult))
                c(dve.tensor_reduce(sums[:, 2:3], ea[:, :], AX.X, ALU.add))
                c(dve.tensor_tensor(junk[:, :], ea[:, :], at[:, :], ALU.mult))
                c(dve.tensor_reduce(sums[:, 3:4], junk[:, :], AX.X, ALU.add))
                c(dve.tensor_tensor(sums[:, 4:6], sums[:, 0:2], sums[:, 2:4], ALU.subtract))
        finish_bn(k, sums, 4, 5, vec[:, 0:1], vec[:, 1:2], coef[:, 0:1], coef[:, 1:2])
        ch2 = k.sem("bn0ch2")
        with ExitStack() as st1:
            block = st1.enter_context(k.block())

            @block.vector
            def _(dve):
                c = Chain(dve, ch2)
                c(dve.tensor_scalar(at[:, :], at[:, :], coef[:, 0:1], coef[:, 1:2], ALU.mult, ALU.add))
                c(dve.memset(sums[:, :], 0.0))


def edge_kept(k, fc, coef, sums, agg, kept, goes_on, running):
    with ExitStack() as st:
        s = k.sub(st)
        W = J * P
        tb, r4, z = (s.sb(n, [P, R, W]) for n in ("tb", "r4", "z"))
        zsum, run = s.sb("zsum", [P, R, D]), s.sb("run", [P, R, D])
        last_group = s.sb("last_group", [P, T], I32)
        stats, fold = s.sb("stats", [P, CAP, 2, 3]), s.sb("fold", [P, CAP, 2])
        warm = s.sb("warm", [P, 1])
        e1 = s.ps("e1", [P, R, 512])
        relued, product, posted, zused, ch, vt, at_, pt, st_, summed, clear, all_out, gt = (
            k.sem(n) for n in ("relued", "product", "posted", "z_used", "ch", "vt", "at_", "pt", "st_", "summed",
                               "run_clear", "all_out", "gt"))
        fetched = [k.sem(f"sums{h}_in") for h in range(2)]
        stored = [k.sem(f"run{r}_out") for r in range(R)]
        loaded = [k.sem(f"tb{r}_in") for r in range(R)]
        block = st.enter_context(k.block())

        def when(eng):
            return eng.If(rounds(k, eng) <= CAP // R)

        def fetch_sums(eng, half):
            for t in range(half, T, 2):
                g = eng.value_load(last_group[0:1, t:t + 1], min_val=0, max_val=CAP - 1)
                eng.dma_start(agg[:, t * P:(t + 1) * P], running[ds(g, 1), :, :].rearrange("g p c -> (g p) c")
                              ).then_inc(fetched[half], 16)
            eng.wait_ge(fetched[half], 16 * len(range(half, T, 2)))

        def fetch_rows(eng, hold):
            with eng.Fori(0, rounds(k, eng)) as i:
                for r in range(R):
                    g = (R * i + r).with_bounds(min_val=0, max_val=CAP - 1)
                    hold(relued, R * i + r + 1)
                    eng.dma_start(tb[:, r, :], kept[ds(g, 1), :, :].rearrange("g p c -> (g p) c")
                                  ).then_inc(loaded[r], 16)

        @block.sync
        def _(sp):
            with when(sp):
                fetch_rows(sp, Hold(sp, st_))
                if agg is not None:
                    sp.wait_ge(all_out, 1)
                    fetch_sums(sp, 0)

        @block.gpsimd
        def _(pool):
            hold = Hold(pool, gt)

            def store(r, group):
                pool.dma_start(running[ds(group, 1), :, :].rearrange("g p c -> (g p) c"),
                               run[:, r, :]).then_inc(stored[r], 16)

            if agg is not None:
                with when(pool):
                    pool.wait_ge(clear, 1)
                    for r in range(R):
                        store(r, CAP + r)
                    n = rounds(k, pool)
                    with pool.Fori(0, n) as i:
                        for r in range(R):
                            hold(summed, R * i + r + 1)
                            store(r, (R * i + r).with_bounds(min_val=0, max_val=CAP - 1))
                    for r in range(R):
                        hold(stored[r], 16 * (n + 1))
                    pool.sem_inc(all_out, 1)

        @block.vector
        def _(dve):
            c = Chain(dve, ch)
            hold = Hold(dve, vt)
            with when(dve):
                for sem in (relued, product, posted, zused):
                    dve.sem_inc(sem, R)
                if agg is None:
                    c(dve.memset(stats[:, :, :, :], 0.0))
                    c.reset()
                    with dve.Fori(0, rounds(k, dve)) as i:
                        for r in range(R):
                            g = (R * i + r).with_bounds(min_val=0, max_val=CAP - 1)
                            hold(product, R * i + r + 1 + R)
                            dve.bn_stats(stats[:, ds(g, 1)].rearrange("p g h v -> p (g h v)"),
                                         e1[:, r, :]).then_inc(posted, 1)
                    total = dve.value_load(k.total[0:1, 0:1], min_val=1, max_val=GMAX)
                    hold(posted, total + R)
                    means = stats[:, :, :, 1]
                    half = float(W // 2)
                    c.go(dve.tensor_reduce(sums[:, 0:1], means, AX.XY, ALU.add))
                    c.go(dve.tensor_reduce(sums[:, 2:3], stats[:, :, :, 2], AX.XY, ALU.add))
                    c(dve.tensor_tensor(fold[:, :, :], means, means, ALU.mult))
                    c(dve.tensor_reduce(sums[:, 1:2], fold[:, :, :], AX.XY, ALU.add))
                    c(dve.tensor_scalar(sums[:, 0:1], sums[:, 0:1], half, None, ALU.mult))
                    c(dve.scalar_tensor_tensor(sums[:, 1:2], sums[:, 1:2], half, sums[:, 2:3], ALU.mult,
                                               ALU.add))
                else:
                    c(dve.memset(run[:, :, :], 0.0))
                    c(dve.tensor_tensor(last_group[:, :], k.group0[:, :], k.groups[:, :], ALU.add))
                    c(dve.tensor_scalar(last_group[:, :], last_group[:, :], -1.0, None, ALU.add))
                    dve.sem_inc(clear, 1)
                    c.reset()
                    with dve.Fori(0, rounds(k, dve)) as i:
                        reduced, added = {}, {}
                        for r in range(R + 1):
                            if r < R:
                                hold(posted, R * i + r + 1 + R)
                                reduced[r] = c.go(dve.tensor_reduce(
                                    zsum[:, r, :], z[:, r, :].rearrange("p (j c) -> p c j", j=J), AX.X, ALU.add))
                            if r:
                                q = r - 1
                                g = (R * i + q).with_bounds(min_val=0, max_val=CAP - 1)
                                hold(stored[q], 16 * (i + 1))
                                c.until(reduced[q])
                                dve.sem_inc(zused, 1)
                                if q:
                                    c.until(added[q - 1])
                                    dve.sem_inc(summed, 1)
                                added[q] = c.go(dve.scalar_tensor_tensor(
                                    run[:, q, :], run[:, (q - 1) % R, :], goes_on[:, ds(g, 1)], zsum[:, q, :],
                                    ALU.mult, ALU.add))
                        c.until(added[R - 1])
                        dve.sem_inc(summed, 1)
                        c.reset()

        @block.tensor
        def _(pe):
            hold = Hold(pe, pt)
            with when(pe):
                with pe.Fori(0, rounds(k, pe)) as i:
                    for r in range(R):
                        g = R * i + r
                        hold(relued, g + 1 + R)
                        hold(posted, g + 1)
                        pe.matmul(e1[:, r, :], fc[:, :], r4[:, r, :], start=True, stop=True
                                  ).then_inc(product, 1)

        @block.scalar
        def _(act):
            hold = Hold(act, at_)

            def first(i, r):
                g, slot = R * i + r, r % R
                hold(loaded[slot], 16 * (i + 1 + r // R))
                hold(product, g + 1)
                act.activation(r4[:, slot, :], tb[:, slot, :], ACT.Relu, bias=coef[:, 1:2],
                               scale=coef[:, 0:1]).then_inc(relued, 1)

            def second(i, r):
                g = R * i + r
                hold(product, g + 1 + R)
                hold(zused, g + 1)
                act.activation(z[:, r, :], e1[:, r, :], ACT.Relu, bias=coef[:, 3:4],
                               scale=coef[:, 2:3]).then_inc(posted, 1)

            act.activation(warm[:, :], k.ones[:, 0:1], ACT.Relu)
            with when(act):
                if agg is None:
                    with act.Fori(0, rounds(k, act)) as i:
                        for r in range(R):
                            first(i, r)
                else:
                    for r in range(2):
                        act.wait_ge(loaded[r], 16)
                        act.wait_ge(product, r + 1)
                        act.activation(r4[:, r, :], tb[:, r, :], ACT.Relu, bias=coef[:, 1:2],
                                       scale=coef[:, 0:1]).then_inc(relued, 1)
                    last = act.value_load(k.total[0:1, 4:5], min_val=1, max_val=GMAX // R)
                    with act.Fori(0, last) as i:
                        for r in range(R):
                            first(i, r + 2)
                            second(i, r)
                    for r in range(R):
                        if r + 2 < R:
                            first(last, r + 2)
                        second(last, r)
                    act.wait_ge(all_out, 1)
                    fetch_sums(act, 1)


def edge_regather(k, table, slot_src, at, fc, coef, sums, agg):
    with ExitStack() as st:
        s = k.sub(st)
        ga = Gather(k, s, table, D, slot_src)
        stage = s.sb("mstage", [P, J, D])
        att, pre, r, z = s.sb("att", [P, D]), s.sb("pre", [P, J, D]), s.sb("r", [P, J, D]), s.sb("z", [P, J, D])
        stats, acc = s.sb("stats", [P, 6]), StatSums(s)
        zsum, zacc = s.sb("zsum", [P, D]), s.sb("zacc", [P, D])
        bt, e1 = s.ps("bt", [P, 512]), s.ps("e1", [P, 512])
        staged, turned, pre_ready, r_ready, e1_ready, z_ready, turns, ch = (
            k.sem(n) for n in ("staged", "turned", "pre_ready", "r_ready", "e1_ready", "z_ready", "turns", "ch"))
        block = st.enter_context(k.block())

        def program(eng_name):
            def wrap(f):
                def g(eng):
                    with eng.If(rounds(k, eng) > CAP // R):
                        f(eng)
                eng_name(g)
            return wrap

        program(block.gpsimd)(ga.pool)
        program(block.sync)(ga.sync)

        @program(block.vector)
        def _(dve):
            c = Chain(dve, ch)
            hold = Hold(dve, turns)
            dve.sem_inc(ga.used, R)
            acc.clear(dve, c)
            c.reset()
            bounds = tiles_loop(k, dve)
            with dve.Fori(0, T) as t:
                g0, n = bounds(t)
                c(dve.tensor_copy(att[:, :], at[:, ds(t * P, P)]))
                if agg is not None:
                    c(dve.memset(zacc[:, :], 0.0))
                c.reset()
                with dve.Fori(g0, g0 + n) as g:
                    hold(ga.landed, g + 1)
                    c(dve.tensor_copy(stage[:, :, :], ga.group(g)))
                    dve.sem_inc(ga.used, 1)
                    dve.sem_inc(staged, 1)
                    take(dve, turned)
                    c(dve.scalar_tensor_tensor(pre[:, :, :], bt[:, :].rearrange("p (j c) -> p j c", j=J),
                                               coef[:, 0:1], att[:, :].unsqueeze(1).broadcast_to([P, J, D]),
                                               ALU.mult, ALU.add))
                    dve.sem_inc(pre_ready, 1)
                    take(dve, z_ready)
                    if agg is None:
                        c(dve.bn_stats(stats[:, :], z[:, :, :].rearrange("p j c -> p (j c)")))
                        acc.add(dve, c, stats)
                    else:
                        c(dve.tensor_reduce(zsum[:, :], z[:, :, :].rearrange("p j c -> p c j"), AX.X, ALU.add))
                        c(dve.tensor_tensor(zacc[:, :], zacc[:, :], zsum[:, :], ALU.add))
                    c.reset()
                if agg is not None:
                    c(dve.tensor_copy(agg[:, ds(t * P, P)], zacc[:, :]))
                    c.reset()
            if agg is None:
                acc.finish(dve, c, sums[:, 0:1], sums[:, 1:2])

        @program(block.tensor)
        def _(pe):
            n = pe.value_load(k.total[0:1, 0:1], min_val=1, max_val=GMAX)
            with pe.Fori(0, n):
                take(pe, staged)
                for j in range(J):
                    mm = pe.transpose(bt[:, j * P:(j + 1) * P], stage[:, j, :], k.ident[:, :])
                mm.then_inc(turned, 1)
                take(pe, r_ready)
                pe.matmul(e1[:, :], fc[:, :], r[:, :, :].rearrange("p j c -> p (j c)"), start=True,
                          stop=True).then_inc(e1_ready, 1)

        @program(block.scalar)
        def _(act):
            n = act.value_load(k.total[0:1, 0:1], min_val=1, max_val=GMAX)
            with act.Fori(0, n):
                take(act, pre_ready)
                rf, pf, zf = (a[:, :, :].rearrange("p j c -> p (j c)") for a in (r, pre, z))
                act.activation(rf, pf, ACT.Relu).then_inc(r_ready, 1)
                take(act, e1_ready)
                if agg is None:
                    act.activation(zf, e1[:, :], ACT.Copy).then_inc(z_ready, 1)
                else:
                    act.activation(zf, e1[:, :], ACT.Relu, bias=coef[:, 3:4], scale=coef[:, 2:3]).then_inc(z_ready, 1)


def edge_dummy(k, at, fc, coef, sums, empr, vec, spare, final):
    with ExitStack() as st:
        s = k.sub(st)
        e1 = s.sb("e1a", [P, NP])
        r = spare

        with ExitStack() as st1:
            ch = k.sem("edch")
            block = st1.enter_context(k.block())

            @block.vector
            def _(dve):
                c = Chain(dve, ch)
                c(dve.tensor_scalar(r[:, :], at[:, :], 0.0, None, ALU.max))

        def store(dve, c, ps, i, o):
            c(dve.tensor_copy(e1[:, ds(i * BLK, BLK)], ps))

        dense_cols(k, [r], [[fc[:, :]]], store)
        with ExitStack() as st1:
            ch = k.sem("edch2")
            block = st1.enter_context(k.block())

            @block.vector
            def _(dve):
                c = Chain(dve, ch)
                if final:
                    c(dve.tensor_scalar(e1[:, :], e1[:, :], coef[:, 2:3], coef[:, 3:4], ALU.mult, ALU.add))
                    c(dve.scalar_tensor_tensor(spare[:, :], e1[:, :], 0.0, empr[:, :], ALU.max, ALU.mult))
                else:
                    c(dve.tensor_tensor(r[:, :], e1[:, :], empr[:, :], ALU.mult))
                    c(dve.tensor_reduce(sums[:, 2:3], r[:, :], AX.X, ALU.add))
                    c(dve.tensor_tensor(r[:, :], r[:, :], e1[:, :], ALU.mult))
                    c(dve.tensor_reduce(sums[:, 3:4], r[:, :], AX.X, ALU.add))
                    c(dve.tensor_tensor(sums[:, 4:6], sums[:, 0:2], sums[:, 2:4], ALU.subtract))

        if not final:
            finish_bn(k, sums, 4, 5, vec[:, 2:3], vec[:, 3:4], coef[:, 2:3], coef[:, 3:4])


def build(nc, a, out):
    def dram(name, shape, dt=F32):
        return nc.dram_tensor(name, shape, dt, kind="Internal").ap()

    with ExitStack() as whole:
        k = Kit(nc)
        m = k.sub(whole)
        k.ident, k.ones, k.before = (m.sb(n, [P, P]) for n in ("ident", "ones", "before"))
        k.ramp = m.sb("ramp", [P, P])
        k.pos, k.posf = m.sb("pos", [P, T], I32), m.sb("posf", [P, T])
        k.deg, k.empty = m.sb("deg", [P, T]), m.sb("empty", [P, T])
        k.node, k.nodec, k.row0, k.shift = (m.sb(n, [P, T], I32) for n in ("node", "nodec", "row0", "shift"))
        k.groups, k.group0, k.chunks, k.chunk0 = (m.sb(n, [P, T], I32) for n in (
            "groups", "group0", "chunks", "chunk0"))
        k.bgroups, k.bgroup0 = m.sb("bgroups", [P, NB], I32), m.sb("bgroup0", [P, NB], I32)
        k.total = m.sb("total", [P, 5], I32)
        k.out = m.sb("layer_out", [P, T, D])
        xs = m.sb("x_state", [P, T, D])
        x = xs[:, :, :]

        dense = dram("dense_weights", (NP * PITCH, 1))
        slot_src, slot_weight = dram("slot_src", (GMAX, P, J), I32), dram("slot_weight", (GMAX, P, J), I32)
        keys, info = dram("keys", (NP,)), dram("info", (NP, 4), I32)
        gat_table = dram("gat_table", (NP + 1, 136))
        kv_table = dram("kv_table", (NP + 1, 272))
        b_table = dram("b_table", (NP + 1, D))
        by_node = dram("by_node", (NP, D))
        kept, running = dram("kept", (CAP + R, P, J * P)), dram("running", (CAP + R, P, D))
        empty_row, cnt_row = dram("empty_row", (NP,)), dram("cnt_row", (NP,))

        make_constants(k)
        order_nodes(k, a["dst"], keys, info, dense)
        build_slots(k, a["edges"], slot_src, slot_weight)
        gather_rows(k, a["x"], x, k.nodec)
        gat_conv(k, x, a["L0_gnn_W1"], a["L0_gnn_a1_src"], a["L0_gnn_a1_dst"], a["L0_gnn_b1"], gat_table,
                 slot_src, True)
        gat_conv(k, k.out[:, :, :], a["L0_gnn_W2"], a["L0_gnn_a2_src"], a["L0_gnn_a2_dst"], a["L0_gnn_b2"],
                 gat_table, slot_src, False)
        add_rows(k, k.out[:, :, :], k.out[:, :, :], x)
        layernorm(k, k.out[:, :, :], x, 1e-5)
        residual_layer(k, x, a["L1_gnn_W_self"], a["L1_gnn_b_self"], a["L1_gnn_W_neigh"], a["L1_gnn_b_neigh"],
                       a["L1_gnn_scale"], a["L1_gnn_offset"], dense, slot_src, slot_weight, by_node)
        attention_layer(k, x, {n[7:]: v for n, v in a.items() if n.startswith("L2_gnn_")}, kv_table, slot_src)
        edge_mlp_layer(k, x, {n[7:]: v for n, v in a.items() if n.startswith("L3_gnn_")}, b_table, slot_src,
                       kept, running, empty_row, cnt_row, out)


TRANSPOSED = ("L1_gnn_W_self", "L1_gnn_W_neigh", "L2_gnn_q_w", "L2_gnn_k_w", "L2_gnn_v_w", "L2_gnn_out_w",
              "L2_gnn_lin1_w", "L2_gnn_lin2_w", "L3_gnn_theta_w", "L3_gnn_phi_w", "L3_gnn_fc1_w")
COLUMNS = ("L2_gnn_out_b", "L2_gnn_g1", "L2_gnn_b1", "L2_gnn_lin2_b", "L2_gnn_g2", "L2_gnn_b2",
           "L3_gnn_bn0_g", "L3_gnn_bn0_b", "L3_gnn_bn1_g", "L3_gnn_bn1_b")


def kernel(**inputs):
    import numpy as _np
    import concourse.bacc as _bacc
    from concourse import mybir as _mybir
    from concourse.bass_utils import run_bass_kernel_spmd as _run

    nc = _bacc.Bacc("TRN2", target_bir_lowering=False, num_devices=1)
    arrays, args = {}, {}
    rows_of = [_np.concatenate([_np.asarray(inputs.pop(n)).view(_np.int32),
                                _np.zeros((EROWS + 1) * CH - E, _np.int32)]).reshape(EROWS + 1, CH)
               for n in ("src", "edge_weight")]
    inputs["edges"] = _np.concatenate([part for r in rows_of for part in (r[:-1], r[1:])], axis=1)
    for name, value in inputs.items():
        v = _np.asarray(value)
        if name == "dst":
            v = _np.concatenate([v, _np.full(P * ECOLS - E, NP, v.dtype)]).reshape(P, ECOLS)
        elif name in TRANSPOSED:
            v = v.T
        elif name in COLUMNS:
            v = v.reshape(-1, 1)
        elif name == "L2_gnn_lin1_b":
            v = v.reshape(-1, P).T
        v = _np.ascontiguousarray(v)
        arrays[f"in_{name}_dram"] = v
        args[name] = nc.dram_tensor(f"in_{name}_dram", v.shape, _mybir.dt.from_np(v.dtype),
                                    kind="ExternalInput").ap()
    out = nc.dram_tensor("out_0_dram", (N, D), _mybir.dt.float32, kind="ExternalOutput").ap()
    build(nc, args, out)
    r = _run(nc, [arrays], core_ids=[0])
    return r.results[0]["out_0_dram"]
```
